# Optimizing a Trainium2 kernel written in Bass

```python
import numpy as np
import jax
import jax.numpy as jnp

def _softmax(x, axis=-1):
    return jax.nn.softmax(x, axis=axis)

def _gelu(x):
    return jax.nn.gelu(x, approximate=True)

def _silu(x):
    return jax.nn.silu(x)

def _sigmoid(x):
    return jax.nn.sigmoid(x)

def _layernorm(x, axis=-1, eps=1e-05):
    m = jnp.mean(x, axis=axis, keepdims=True)
    v = jnp.var(x, axis=axis, keepdims=True)
    return (x - m) / jnp.sqrt(v + eps)

def _scatter_add(tgt, idx, src, axis=0):
    return tgt.at[idx].add(src)

def _segment_sum(src, seg, n):
    return jax.ops.segment_sum(src, seg, n)
kernel_name = 'mk_decoder_postln_d1_seqx_r8_844c80'

def setup_inputs(seed: int=0):
    np.random.seed(seed)
    _w = jnp.asarray

    def _rec_inputs():
        import jax
        import jax.numpy as jnp
        _rk = jax.random.key(seed)
        x = 0.5 + 0.2887 * jax.random.normal(jax.random.fold_in(_rk, 1), (4, 256, 256), jnp.float32)
        _lenS = 256 - jax.random.randint(jax.random.fold_in(_rk, 7), (4,), 0, max(1, 256 // 4) + 1, jnp.int32)
        _lenS2 = 256 - jax.random.randint(jax.random.fold_in(_rk, 8), (4,), 0, max(1, 256 // 4) + 1, jnp.int32)
        _ctx_512P = jax.random.normal(jax.random.fold_in(_rk, 11), (4, 16, 64), jnp.float32)
        _ctx_512c = jax.random.dirichlet(jax.random.fold_in(_rk, 511), 0.3 * jnp.ones((16,), jnp.float32), (4, 256))
        _ctx_512t = jnp.einsum('bsk,bkd->bsd', _ctx_512c, _ctx_512P)
        _ctx_512t = _ctx_512t * jax.lax.rsqrt(jnp.mean(jnp.square(_ctx_512t)) + 1e-12) * 0.953939
        ctx_512 = -0.000392918 + 0.999932 * (_ctx_512t + 0.3 * jax.random.normal(jax.random.fold_in(_rk, 611), (4, 256, 64), jnp.float32))
        return (x, ctx_512)
    x, ctx_512 = _rec_inputs()

    def _L0_attn_setup():
        import jax, jax.numpy as jnp
        import numpy as np
        import math
        D_MODEL = 256
        N_HEADS = 16
        D_HEAD = 128
        BATCH = 2
        SEQ = 256
        key = jax.random.key(seed)
        ks = jax.random.split(key, 5)
        std = 0.02
        x = jax.random.normal(ks[0], (BATCH, SEQ, D_MODEL), dtype=jnp.float32)
        W_Q = std * jax.random.normal(ks[1], (N_HEADS, D_HEAD, D_MODEL), dtype=jnp.float32)
        W_K = std * jax.random.normal(ks[2], (N_HEADS, D_HEAD, D_MODEL), dtype=jnp.float32)
        W_V = std * jax.random.normal(ks[3], (N_HEADS, D_HEAD, D_MODEL), dtype=jnp.float32)
        W_O = std * jax.random.normal(ks[4], (N_HEADS, D_MODEL, D_HEAD), dtype=jnp.float32)
        return {'x': x, 'W_Q': W_Q, 'W_K': W_K, 'W_V': W_V, 'W_O': W_O}
    _L0_attn_all = _L0_attn_setup()
    _L0_attn_in = {k: v for k, v in _L0_attn_all.items() if k in ('W_Q', 'W_K', 'W_V', 'W_O')}
    del _L0_attn_all

    def _L0_xattn_setup():
        import jax, jax.numpy as jnp
        import numpy as np
        B, N, D = (16, 256, 64)
        H = 4
        TOP_K_RATIO = 0.3
        key = jax.random.key(seed)
        k1, k2, k3, k4 = jax.random.split(key, 4)
        h = jax.random.normal(k1, (B, N, D), dtype=jnp.float32)
        adj_raw = jax.random.uniform(k2, (B, N, N), dtype=jnp.float32)
        lim = 1.0 / np.sqrt(D)
        Wq = jax.random.uniform(k3, (D, D), minval=-lim, maxval=lim, dtype=jnp.float32)
        Wk = jax.random.uniform(k4, (D, D), minval=-lim, maxval=lim, dtype=jnp.float32)
        gamma_raw = jnp.float32(-0.85)
        return {'h': h, 'adj_raw': adj_raw, 'Wq': Wq, 'Wk': Wk, 'gamma_raw': gamma_raw}
    _L0_xattn_all = _L0_xattn_setup()
    _L0_xattn_in = {k: v for k, v in _L0_xattn_all.items() if k in ('Wq', 'Wk', 'gamma_raw')}
    del _L0_xattn_all

    def _L0_ffn_setup():
        import jax, jax.numpy as jnp
        import numpy as np
        NUM_EXPERTS = 32
        TOP_K = 8
        SELECT_TOP_K = 4
        THRESHOLD = 0.5
        HIDDEN = 256
        D_FF = 96

        def _moe_forward(hidden_states, gate_weight, gate_up_proj, down_proj, similarity):
            B, S_len, H = hidden_states.shape
            E, K, Ssel = (NUM_EXPERTS, TOP_K, SELECT_TOP_K)
            x = hidden_states.reshape(-1, H)
            router_logits = x @ gate_weight.T
            router_probs = jax.nn.softmax(router_logits.astype(jnp.float32), axis=-1).astype(router_logits.dtype)
            router_top_value, router_indices = jax.lax.top_k(router_probs, K)
            routing_weights = router_top_value / jnp.clip(jnp.sum(router_top_value, axis=-1, keepdims=True), 1e-12, None)
            sim = similarity.astype(jnp.float32)
            sim = sim.at[jnp.arange(E), jnp.arange(E)].set(1.0)
            prim = router_indices[:, :Ssel]
            sec = router_indices[:, Ssel:]
            sim_cand = sim[sec[:, :, None], prim[:, None, :]]
            best_sim = jnp.max(sim_cand, axis=-1)
            best_i = jnp.argmax(sim_cand, axis=-1)
            prim_rep = jnp.broadcast_to(prim[:, None, :], sim_cand.shape)
            best_primary = jnp.take_along_axis(prim_rep, best_i[..., None], axis=-1)[..., 0]
            new_sec = jnp.where(best_sim < THRESHOLD, sec, best_primary) if THRESHOLD > 0.0 else best_primary
            rerouted_indices = jnp.concatenate([prim, new_sec], axis=1)
            combine = jnp.sum(jax.nn.one_hot(rerouted_indices, E, dtype=routing_weights.dtype) * routing_weights[..., None], axis=1)

            def expert_step(y, params):
                wgu, wd, cw = params
                gu = x @ wgu.T
                g, u = jnp.split(gu, 2, axis=-1)
                h = jax.nn.silu(g) * u
                y = y + h @ wd.T * cw[:, None]
                return (y, None)
            y0 = jnp.zeros_like(x)
            y, _ = jax.lax.scan(expert_step, y0, (gate_up_proj, down_proj, combine.T))
            return y.reshape(B, S_len, H)
        key = jax.random.key(seed)
        ks = jax.random.split(key, 5)
        hidden_states = jax.random.normal(ks[0], (4, 256, HIDDEN), dtype=jnp.float32)
        gate_weight = jax.random.normal(ks[1], (NUM_EXPERTS, HIDDEN), dtype=jnp.float32) * 0.02
        gate_up_proj = jax.random.normal(ks[2], (NUM_EXPERTS, 2 * D_FF, HIDDEN), dtype=jnp.float32) * 0.02
        down_proj = jax.random.normal(ks[3], (NUM_EXPERTS, HIDDEN, D_FF), dtype=jnp.float32) * 0.02
        similarity = jax.random.uniform(ks[4], (NUM_EXPERTS, NUM_EXPERTS), dtype=jnp.float32)
        return {'hidden_states': hidden_states, 'gate_weight': gate_weight, 'gate_up_proj': gate_up_proj, 'down_proj': down_proj, 'similarity': similarity}
    _L0_ffn_all = _L0_ffn_setup()
    _L0_ffn_in = {k: v for k, v in _L0_ffn_all.items() if k in ('gate_weight', 'gate_up_proj', 'down_proj', 'similarity')}
    del _L0_ffn_all
    return {'x': x, 'ctx_512': ctx_512, 'L0_attn_W_Q': _L0_attn_in['W_Q'], 'L0_attn_W_K': _L0_attn_in['W_K'], 'L0_attn_W_V': _L0_attn_in['W_V'], 'L0_attn_W_O': _L0_attn_in['W_O'], 'L0_xattn_Wq': _L0_xattn_in['Wq'], 'L0_xattn_Wk': _L0_xattn_in['Wk'], 'L0_xattn_gamma_raw': _L0_xattn_in['gamma_raw'], 'L0_ffn_gate_weight': _L0_ffn_in['gate_weight'], 'L0_ffn_gate_up_proj': _L0_ffn_in['gate_up_proj'], 'L0_ffn_down_proj': _L0_ffn_in['down_proj'], 'L0_ffn_similarity': _L0_ffn_in['similarity']}

def reference(x, ctx_512, L0_attn_W_Q, L0_attn_W_K, L0_attn_W_V, L0_attn_W_O, L0_xattn_Wq, L0_xattn_Wk, L0_xattn_gamma_raw, L0_ffn_gate_weight, L0_ffn_gate_up_proj, L0_ffn_down_proj, L0_ffn_similarity):
    import jax
    import jax.numpy as jnp

    def _L0_attn_ref(x, W_Q, W_K, W_V, W_O):
        import jax, jax.numpy as jnp
        import numpy as np
        import math
        D_MODEL = 256
        N_HEADS = 16
        D_HEAD = 128
        BATCH = 2
        SEQ = 256
        d_head = W_Q.shape[1]
        seq_len = x.shape[1]
        scale = 1.0 / math.sqrt(d_head)
        q = jnp.einsum('bsd,hed->bhse', x, W_Q)
        k = jnp.einsum('bsd,hed->bhse', x, W_K)
        v = jnp.einsum('bsd,hed->bhse', x, W_V)
        scores = jnp.einsum('bhse,bhme->bhsm', q, k) * scale
        causal = jnp.triu(jnp.ones((seq_len, seq_len), dtype=bool), k=1)
        scores = jnp.where(causal, jnp.float32(-1000000000.0), scores)
        pattern = jax.nn.softmax(scores, axis=-1)
        z = jnp.einsum('bhsm,bhme->bhse', pattern, v)
        out = jnp.einsum('bhse,hde->bsd', z, W_O)
        return out

    def _L0_xattn_ref(h, adj_raw, Wq, Wk, gamma_raw):
        import jax, jax.numpy as jnp
        import numpy as np
        B, N, D = (16, 256, 64)
        H = 4
        TOP_K_RATIO = 0.3
        b, n, dm = h.shape
        d = dm // H
        Q = (h @ Wq.T).reshape(b, n, H, d).transpose(0, 2, 1, 3)
        K = (h @ Wk.T).reshape(b, n, H, d).transpose(0, 2, 1, 3)
        sim = jnp.einsum('bhnd,bhmd->bnm', Q, K) / (jnp.sqrt(jnp.float32(d)) * H)
        k = max(1, int(n * TOP_K_RATIO))
        topk_vals = jax.lax.top_k(sim, k)[0]
        threshold = topk_vals[:, :, -1:]
        sparse_mask = (sim >= threshold).astype(sim.dtype)
        A_learned = jax.nn.sigmoid(sim) * sparse_mask
        A_learned = (A_learned + jnp.swapaxes(A_learned, -1, -2)) * 0.5
        gamma = jax.nn.sigmoid(gamma_raw)
        return (1.0 - gamma) * adj_raw + gamma * A_learned

    def _L0_ffn_ref(hidden_states, gate_weight, gate_up_proj, down_proj, similarity):
        import jax, jax.numpy as jnp
        import numpy as np
        NUM_EXPERTS = 32
        TOP_K = 8
        SELECT_TOP_K = 4
        THRESHOLD = 0.5
        HIDDEN = 256
        D_FF = 96

        def _moe_forward(hidden_states, gate_weight, gate_up_proj, down_proj, similarity):
            B, S_len, H = hidden_states.shape
            E, K, Ssel = (NUM_EXPERTS, TOP_K, SELECT_TOP_K)
            x = hidden_states.reshape(-1, H)
            router_logits = x @ gate_weight.T
            router_probs = jax.nn.softmax(router_logits.astype(jnp.float32), axis=-1).astype(router_logits.dtype)
            router_top_value, router_indices = jax.lax.top_k(router_probs, K)
            routing_weights = router_top_value / jnp.clip(jnp.sum(router_top_value, axis=-1, keepdims=True), 1e-12, None)
            sim = similarity.astype(jnp.float32)
            sim = sim.at[jnp.arange(E), jnp.arange(E)].set(1.0)
            prim = router_indices[:, :Ssel]
            sec = router_indices[:, Ssel:]
            sim_cand = sim[sec[:, :, None], prim[:, None, :]]
            best_sim = jnp.max(sim_cand, axis=-1)
            best_i = jnp.argmax(sim_cand, axis=-1)
            prim_rep = jnp.broadcast_to(prim[:, None, :], sim_cand.shape)
            best_primary = jnp.take_along_axis(prim_rep, best_i[..., None], axis=-1)[..., 0]
            new_sec = jnp.where(best_sim < THRESHOLD, sec, best_primary) if THRESHOLD > 0.0 else best_primary
            rerouted_indices = jnp.concatenate([prim, new_sec], axis=1)
            combine = jnp.sum(jax.nn.one_hot(rerouted_indices, E, dtype=routing_weights.dtype) * routing_weights[..., None], axis=1)

            def expert_step(y, params):
                wgu, wd, cw = params
                gu = x @ wgu.T
                g, u = jnp.split(gu, 2, axis=-1)
                h = jax.nn.silu(g) * u
                y = y + h @ wd.T * cw[:, None]
                return (y, None)
            y0 = jnp.zeros_like(x)
            y, _ = jax.lax.scan(expert_step, y0, (gate_up_proj, down_proj, combine.T))
            return y.reshape(B, S_len, H)
        return _moe_forward(hidden_states, gate_weight, gate_up_proj, down_proj, similarity)
    x = _layernorm(x + _L0_attn_ref(x, L0_attn_W_Q, L0_attn_W_K, L0_attn_W_V, L0_attn_W_O), axis=-1)
    x = _layernorm(x + _L0_xattn_ref(ctx_512, x, L0_xattn_Wq, L0_xattn_Wk, L0_xattn_gamma_raw), axis=-1)
    x = _layernorm(x + _L0_ffn_ref(x, L0_ffn_gate_weight, L0_ffn_gate_up_proj, L0_ffn_down_proj, L0_ffn_similarity), axis=-1)
    return x

_drawn_inputs = setup_inputs


def setup_inputs(seed=0):
    import zlib

    import numpy as np

    out = dict(_drawn_inputs(seed))
    spreads = {}
    factors = {'L0_attn_W_Q': 8.0,
     'L0_attn_W_K': 8.0,
     'L0_ffn_gate_weight': 8.0,
     'L0_ffn_gate_up_proj': 8.0,
     'L0_ffn_down_proj': 8.0,
     'L0_ffn_similarity': 8.0}
    for name, (base, spread) in spreads.items():
        noise = np.random.default_rng([zlib.crc32(name.encode()), seed]).standard_normal(out[name].shape)
        drawn = base * np.exp(spread * noise) if base else spread * noise
        out[name] = jnp.asarray(drawn.astype(out[name].dtype))
    for name, factor in factors.items():
        out[name] = (out[name] * factor).astype(out[name].dtype)
    return out
```

```python
from contextlib import ExitStack

import concourse.bass as bass
from concourse import mybir

F32 = mybir.dt.float32
F32R = mybir.dt.float32r
U32 = mybir.dt.uint32
ALU = mybir.AluOpType
ACT = mybir.ActivationFunctionType
AX = mybir.AxisListType

P = 128
BATCH, SEQ, D = 4, 256, 256
TOK = BATCH * SEQ
TILES = TOK // P
KC = D // P
HEADS, DH = 16, 128
PAIRS = HEADS // 2
CTX = 64
TOPK_ADJ = int(SEQ * 0.3)
E, FF = 32, 96
TOP, PRIM = 8, 4
FT = E * FF // P
FG = 3
FSTEPS = FT // FG
BLK = 512
NBLK = TOK // BLK
NEG = -1.0e9
EPS = 1.0e-5
SCALE = float(DH) ** -0.5
ROUNDS = (TOPK_ADJ + 7) // 8


def fills_of_slot(n):
    return {0: [("q", 1), ("v", 1)], 1: [("k", 1), ("v", 2)], 2: [("q", 2), ("v", 3)], 3: [("k", 2)],
            4: [("q", 3)], 5: [("k", 3)], 6: [("q", 0)], 7: [("k", 0), ("v", 0)]}[n]


PER_PAIR = sum(len(fills_of_slot(n)) for n in range(8))
FIRST = [("q", 0), ("k", 0), ("v", 0)]
AT_SLOT = [sum(len(fills_of_slot(m)) for m in range(n)) for n in range(8)]
ORDER = {f: n for n, f in enumerate(FIRST)}
ORDER.update({f: len(FIRST) + AT_SLOT[n] + m
              for n in range(8) for m, f in enumerate(fills_of_slot(n)) if f[1]})


def program(nc, x_tok, x_t, w_qk, w_v, w_o, ctx_t, w_ctx, gamma_raw, gate_t, w_ffn, sim_t, out):
    ctx = ExitStack()
    with ctx:
        def sb(name, shape, dt=F32):
            return ctx.enter_context(nc.sbuf_tensor(name, shape, dt))

        def pair(name, shape):
            return sb(name + "_hi", shape, F32R), sb(name + "_lo", shape, F32R)

        def ps(name, shape):
            return ctx.enter_context(nc.psum_tensor(name, shape, F32))

        def sem(name):
            return ctx.enter_context(nc.semaphore(name))

        ident = sb("ident", [P, P])
        mask = sb("mask", [P, 2 * P])
        iota_e = sb("iota_e", [P, E])
        xs = sb("xs", [P, TILES, D])
        xt_hi, xt_lo = pair("xt", [P, KC, TOK])
        one = sb("one", [P, 1])
        zero = sb("zero", [P, 1])
        adj = sb("adj", [P, TILES * SEQ])
        gam = sb("gam", [P, 4])
        stats = sb("stats", [P, TILES, 6])
        mv = sb("mv", [P, TILES, 2])
        vare, std, rstd = sb("vare", [P, TILES]), sb("std", [P, TILES]), sb("rstd", [P, TILES])
        gate_raw = sb("gate_raw", [P, KC, E])
        gate_hi, gate_lo = pair("gate", [P, KC, E])
        blockdiag = sb("blockdiag", [P, P])
        wf_raw = [sb(f"wf_raw{i}", [P, 6 * P]) for i in range(FG)]
        wf = [pair(f"wf{i}", [P, 6 * P]) for i in range(FG)]
        att = ExitStack()

        def att_sb(name, shape, dt=F32):
            return att.enter_context(nc.sbuf_tensor(name, shape, dt))

        def att_pair(name, shape):
            return att_sb(name + "_hi", shape, F32R), att_sb(name + "_lo", shape, F32R)

        xt_raw = att_sb("xt_raw", [P, KC, TOK])
        raw_a, raw_b = att_sb("raw_a", [P, 2, KC, P]), att_sb("raw_b", [P, 2, KC, P])
        raw_v = att_sb("raw_v", [P, KC, 2 * P])
        raw_o = [att_sb("raw_o0", [P, D]), att_sb("raw_o1", [P, D])]
        wa_hi, wa_lo = att_pair("wa", [P, 2, KC, P])
        wb_hi, wb_lo = att_pair("wb", [P, 2, KC, P])
        wv_hi, wv_lo = att_pair("wv", [P, KC, 2 * P])
        wo = [att_pair("wo0", [P, D]), att_pair("wo1", [P, D])]
        qk = [att_pair("qk0", [P, 2, BLK]), att_pair("qk1", [P, 2, BLK])]
        v_hi, v_lo = att_pair("v", [P, TILES, 2 * DH])
        s_masked_sb = att_sb("s_masked_sb", [P, 3 * P])
        row_max, neg_max = att_sb("row_max", [P, 2]), att_sb("neg_max", [P, 2])
        row_sum, inv_sum = att_sb("row_sum", [P, 2]), att_sb("inv_sum", [P, 2])
        probs, probs_n = att_sb("probs", [P, 3 * P]), [att_sb(f"probs_n{i}", [P, 3 * P]) for i in range(2)]
        pt_hi, pt_lo = att_pair("pt", [P, 3 * P])
        z_hi, z_lo = att_pair("z", [P, 2 * P])
        ctx_sb = att_sb("ctx_sb", [CTX, TOK])
        wctx_sb = att_sb("wctx_sb", [CTX, 2, CTX])
        cq, ck = att_sb("cq", [CTX, TOK]), att_sb("ck", [CTX, TOK])
        sims = att_sb("sims", [P, TILES * SEQ])
        topk_work = [att_sb("topk_work0", [P, SEQ]), att_sb("topk_work1", [P, SEQ])]
        topk_8 = att_sb("topk_8", [P, 8])
        att.close()
        x1 = sb("x1", [P, TILES, D])
        mixed = sb("mixed", [P, TILES, D])
        logits, shifted = sb("logits", [P, TILES, E]), sb("shifted", [P, TILES, E])
        top_v, top_s = sb("top_v", [P, TILES, TOP]), sb("top_s", [P, TILES, TOP])
        top_i, top_if = sb("top_i", [P, TILES, TOP], U32), sb("top_if", [P, TILES, TOP])
        exp_all, exp_top = sb("exp_all", [P, TILES, E]), sb("exp_top", [P, TILES, TOP])
        sum_all, inv_all = sb("sum_all", [P, TILES]), sb("inv_all", [P, TILES])
        sum_top, inv_top = sb("sum_top", [P, TILES]), sb("inv_top", [P, TILES])
        sum_top_c = sb("sum_top_c", [P, TILES])
        prob_top, route_w = sb("prob_top", [P, TILES, TOP]), sb("route_w", [P, TILES, TOP])
        onehot = sb("onehot", [P, TILES, TOP, E])
        onehot_t = sb("onehot_t", [P, TILES, P])
        sec_each = sb("sec_each", [P, TILES, TOP - PRIM, E])
        sec_w = sb("sec_w", [P, TILES, E])
        cand = sb("cand", [P, TILES, PRIM, E])
        best = sb("best", [P, TILES, E])
        moved = [sb(f"moved{i}", [P, TILES, E]) for i in range(PRIM + 1)]
        is_best = sb("is_best", [P, TILES, PRIM, E])
        take = sb("take", [P, TILES, PRIM, E])
        taken, prim_w = sb("taken", [P, TILES, PRIM]), sb("prim_w", [P, TILES, PRIM])
        prim_each = sb("prim_each", [P, TILES, PRIM, E])
        prim_all, kept = sb("prim_all", [P, TILES, E]), sb("kept", [P, TILES, E])
        combine = sb("combine", [P, TILES, E])
        combine_t = sb("combine_t", [E, TOK])
        cw = [sb(f"cw{i}", [P, TOK]) for i in range(FG)]
        silu_g = [sb(f"silu_g{i}", [P, BLK]) for i in range(2)]
        silu_c = [sb(f"silu_c{i}", [P, BLK]) for i in range(2)]
        h_sb = [sb(f"h_sb{i}", [P, BLK]) for i in range(2)]
        h = [pair(f"h{i}", [P, BLK]) for i in range(3)]
        y_sb = sb("y_sb", [P, TILES, D])

        combine_dram = nc.dram_tensor("combine_dram", [E, TOK], F32, kind="Internal").ap()

        acc = [ps(f"acc{b}", [P, 2, D]) for b in range(BATCH)]
        bank_f, bank_s = ps("bank_f", [P, BLK]), ps("bank_s", [P, BLK])
        bank_t, bank_z = ps("bank_t", [P, BLK]), ps("bank_z", [P, BLK])
        sim_banks = [bank_f, bank_s, bank_t, bank_z]

        in_x, in_xt, in_ctx, in_wctx, in_gam = (sem(f"in_{n}") for n in ("x", "xt", "ctx", "wctx", "gam"))
        in_gate, in_sim = sem("in_gate"), sem("in_sim")
        PIECES = "abvop"
        w_in, w_hi_done, w_lo_done = ({k: sem(f"w{k}_{s}") for k in PIECES} for s in ("in", "hi_done", "lo_done"))
        const_made, const_zero = sem("const_made"), sem("const_zero")
        xt_hi_done, xt_lo_done = sem("xt_hi_done"), sem("xt_lo_done")
        ctx_proj, ctx_proj_sb = sem("ctx_proj"), sem("ctx_proj_sb")
        sims_ready, sims_copied, sig_done, adj_scaled = (sem(n) for n in ("sims_ready", "sims_copied", "sig_done", "adj_scaled"))
        gam_sig, gam_done = sem("gam_sig"), sem("gam_done")
        seeded = sem("seeded")
        passed_pool, passed_dve = sem("passed_pool"), sem("passed_dve")
        filled, fill_hi, fill_lo = sem("filled"), sem("fill_hi"), sem("fill_lo")
        scored, masked, neg_done, exp_done = (sem(n) for n in ("scored", "masked", "neg_done", "exp_done"))
        inv_done, norm_done, turned = sem("inv_done"), sem("norm_done"), sem("turned")
        pt_hi_done, pt_lo_done, pv_done = sem("pt_hi_done"), sem("pt_lo_done"), sem("pv_done")
        z_hi_done, z_lo_done, projected = sem("z_hi_done"), sem("z_lo_done"), sem("projected")
        topk_step = sem("topk_step")
        ln_step, std_done, eps_done = sem("ln_step"), sem("std_done"), sem("eps_done")
        adj_sum, x1_done, mixed_done, x2_done = (sem(n) for n in ("adj_sum", "x1_done", "mixed_done", "x2_done"))
        x2_turned, x2t_hi_done, x2t_lo_done = sem("x2_turned"), sem("x2t_hi_done"), sem("x2t_lo_done")
        gate_hi_done, gate_lo_done, logits_done = sem("gate_hi_done"), sem("gate_lo_done"), sem("logits_done")
        route, exps_done, onehot_turned, onehot_sb, cand_done = (sem(n) for n in ("route", "exps_done", "onehot_turned", "onehot_sb", "cand_done"))
        bd_made = sem("bd_made")
        seeded2, combine_turned, combine_sb, combine_out = (sem(n) for n in ("seeded2", "combine_turned", "combine_sb", "combine_out"))
        wf_in, wf_hi_done, wf_lo_done, cw_in = ([sem(f"{n}{i}") for i in range(FG)] for n in ("wf_in", "wf_hi", "wf_lo", "cw_in"))
        gu_done, silu_done, silu_c_done, h_done, h_hi_done, h_lo_done, down_done = (
            sem(n) for n in ("gu_done", "silu_done", "silu_c_done", "h_done", "h_hi_done", "h_lo_done", "down_done"))
        y_done, y_out = sem("y_done"), [sem(f"y_out{b}") for b in range(BATCH)]

        def wait(eng, semaphore, value):
            if not isinstance(value, int) or value > 0:
                eng.wait_ge(semaphore, value)

        def settle(eng):
            eng.sem_inc(passed_pool if eng is nc.gpsimd else passed_dve, 1)

        raw_of = {"a": raw_a[:].rearrange("p s c e -> p (s c e)"), "b": raw_b[:].rearrange("p s c e -> p (s c e)"),
                  "v": raw_v[:].rearrange("p c e -> p (c e)"), "o": raw_o[0][:], "p": raw_o[1][:]}
        hi_of = {"a": wa_hi[:].rearrange("p s c e -> p (s c e)"), "b": wb_hi[:].rearrange("p s c e -> p (s c e)"),
                 "v": wv_hi[:].rearrange("p c e -> p (c e)"), "o": wo[0][0][:], "p": wo[1][0][:]}
        lo_of = {"a": wa_lo[:].rearrange("p s c e -> p (s c e)"), "b": wb_lo[:].rearrange("p s c e -> p (s c e)"),
                 "v": wv_lo[:].rearrange("p c e -> p (c e)"), "o": wo[0][1][:], "p": wo[1][1][:]}

        def piece_dram(k, q):
            if k == "v":
                return w_v[bass.ds(q, 1)].rearrange("o p n -> p (o n)")
            src, head = (w_qk if k in "ab" else w_o), 2 * q + (k in "bp")
            return src[bass.ds(head, 1)].rearrange("o p n -> p (o n)")

        SPLIT_SLOT = {3: ("a", 1), 4: ("v", 1), 5: ("p", 0), 7: ("b", 1), 0: ("o", 0)}
        LAG_PV, LAG_OUT = 2, 3

        def item_loop(eng, slot):
            for k in range(LAG_OUT):
                slot(k, k, 0, lambda lag, k=k: k >= lag, True)
            with eng.Fori(0, PAIRS - 1) as q:
                for k in range(LAG_OUT, LAG_OUT + 8):
                    slot(q * 8 + k, k % 8, q + k // 8, lambda lag: True, True)
            for k in range(LAG_OUT, LAG_OUT + 8):
                slot(8 * (PAIRS - 1) + k, k % 8, PAIRS - 1, lambda lag, k=k: k - lag < 8, False)

        def fills_in(n, q, live, more):
            fills = [f for f in fills_of_slot(n) if live(0) and (more or f[1])]
            return fills, PER_PAIR * q + len(FIRST) + AT_SLOT[n]

        def fill_views(what, f):
            if what == "v":
                return v_hi[:, 2 * f:2 * f + 2, :], v_lo[:, 2 * f:2 * f + 2, :]
            hi, lo = qk[f % 2]
            s = "qk".index(what)
            return hi[:, s, :], lo[:, s, :]

        def fill_src(what):
            return bank_f[:] if what != "v" else bank_f[:].rearrange("p (t e) -> p t e", t=2)

        def turn_bank(t):
            return [bank_s, bank_t, bank_z, bank_f][t // 2][:, (t % 2) * 2 * P:(t % 2 + 1) * 2 * P].rearrange("p (c n) -> p c n", c=KC)

        def turned_batch(b):
            return [bank_s, bank_t, bank_z, bank_f][b][:].rearrange("p (t c n) -> p t c n", t=2, c=KC)

        def of_batch(xt, b):
            return xt[:, :, b * SEQ:(b + 1) * SEQ].rearrange("p c (t n) -> p t c n", t=2)

        G, U = [bank_f, bank_t], [bank_s, bank_z]

        def split_at_slot(k, s, K, last, split):
            if k == 4 and not last:
                split(0, s + 1)
            elif k == 0 and not isinstance(K, int):
                split(1, s)
            elif k == 2:
                split(2, s)

        def ffn_loop(eng, slot):
            slot(0, 0, 0, False)
            slot(1, 1, 0, False)
            with eng.Fori(0, FSTEPS - 1) as s:
                for k in range(2, 2 * FG + 2):
                    slot(s * 2 * FG + k, k % (2 * FG), s + k // (2 * FG), False)
            for k in range(2, 2 * FG + 2):
                slot(2 * FG * (FSTEPS - 1) + k, k % (2 * FG), FSTEPS - 1, True)

        block = ctx.enter_context(nc.Block())

        @block.sync
        def _(sp):
            def load_piece(k, q):
                wait(sp, w_lo_done[k], q)
                sp.dma_start(raw_of[k], piece_dram(k, q)).then_inc(w_in[k], 16)

            sp.dma_start(ctx_sb[:], ctx_t).then_inc(in_ctx, 16)
            sp.dma_start(wctx_sb[:], w_ctx).then_inc(in_wctx, 16)
            sp.dma_start(gam[:, 0:1], gamma_raw.to_broadcast([P, 1])).then_inc(in_gam, 16)
            sp.dma_start(xt_raw[:], x_t).then_inc(in_xt, 16)
            load_piece("a", 0)
            load_piece("v", 0)
            sp.dma_start(xs[:], x_tok.rearrange("(t p) d -> p t d", p=P)).then_inc(in_x, 16)
            for k in "bop":
                load_piece(k, 0)
            sp.dma_start(gate_raw[:], gate_t).then_inc(in_gate, 16)
            sp.wait_ge(const_zero, 2)
            for i in range(PRIM):
                sp.dma_start(blockdiag[i * E:(i + 1) * E, i * E:(i + 1) * E], sim_t).then_inc(in_sim, 16)
            for i in range(FG):
                sp.dma_start(wf_raw[i][:], w_ffn[i]).then_inc(wf_in[i], 16)
            with sp.Fori(1, PAIRS) as q:
                for k in "avbop":
                    load_piece(k, q)

            sp.wait_ge(combine_sb, 1)
            sp.dma_start(combine_dram, combine_t[:]).then_inc(combine_out, 16)
            sp.wait_ge(combine_out, 16)

            def load_cw(i, row_of):
                at = 0
                while at < P:
                    expert, inside = divmod(i * P + at, FF)
                    n = min(FF - inside, P - at)
                    src = combine_dram[bass.ds(row_of(expert), 1), :].to_broadcast([n, TOK])
                    sp.dma_start(cw[i][at:at + n, :], src).then_inc(cw_in[i], 16)
                    at += n

            for i in range(FG):
                load_cw(i, lambda expert: expert)
            with sp.Fori(1, FSTEPS) as s:
                for i in range(FG):
                    sp.wait_ge(wf_lo_done[i], s)
                    sp.dma_start(wf_raw[i][:], w_ffn[bass.ds(s * FG + i, 1)].rearrange("o p n -> p (o n)"))\
                        .then_inc(wf_in[i], 16)
                    sp.wait_ge(silu_c_done, s * 2 * FG - 2 * FG + 2 * i + 2)
                    load_cw(i, lambda expert: s * 4 + expert)
            for b in range(BATCH):
                sp.wait_ge(y_done, 2 * b + 2)
                sp.dma_start(out[b * SEQ:(b + 1) * SEQ].rearrange("(t p) d -> p t d", p=P),
                             y_sb[:, 2 * b:2 * b + 2, :]).then_inc(y_out[b], 16)
            for b in range(BATCH):
                sp.wait_ge(y_out[b], 16)

        @block.gpsimd
        def _(pool):
            pool.memset(ident[:], 0.0).then_inc(const_zero, 1)
            pool.memset(blockdiag[:], 0.0).then_inc(const_zero, 1)
            pool.memset(mask[:], 0.0).then_inc(const_zero, 1)
            pool.memset(one[:], 1.0).then_inc(const_zero, 1)
            pool.memset(zero[:], 0.0).then_inc(const_zero, 1)
            pool.wait_ge(const_zero, 5)
            pool.affine_select(out=ident[:], in_=ident[:], compare_op=ALU.not_equal, fill=1.0, base=0,
                               pattern=[[-1, P]], channel_multiplier=1).then_inc(const_made, 1)
            pool.affine_select(out=mask[:, P:], in_=mask[:, P:], compare_op=ALU.is_ge, fill=NEG, base=0,
                               pattern=[[-1, P]], channel_multiplier=1).then_inc(const_made, 1)
            pool.iota(iota_e[:], pattern=[[1, E]], base=0, channel_multiplier=0,
                      allow_small_or_imprecise_dtypes=True).then_inc(const_made, 1)

            def round_to_hi(dst, src):
                return pool.tensor_scalar(dst, src, one[0:src.shape[0], 0:1], zero[0:src.shape[0], 0:1], ALU.mult, ALU.add)

            def split_hi(k, q, free=None):
                pool.wait_ge(w_in[k], (q + 1) * 16)
                if free is not None:
                    pool.wait_ge(*free)
                settle(pool)
                round_to_hi(hi_of[k], raw_of[k]).then_inc(w_hi_done[k], 1)

            for k in "avbo":
                split_hi(k, 0)
            for b in range(BATCH):
                pool.wait_ge(sig_done, b + 1)
                pool.wait_ge(gam_done, 1)
                part = slice(2 * b * SEQ, 2 * (b + 1) * SEQ)
                pool.tensor_scalar(adj[:, part], adj[:, part],
                                   gam[:, 2:3], zero[:, 0:1], ALU.mult, ALU.add).then_inc(adj_scaled, 1)
            pool.wait_ge(in_sim, 16 * PRIM)
            pool.affine_select(out=blockdiag[:], in_=blockdiag[:], compare_op=ALU.not_equal, fill=1.0, base=0,
                               pattern=[[-1, P]], channel_multiplier=1).then_inc(bd_made, 1)
            pool.wait_ge(in_gate, 16)
            round_to_hi(gate_hi[:].rearrange("p c e -> p (c e)"), gate_raw[:].rearrange("p c e -> p (c e)")).then_inc(gate_hi_done, 1)

            def slot(N, n, q, live, more):
                if live(0):
                    dst = probs_n[n % 2]
                    pool.wait_ge(inv_done, N + 1)
                    wait(pool, turned, N - 1)
                    settle(pool)
                    pool.tensor_scalar(dst[:, 0:P], probs[:, 0:P], inv_sum[:, 0:1], zero[:, 0:1],
                                       ALU.mult, ALU.add).then_inc(norm_done, 1)
                    pool.tensor_scalar(dst[:, P:], probs[:, P:], inv_sum[:, 1:2], zero[:, 0:1],
                                       ALU.mult, ALU.add).then_inc(norm_done, 1)
                k, ahead = SPLIT_SLOT.get(n, (None, 0))
                if k and live(0) and (more or not ahead) and not (isinstance(N, int) and N == 0):
                    free = {"a": (filled, PER_PAIR * q + ORDER["k", 1] + 1),
                            "v": (filled, PER_PAIR * q + ORDER["v", 3] + 1),
                            "b": (filled, PER_PAIR * q + ORDER["k", 3] + 1),
                            "o": (projected, q * 8 - 4), "p": (projected, q * 8 + 1)}[k]
                    split_hi(k, q + ahead, free)
                    pool.wait_ge(w_hi_done[k], q + ahead + 1)
                    pool.tensor_tensor(lo_of[k], raw_of[k], hi_of[k].bitcast(F32), ALU.subtract).then_inc(w_lo_done[k], 1)

            item_loop(pool, slot)

            def split_ffn(i, s):
                pool.wait_ge(wf_in[i], (s + 1) * 16)
                settle(pool)
                round_to_hi(wf[i][0][:], wf_raw[i][:]).then_inc(wf_hi_done[i], 1)

            for i in range(FG - 1):
                split_ffn(i, 0)

            def ffn_slot(K, k, s, last):
                if last and k < 2:
                    return
                i, c = k // 2, k % 2
                pool.wait_ge(cw_in[i], s * 32 + 32)
                pool.wait_ge(silu_done, K + 1)
                wait(pool, h_done, K - 1)
                pool.tensor_tensor(silu_c[k % 2][:], silu_g[k % 2][:], cw[i][:, c * BLK:(c + 1) * BLK],
                                   ALU.mult).then_inc(silu_c_done, 1)
                split_at_slot(k, s, K, last, split_ffn)

            ffn_loop(pool, ffn_slot)

        @block.scalar
        def _(act):
            for n, dst in enumerate((cq, cq, ck, ck)):
                if n % 2 == 0:
                    act.wait_ge(ctx_proj, n + 1)
                    act.activation(dst[:, 0:BLK], acc[n][0:CTX].rearrange("p a b -> p (a b)"), ACT.Copy).then_inc(ctx_proj_sb, 1)
            act.wait_ge(in_gam, 16)
            act.activation(gam[:, 1:2], gam[:, 0:1], ACT.Sigmoid).then_inc(gam_sig, 1)
            for b in range(BATCH):
                act.wait_ge(sims_copied, b + 1)
                part = slice(2 * b * SEQ, 2 * (b + 1) * SEQ)
                act.activation(adj[:, part], sims[:, part], ACT.Sigmoid, scale=1.0 / 16).then_inc(sig_done, 1)
            for c in range(NBLK):
                act.wait_ge(in_xt, 16)
                act.activation(xt_hi[:, :, c * BLK:(c + 1) * BLK], xt_raw[:, :, c * BLK:(c + 1) * BLK], ACT.Copy).then_inc(xt_hi_done, 1)

            def fill_copy(what, f, index):
                act.wait_ge(filled, index + 1)
                act.activation(fill_views(what, f)[0], fill_src(what), ACT.Copy).then_inc(fill_hi, 1)

            for index, (what, f) in enumerate(FIRST):
                fill_copy(what, f, index)

            def slot(N, n, q, live, more):
                fills, base = fills_in(n, q, live, more)
                if live(LAG_OUT):
                    act.wait_ge(pv_done, N - LAG_OUT + 1)
                    act.activation(z_hi[:], bank_z[:, 0:2 * P], ACT.Copy).then_inc(z_hi_done, 1)
                if live(LAG_PV):
                    act.wait_ge(turned, N - LAG_PV + 1)
                    act.activation(pt_hi[:], bank_t[:, 0:3 * P], ACT.Copy).then_inc(pt_hi_done, 1)
                if fills:
                    fill_copy(*fills[0], base)
                if live(0):
                    act.wait_ge(neg_done, N + 1)
                    wait(act, norm_done, N * 2)
                    for j, (lo, hi) in enumerate(((0, P), (P, 3 * P))):
                        act.activation(probs[:, lo:hi], s_masked_sb[:, lo:hi], ACT.Exp, bias=neg_max[:, j:j + 1],
                                       scale=SCALE, accum_out=row_sum[:, j:j + 1]).then_inc(exp_done, 1)
                if len(fills) > 1:
                    fill_copy(*fills[1], base + 1)

            item_loop(act, slot)

            act.wait_ge(eps_done, 1)
            act.activation(std[:], vare[:], ACT.Sqrt).then_inc(std_done, 1)
            act.wait_ge(eps_done, 2)
            act.activation(std[:], vare[:], ACT.Sqrt).then_inc(std_done, 1)
            for b in range(BATCH):
                act.wait_ge(x2_turned, 2 * b + 2)
                act.activation(of_batch(xt_hi, b), turned_batch(b), ACT.Copy).then_inc(x2t_hi_done, 1)
            act.wait_ge(route, 3)
            act.activation(exp_all[:], shifted[:], ACT.Exp).then_inc(exps_done, 1)
            act.activation(exp_top[:], top_s[:], ACT.Exp).then_inc(exps_done, 1)

            def ffn_slot(K, k, s, last):
                if not (last and k < 2):
                    act.wait_ge(gu_done, K + 1)
                    wait(act, silu_c_done, K - 1)
                    act.activation(silu_g[k % 2][:], G[k % 2][:], ACT.Silu).then_inc(silu_done, 1)
                if not isinstance(K, int) or K >= 1:
                    if last and k == 1:
                        return
                    act.wait_ge(h_done, K)
                    act.activation(h[(k - 1) % 3][0][:], h_sb[(k - 1) % 2][:], ACT.Copy).then_inc(h_hi_done, 1)

            ffn_loop(act, ffn_slot)
            act.wait_ge(eps_done, 3)
            act.activation(std[:], vare[:], ACT.Sqrt).then_inc(std_done, 1)

        @block.vector
        def _(dve):
            for n, dst in enumerate((cq, cq, ck, ck)):
                if n % 2 == 1:
                    dve.wait_ge(ctx_proj, n + 1)
                    dve.tensor_copy(dst[:, BLK:], acc[n][0:CTX].rearrange("p a b -> p (a b)")).then_inc(ctx_proj_sb, 1)
            dve.wait_ge(gam_sig, 1)
            dve.tensor_scalar(gam[:, 2:3], gam[:, 1:2], 0.5, None, ALU.mult).then_inc(gam_done, 1)
            dve.tensor_scalar(gam[:, 3:4], gam[:, 1:2], -1.0, 2.0, ALU.mult, ALU.add).then_inc(gam_done, 1)
            for b in range(BATCH):
                dve.wait_ge(sims_ready, 2 * b + 2)
                dve.tensor_copy(sims[:, 2 * b * SEQ:2 * (b + 1) * SEQ], sim_banks[b][:]).then_inc(sims_copied, 1)

            def minus_hi(dst, src, hi):
                return dve.tensor_tensor(dst, src, hi.bitcast(F32), ALU.subtract)

            def split_lo(k, q):
                dve.wait_ge(w_hi_done[k], q + 1)
                minus_hi(lo_of[k], raw_of[k], hi_of[k]).then_inc(w_lo_done[k], 1)

            for c in range(NBLK):
                dve.wait_ge(xt_hi_done, c + 1)
                part = slice(c * BLK, (c + 1) * BLK)
                minus_hi(xt_lo[:, :, part], xt_raw[:, :, part], xt_hi[:, :, part]).then_inc(xt_lo_done, 1)
                split_lo("av"[c], 0)

            def fill_rest(what, f, index):
                dve.wait_ge(fill_hi, index + 1)
                hi, lo = fill_views(what, f)
                minus_hi(lo, fill_src(what), hi).then_inc(fill_lo, 1)

            for index, (what, f) in enumerate(FIRST):
                fill_rest(what, f, index)
            split_lo("b", 0)
            split_lo("o", 0)
            dve.wait_ge(gate_hi_done, 1)
            minus_hi(gate_lo[:], gate_raw[:], gate_hi[:]).then_inc(gate_lo_done, 1)

            dve.wait_ge(adj_scaled, BATCH)
            STEPS = 2 * ROUNDS + 1

            def topk(t, j):
                base = t * STEPS if not isinstance(t, int) else t * STEPS
                if j:
                    dve.wait_ge(topk_step, base + j)
                    settle(dve)
                tile = sims[:, bass.ds(t * SEQ, SEQ)]
                if j == 0:
                    ins = dve.tensor_copy(topk_work[0][:], tile)
                elif j == STEPS - 1:
                    last = (TOPK_ADJ - 1) % 8
                    view = adj[:, bass.ds(t * SEQ, SEQ)]
                    ins = dve.scalar_tensor_tensor(out=view, in0=tile, scalar=topk_8[:, last:last + 1], in1=view,
                                                   op0=ALU.is_ge, op1=ALU.mult)
                elif j % 2:
                    ins = dve.max(topk_8[:], topk_work[(j // 2) % 2][:])
                else:
                    ins = dve.match_replace(out=topk_work[(j // 2) % 2][:], in_to_replace=topk_8[:],
                                            in_values=topk_work[(j // 2 + 1) % 2][:], imm_value=-3.0e38)
                ins.then_inc(topk_step, 1)

            TOPK_OF = {3: (0, 3), 4: (3, 6), 5: (6, 9), 6: (9, 12), 7: (12, 15), 0: (15, 17), 1: (17, 19), 2: (19, STEPS)}

            def slot(N, n, q, live, more):
                fills, base = fills_in(n, q, live, more)
                first, end = TOPK_OF[n]
                steps = [(q if n >= LAG_OUT or not more else q - 1, j) for j in range(first, end)] if live(LAG_OUT) else []

                def one_step():
                    if steps:
                        topk(*steps.pop(0))

                if live(LAG_OUT):
                    dve.wait_ge(z_hi_done, N - LAG_OUT + 1)
                    minus_hi(z_lo[:], bank_z[:, 0:2 * P], z_hi[:]).then_inc(z_lo_done, 1)
                one_step()
                if live(LAG_PV):
                    dve.wait_ge(pt_hi_done, N - LAG_PV + 1)
                    minus_hi(pt_lo[:], bank_t[:, 0:3 * P], pt_hi[:]).then_inc(pt_lo_done, 1)
                one_step()
                if fills:
                    fill_rest(*fills[0], base)
                if live(0):
                    dve.wait_ge(scored, N + 1)
                    wait(dve, exp_done, N * 2)
                    settle(dve)
                    dve.tensor_tensor_reduce(out=s_masked_sb[:, 0:P], in0=bank_s[:, 0:P], in1=mask[:, P:], scale=1.0,
                                             scalar=-3.0e38, op0=ALU.add, op1=ALU.max, accum_out=row_max[:, 0:1]).then_inc(masked, 1)
                    dve.tensor_tensor_reduce(out=s_masked_sb[:, P:], in0=bank_s[:, P:3 * P], in1=mask[:], scale=1.0,
                                             scalar=-3.0e38, op0=ALU.add, op1=ALU.max, accum_out=row_max[:, 1:2]).then_inc(masked, 1)
                    dve.wait_ge(masked, N * 2 + 2)
                    dve.tensor_scalar(neg_max[:], row_max[:], -SCALE, None, ALU.mult).then_inc(neg_done, 1)
                one_step()
                if len(fills) > 1:
                    fill_rest(*fills[1], base + 1)
                if live(0):
                    dve.wait_ge(exp_done, N * 2 + 2)
                    wait(dve, norm_done, N * 2)
                    dve.reciprocal(inv_sum[:], row_sum[:]).then_inc(inv_done, 1)
                while steps:
                    one_step()

            item_loop(dve, slot)

            count = [0]

            def link(ins):
                count[0] += 1
                ins.then_inc(ln_step, 1)
                dve.wait_ge(ln_step, count[0])

            def moments(src):
                for t in range(TILES):
                    ins = dve.bn_stats(stats[:, t, :], src(t))
                link(ins)
                for t in range(TILES):
                    ins = dve.bn_aggr(mv[:, t, :], stats[:, t, :])
                link(ins)
                dve.tensor_scalar(vare[:], mv[:, :, 1], EPS, None, ALU.add).then_inc(eps_done, 1)

            def inverse(n):
                dve.wait_ge(std_done, n)
                link(dve.reciprocal(rstd[:], std[:]))

            dve.wait_ge(projected, BATCH * HEADS)
            moments(lambda t: acc[t // 2][:, t % 2, :])
            inverse(1)
            for t in range(TILES):
                dve.tensor_scalar(x1[:, t, :], acc[t // 2][:, t % 2, :], mv[:, t, 0:1], rstd[:, t:t + 1],
                                  ALU.subtract, ALU.mult).then_inc(x1_done, 1)
            for t in range(TILES):
                dve.wait_ge(x1_done, t + 1)
                dve.wait_ge(adj_sum, 2 * (t // 2) + 2)
                dve.scalar_tensor_tensor(out=mixed[:, t, :], in0=x1[:, t, :], scalar=gam[:, 3:4],
                                         in1=sim_banks[t // 2][:, (t % 2) * SEQ:(t % 2 + 1) * SEQ],
                                         op0=ALU.mult, op1=ALU.add).then_inc(mixed_done, 1)
            dve.wait_ge(mixed_done, TILES)
            moments(lambda t: mixed[:, t, :])
            inverse(2)
            for t in range(TILES):
                dve.tensor_scalar(xs[:, t, :], mixed[:, t, :], mv[:, t, 0:1], rstd[:, t:t + 1],
                                  ALU.subtract, ALU.mult).then_inc(x2_done, 1)
            for b in range(BATCH):
                dve.wait_ge(x2t_hi_done, b + 1)
                minus_hi(of_batch(xt_lo, b), turned_batch(b), of_batch(xt_hi, b)).then_inc(x2t_lo_done, 1)

            dve.wait_ge(logits_done, 1)
            link(dve.tensor_copy(logits[:], bank_f[:, 0:TILES * E].rearrange("p (t e) -> p t e", e=E)))
            for t in range(TILES):
                ins = dve.max(top_v[:, t, :], logits[:, t, :])
            link(ins)
            for t in range(TILES):
                ins = dve.max_index(top_i[:, t, :], top_v[:, t, :], logits[:, t, :])
            ins.then_inc(route, 1)
            first = top_v[:, :, 0:1]
            dve.tensor_tensor(shifted[:], logits[:], first.to_broadcast([P, TILES, E]), ALU.subtract).then_inc(route, 1)
            dve.tensor_tensor(top_s[:], top_v[:], first.to_broadcast([P, TILES, TOP]), ALU.subtract).then_inc(route, 1)
            dve.wait_ge(route, 1)
            link(dve.tensor_copy(top_if[:], top_i[:]))
            iota_b = iota_e[:].rearrange("p (a e) -> p a e", a=1).to_broadcast([P, TILES * TOP, E])
            idx_b = top_if[:].rearrange("p t (k a) -> p (t k) a", a=1).to_broadcast([P, TILES * TOP, E])
            dve.tensor_tensor(onehot[:].rearrange("p t k e -> p (t k) e"), idx_b, iota_b, ALU.is_equal).then_inc(route, 1)
            dve.wait_ge(exps_done, 2)
            link(dve.tensor_reduce(sum_all[:], exp_all[:], AX.X, ALU.add))
            link(dve.reciprocal(inv_all[:], sum_all[:]))
            def col(a, n):
                return a[:].rearrange("p (t o) -> p t o", o=1).to_broadcast([P, TILES, n])
            link(dve.tensor_tensor(prob_top[:], exp_top[:], col(inv_all, TOP), ALU.mult))
            link(dve.tensor_reduce(sum_top[:], prob_top[:], AX.X, ALU.add))
            link(dve.tensor_scalar(sum_top_c[:], sum_top[:], 1.0e-12, None, ALU.max))
            link(dve.reciprocal(inv_top[:], sum_top_c[:]))
            link(dve.tensor_tensor(route_w[:], prob_top[:], col(inv_top, TOP), ALU.mult))
            for t in range(TILES):
                w_b = route_w[:, t, PRIM:].rearrange("p (k a) -> p k a", a=1).to_broadcast([P, TOP - PRIM, E])
                ins = dve.tensor_tensor(sec_each[:, t], onehot[:, t, PRIM:, :], w_b, ALU.mult)
            link(ins)
            link(dve.tensor_reduce(sec_w[:], sec_each[:].rearrange("p t k e -> p t e k"), AX.X, ALU.add))
            dve.wait_ge(onehot_turned, TILES)
            for half in range(2):
                dve.tensor_copy(onehot_t[:, 4 * half:4 * half + 4, :],
                                (bank_s if half == 0 else bank_t)[:].rearrange("p (t n) -> p t n", t=4)).then_inc(onehot_sb, 1)
            for half in range(2):
                dve.wait_ge(cand_done, 4 * half + 4)
                ins = dve.tensor_copy(cand[:, 4 * half:4 * half + 4].rearrange("p t k e -> p (t k e)"), (bank_z if half == 0 else bank_f)[:])
            link(ins)
            link(dve.tensor_reduce(best[:], cand[:].rearrange("p t k e -> p t e k"), AX.X, ALU.max))
            link(dve.scalar_tensor_tensor(out=moved[0][:], in0=best[:], scalar=0.5, in1=sec_w[:], op0=ALU.is_ge, op1=ALU.mult))
            dve.tensor_tensor(kept[:], sec_w[:], moved[0][:], ALU.subtract)
            for i in range(PRIM):
                ins = dve.tensor_tensor(is_best[:, :, i, :], cand[:, :, i, :], best[:], ALU.is_equal)
            link(ins)
            for i in range(PRIM):
                link(dve.tensor_tensor(take[:, :, i, :], is_best[:, :, i, :], moved[i][:], ALU.mult))
                if i < PRIM - 1:
                    link(dve.tensor_tensor(moved[i + 1][:], moved[i][:], take[:, :, i, :], ALU.subtract))
            link(dve.tensor_reduce(taken[:], take[:], AX.X, ALU.add))
            link(dve.tensor_tensor(prim_w[:], taken[:], route_w[:, :, 0:PRIM], ALU.add))
            for t in range(TILES):
                w_b = prim_w[:, t].rearrange("p (k a) -> p k a", a=1).to_broadcast([P, PRIM, E])
                ins = dve.tensor_tensor(prim_each[:, t], onehot[:, t, 0:PRIM, :], w_b, ALU.mult)
            link(ins)
            link(dve.tensor_reduce(prim_all[:], prim_each[:].rearrange("p t k e -> p t e k"), AX.X, ALU.add))
            dve.tensor_tensor(combine[:], prim_all[:], kept[:], ALU.add).then_inc(route, 1)
            dve.wait_ge(combine_turned, TILES)
            dve.tensor_copy(combine_t[:, 0:BLK], bank_s[0:E, :])
            dve.tensor_copy(combine_t[:, BLK:], bank_t[0:E, :]).then_inc(combine_sb, 1)

            def split_ffn(i, s):
                dve.wait_ge(wf_hi_done[i], s + 1)
                minus_hi(wf[i][1][:], wf_raw[i][:], wf[i][0][:]).then_inc(wf_lo_done[i], 1)

            for i in range(FG - 1):
                split_ffn(i, 0)

            def ffn_slot(K, k, s, last):
                if not (last and k < 2):
                    dve.wait_ge(silu_c_done, K + 1)
                    wait(dve, h_lo_done, K - 1)
                    dve.tensor_tensor(h_sb[k % 2][:], U[k % 2][:], silu_c[k % 2][:], ALU.mult).then_inc(h_done, 1)
                if (not isinstance(K, int) or K >= 1) and not (last and k == 1):
                    dve.wait_ge(h_hi_done, K)
                    minus_hi(h[(k - 1) % 3][1][:], h_sb[(k - 1) % 2][:], h[(k - 1) % 3][0][:]).then_inc(h_lo_done, 1)
                split_at_slot(k, s, K, last, split_ffn)

            ffn_loop(dve, ffn_slot)

            dve.wait_ge(down_done, FT * NBLK)
            moments(lambda t: acc[t // 2][:, t % 2, :])
            inverse(3)
            for t in range(TILES):
                dve.tensor_scalar(y_sb[:, t, :], acc[t // 2][:, t % 2, :], mv[:, t, 0:1], rstd[:, t:t + 1],
                                  ALU.subtract, ALU.mult).then_inc(y_done, 1)

        @block.tensor
        def _(pe):
            def three(dst, a, b, start, stop, first_of=True):
                (ah, al), (bh, bl) = a, b
                pe.matmul(dst, ah, bh, start=start, stop=False, skip_group_check=True)
                pe.matmul(dst, ah, bl, start=False, stop=False, skip_group_check=True)
                return pe.matmul(dst, al, bh, start=False, stop=stop, skip_group_check=True)

            pe.wait_ge(in_ctx, 16)
            pe.wait_ge(in_wctx, 16)
            for n in range(4):
                pe.matmul(acc[n][0:CTX].rearrange("p a b -> p (a b)"), wctx_sb[:, n // 2, :],
                          ctx_sb[:, (n % 2) * BLK:(n % 2 + 1) * BLK], start=True, stop=True).then_inc(ctx_proj, 1)
            pe.wait_ge(ctx_proj_sb, 4)
            for t in range(TILES):
                b = t // 2
                pe.matmul(sim_banks[t // 2][:, (t % 2) * SEQ:(t % 2 + 1) * SEQ], cq[:, t * P:(t + 1) * P],
                          ck[:, b * SEQ:(b + 1) * SEQ], start=True, stop=True).then_inc(sims_ready, 1)
            pe.wait_ge(in_x, 16)
            pe.wait_ge(const_made, 3)

            def seed(t):
                return pe.matmul(acc[t // 2][:, t % 2, :], ident[:], xs[:, t, :], start=(t % 2 == 0), stop=(t % 2 == 1),
                                 skip_group_check=True)
            for t in range(TILES):
                ins = seed(t)
            ins.then_inc(seeded, 1)

            def fill(what, f, index):
                wait(pe, fill_lo, index)
                g = f // 2
                if what == "v":
                    for j in range(2):
                        t = 2 * f + j
                        for c in range(KC):
                            tok = slice(t * P, (t + 1) * P)
                            ins = three(bank_f[:, j * 2 * P:(j + 1) * 2 * P], (xt_hi[:, c, tok], xt_lo[:, c, tok]),
                                        (wv_hi[:, c, :], wv_lo[:, c, :]), j == 0 and c == 0, j == 1 and c == KC - 1)
                else:
                    hi, lo = (wa_hi, wa_lo) if g == 0 else (wb_hi, wb_lo)
                    s, part = "qk".index(what), slice((f % 2) * BLK, (f % 2 + 1) * BLK)
                    for c in range(KC):
                        ins = three(bank_f[:], (hi[:, s, c, :], lo[:, s, c, :]), (xt_hi[:, c, part], xt_lo[:, c, part]),
                                    c == 0, c == KC - 1)
                ins.then_inc(filled, 1)

            pe.wait_ge(sims_copied, BATCH)
            pe.wait_ge(xt_lo_done, NBLK)
            pe.wait_ge(w_lo_done["a"], 1)
            pe.wait_ge(w_lo_done["v"], 1)
            for index, (what, f) in enumerate(FIRST):
                fill(what, f, index)

            def need_weights(what, f, q):
                if (what, f) == ("q", 0):
                    pe.wait_ge(w_lo_done["a"], q + 2)
                elif (what, f) == ("v", 0):
                    pe.wait_ge(w_lo_done["v"], q + 2)
                elif (what, f) == ("q", 2):
                    pe.wait_ge(w_lo_done["b"], q + 1)

            def slot(N, n, q, live, more):
                fills, base = fills_in(n, q, live, more)
                if live(LAG_PV):
                    pe.wait_ge(norm_done, (N - LAG_PV) * 2 + 2)
                    wait(pe, pt_lo_done, N - LAG_PV)
                    for j in range(3):
                        ins = pe.transpose(bank_t[:, j * P:(j + 1) * P], probs_n[n % 2][:, j * P:(j + 1) * P], ident[:])
                    ins.then_inc(turned, 1)
                if fills:
                    need_weights(*fills[0], q)
                    fill(*fills[0], base)
                if live(0):
                    g = n // 2
                    pe.wait_ge(fill_lo, PER_PAIR * q + ORDER["k", g] + 1)
                    wait(pe, masked, N * 2)
                    (hi, lo), off = qk[g % 2], (n % 2) * SEQ
                    for j in range(2):
                        tok, keys = slice(off + j * P, off + (j + 1) * P), slice(off, off + (j + 1) * P)
                        ins = three(bank_s[:, (0, P)[j]:(P, 3 * P)[j]], (hi[:, 0, tok], lo[:, 0, tok]),
                                    (hi[:, 1, keys], lo[:, 1, keys]), j == 0, j == 1)
                    ins.then_inc(scored, 1)
                if live(LAG_OUT):
                    m = (n - LAG_OUT) % 8
                    a, b = m // 4, m % 4
                    pe.wait_ge(z_lo_done, N - LAG_OUT + 1)
                    if b == 0:
                        pe.wait_ge(w_lo_done["op"[a]], q + 1)
                    for j in range(2):
                        part = slice(j * P, (j + 1) * P)
                        ins = three(acc[b][:, j, :], (z_hi[:, part], z_lo[:, part]), (wo[a][0][:], wo[a][1][:]), False, False)
                    ins.then_inc(projected, 1)
                if len(fills) > 1:
                    need_weights(*fills[1], q)
                    fill(*fills[1], base + 1)
                if live(LAG_PV):
                    m = (n - LAG_PV) % 8
                    a, b = m // 4, m % 4
                    pe.wait_ge(pt_lo_done, N - LAG_PV + 1)
                    if a == 0:
                        pe.wait_ge(fill_lo, PER_PAIR * q + ORDER["v", b] + 1)
                    wait(pe, z_lo_done, N - LAG_PV)
                    e = slice(a * DH, (a + 1) * DH)
                    three(bank_z[:, 0:2 * P], (v_hi[:, 2 * b, e], v_lo[:, 2 * b, e]), (pt_hi[:, 0:2 * P], pt_lo[:, 0:2 * P]), True, False)
                    three(bank_z[:, P:2 * P], (v_hi[:, 2 * b + 1, e], v_lo[:, 2 * b + 1, e]),
                          (pt_hi[:, 2 * P:], pt_lo[:, 2 * P:]), False, True).then_inc(pv_done, 1)

            item_loop(pe, slot)

            pe.wait_ge(topk_step, TILES * (2 * ROUNDS + 1))
            for t in range(TILES):
                b, r = t // 2, t % 2
                dst = sim_banks[b]
                for c in range(2):
                    part = dst[:, r * SEQ + c * P:r * SEQ + (c + 1) * P]
                    blk = adj[:, (2 * b + c) * SEQ + r * P:(2 * b + c) * SEQ + (r + 1) * P]
                    pe.matmul(part, blk, ident[:], start=(r == 0 and c == 0), stop=False, skip_group_check=True)
                ins = pe.matmul(dst[:, r * SEQ:(r + 1) * SEQ], ident[:], adj[:, t * SEQ:(t + 1) * SEQ], start=False,
                                stop=True, skip_group_check=True)
                ins.then_inc(adj_sum, 1)
            pe.wait_ge(mixed_done, TILES)
            for t in range(TILES):
                pe.wait_ge(x2_done, t + 1)
                for c in range(KC):
                    ins = pe.transpose(turn_bank(t)[:, c, :], xs[:, t, c * P:(c + 1) * P], ident[:])
                ins.then_inc(x2_turned, 1)
            for t in range(TILES):
                ins = seed(t)
            ins.then_inc(seeded2, 1)
            pe.wait_ge(gate_lo_done, 1)
            pe.wait_ge(x2t_lo_done, BATCH)
            for t in range(TILES):
                tok = slice(t * P, (t + 1) * P)
                for c in range(KC):
                    ins = three(bank_f[:, t * E:(t + 1) * E], (xt_hi[:, c, tok], xt_lo[:, c, tok]), (gate_hi[:, c, :], gate_lo[:, c, :]),
                                t == 0 and c == 0, t == TILES - 1 and c == KC - 1)
            ins.then_inc(logits_done, 1)
            pe.wait_ge(route, 4)
            for t in range(TILES):
                dst = (bank_s if t < 4 else bank_t)[:, (t % 4) * P:(t % 4 + 1) * P]
                pe.transpose(dst, onehot[:, t, 0:PRIM, :].rearrange("p k e -> p (k e)"), ident[:]).then_inc(onehot_turned, 1)
            pe.wait_ge(bd_made, 1)
            for t in range(TILES):
                pe.wait_ge(onehot_sb, t // 4 + 1)
                dst = (bank_z if t < 4 else bank_f)[:, (t % 4) * P:(t % 4 + 1) * P]
                pe.matmul(dst, onehot_t[:, t, :], blockdiag[:], start=(t % 4 == 0), stop=(t % 4 == 3),
                          skip_group_check=True).then_inc(cand_done, 1)
            pe.wait_ge(route, 5)
            for t in range(TILES):
                dst = (bank_s if t < 4 else bank_t)[0:E, (t % 4) * P:(t % 4 + 1) * P]
                pe.transpose(dst, combine[:, t, :], ident[:]).then_inc(combine_turned, 1)
            pe.wait_ge(combine_sb, 1)

            def ffn_slot(K, k, s, last):
                i, c = k // 2, k % 2
                if not (last and k < 2):
                    if c == 0:
                        pe.wait_ge(wf_lo_done[i], s + 1)
                    wait(pe, h_done, K - 1)
                    hi, lo = wf[i]
                    part = slice(c * BLK, (c + 1) * BLK)
                    for g, bank in enumerate((G[k % 2], U[k % 2])):
                        for d in range(KC):
                            w = slice((g * KC + d) * P, (g * KC + d + 1) * P)
                            ins = three(bank[:], (hi[:, w], lo[:, w]), (xt_hi[:, d, part], xt_lo[:, d, part]), d == 0, d == KC - 1)
                    ins.then_inc(gu_done, 1)
                if not isinstance(K, int) or K >= 2:
                    j = ((k - 2) % (2 * FG)) // 2
                    hi, lo = wf[j]
                    pe.wait_ge(h_lo_done, K - 1)
                    hh, hl = h[(k - 2) % 3]
                    for t in range(4):
                        tile, tok = 4 * c + t, slice(t * P, (t + 1) * P)
                        ins = three(acc[tile // 2][:, tile % 2, :], (hh[:, tok], hl[:, tok]), (hi[:, 4 * P:], lo[:, 4 * P:]), False, False)
                    ins.then_inc(down_done, 1)

            ffn_loop(pe, ffn_slot)


_OUT = [((BATCH, SEQ, D), "float32")]


def kernel(x, ctx_512, L0_attn_W_Q, L0_attn_W_K, L0_attn_W_V, L0_attn_W_O, L0_xattn_Wq, L0_xattn_Wk,
           L0_xattn_gamma_raw, L0_ffn_gate_weight, L0_ffn_gate_up_proj, L0_ffn_down_proj, L0_ffn_similarity):
    import numpy as np
    import concourse.bacc as bacc
    from concourse.bass_utils import run_bass_kernel_spmd as run

    def heads_t(w):
        return np.asarray(w).reshape(HEADS, DH, KC, P).transpose(0, 3, 2, 1)

    tokens = np.asarray(x).reshape(TOK, D)
    w_qk = np.stack([heads_t(L0_attn_W_Q), heads_t(L0_attn_W_K)], axis=2).reshape(HEADS, P, -1)
    w_v = heads_t(L0_attn_W_V).reshape(PAIRS, 2, P, KC, DH).transpose(0, 2, 3, 1, 4).reshape(PAIRS, P, -1)
    gate_up = np.asarray(L0_ffn_gate_up_proj).reshape(E, 2, FF, D).transpose(1, 0, 2, 3).reshape(2, FT, P, KC, P)
    w_ffn = np.concatenate([gate_up.transpose(1, 4, 0, 3, 2).reshape(FT, P, -1),
                            np.asarray(L0_ffn_down_proj).transpose(0, 2, 1).reshape(FT, P, D)], axis=2)
    arrays = {
        "x_tok": tokens,
        "x_t": tokens.reshape(TOK, KC, P).transpose(2, 1, 0),
        "w_qk": w_qk,
        "w_v": w_v,
        "w_o": np.asarray(L0_attn_W_O).transpose(0, 2, 1),
        "ctx_t": np.asarray(ctx_512).reshape(TOK, CTX).T,
        "w_ctx": np.stack([np.asarray(L0_xattn_Wq).T, np.asarray(L0_xattn_Wk).T], axis=1),
        "gamma_raw": np.asarray(L0_xattn_gamma_raw).reshape(1, 1),
        "gate_t": np.asarray(L0_ffn_gate_weight).reshape(E, KC, P).transpose(2, 1, 0),
        "w_ffn": w_ffn,
        "sim_t": np.asarray(L0_ffn_similarity).T,
    }
    arrays = {k: np.ascontiguousarray(v) for k, v in arrays.items()}
    nc = bacc.Bacc("TRN2", target_bir_lowering=False, num_devices=1)
    args = {k: nc.dram_tensor(k, v.shape, mybir.dt.from_np(v.dtype), kind="ExternalInput").ap() for k, v in arrays.items()}
    out = nc.dram_tensor("out", [TOK, D], F32, kind="ExternalOutput").ap()
    program(nc, **args, out=out)
    r = run(nc, [arrays], core_ids=[0])
    return r.results[0]["out"].reshape(BATCH, SEQ, D)
```

```python
from contextlib import ExitStack

import concourse.bass as bass
from concourse import mybir

F32 = mybir.dt.float32
F32R = mybir.dt.float32r
U32 = mybir.dt.uint32
ALU = mybir.AluOpType
ACT = mybir.ActivationFunctionType
AX = mybir.AxisListType

P = 128
BATCH, SEQ, D = 4, 256, 256
TOK = BATCH * SEQ
TILES = TOK // P
KC = D // P
HEADS, DH = 16, 128
PAIRS = HEADS // 2
CTX = 64
TOPK_ADJ = int(SEQ * 0.3)
E, FF = 32, 96
TOP, PRIM = 8, 4
FT = E * FF // P
FG = 3
EARLY = 2 * FG
FSTEPS = (FT - EARLY) // FG
BLK = 512
NBLK = TOK // BLK
EARLY_BLOCKS = [(i, c) for c in range(NBLK) for i in range(EARLY)]
EB = len(EARLY_BLOCKS)
HALF = TILES // 2
NEG = -1.0e9
EPS = 1.0e-5
SCALE = float(DH) ** -0.5
ROUNDS = (TOPK_ADJ + 7) // 8


def fills_of_slot(n):
    return {0: [("v", 1)], 1: [("k", 1), ("v", 2)], 2: [("q", 2)], 3: [("k", 2), ("v", 3)],
            4: [("q", 3)], 5: [("k", 3), ("q", 0)], 6: [("k", 0)], 7: [("v", 0), ("q", 1)]}[n]


PER_PAIR = sum(len(fills_of_slot(n)) for n in range(8))
FIRST = [("q", 0), ("k", 0), ("v", 0), ("q", 1)]
AT_SLOT = [sum(len(fills_of_slot(m)) for m in range(n)) for n in range(8)]
ORDER = {f: n for n, f in enumerate(FIRST)}
ORDER.update({f: len(FIRST) + AT_SLOT[n] + m
              for n in range(8) for m, f in enumerate(fills_of_slot(n)) if f not in FIRST})


def program(nc, x_tok, x_t, w_qk, w_v, w_o, ctx_t, w_ctx, gamma_raw, gate_t, w_ffn, sim_t, out):
    ctx = ExitStack()
    with ctx:
        def sb(name, shape, dt=F32):
            return ctx.enter_context(nc.sbuf_tensor(name, shape, dt))

        def pair(name, shape):
            return sb(name + "_hi", shape, F32R), sb(name + "_lo", shape, F32R)

        def ps(name, shape):
            return ctx.enter_context(nc.psum_tensor(name, shape, F32))

        def sem(name):
            return ctx.enter_context(nc.semaphore(name))

        ident = sb("ident", [P, P])
        mask = sb("mask", [P, 2 * P])
        iota_e = sb("iota_e", [P, E])
        xs = sb("xs", [P, TILES, D])
        xt_hi, xt_lo = pair("xt", [P, KC, TOK])
        one = sb("one", [P, 1])
        zero = sb("zero", [P, 1])
        adj = sb("adj", [P, TILES * SEQ])
        gam = sb("gam", [P, 4])
        stats = sb("stats", [P, TILES, 6])
        mv = sb("mv", [P, TILES, 2])
        std, rstd, shift = sb("std", [P, TILES]), sb("rstd", [P, TILES]), sb("shift", [P, TILES])
        eps_col = sb("eps_col", [P, 1])
        gate_raw = sb("gate_raw", [P, KC, E])
        gate_hi, gate_lo = pair("gate", [P, KC, E])
        blockdiag = sb("blockdiag", [P, P])
        wf_raw = [sb(f"wf_raw{i}", [P, 6 * P]) for i in range(EARLY)]
        wf = [pair(f"wf{i}", [P, 6 * P]) for i in range(EARLY)]
        att = ExitStack()

        def att_sb(name, shape, dt=F32):
            return att.enter_context(nc.sbuf_tensor(name, shape, dt))

        def att_pair(name, shape):
            return att_sb(name + "_hi", shape, F32R), att_sb(name + "_lo", shape, F32R)

        xt_raw = att_sb("xt_raw", [P, KC, TOK])
        raw_a, raw_b = att_sb("raw_a", [P, 2, KC, P]), att_sb("raw_b", [P, 2, KC, P])
        raw_v = att_sb("raw_v", [P, KC, 2 * P])
        raw_o = [att_sb("raw_o0", [P, D]), att_sb("raw_o1", [P, D])]
        wa_hi, wa_lo = att_pair("wa", [P, 2, KC, P])
        wb_hi, wb_lo = att_pair("wb", [P, 2, KC, P])
        wv_hi, wv_lo = att_pair("wv", [P, KC, 2 * P])
        wo = [att_pair("wo0", [P, D]), att_pair("wo1", [P, D])]
        qk = [att_pair("qk0", [P, 2, BLK]), att_pair("qk1", [P, 2, BLK])]
        v_hi, v_lo = att_pair("v", [P, TILES, 2 * DH])
        s_masked_sb = att_sb("s_masked_sb", [P, 3 * P])
        row_max, neg_max = att_sb("row_max", [P, 2]), att_sb("neg_max", [P, 2])
        row_sum, inv_sum = att_sb("row_sum", [P, 2]), att_sb("inv_sum", [P, 2])
        probs, probs_n = att_sb("probs", [P, 3 * P]), [att_sb(f"probs_n{i}", [P, 3 * P]) for i in range(2)]
        pt_hi, pt_lo = att_pair("pt", [P, 3 * P])
        z_hi, z_lo = att_pair("z", [P, 2 * P])
        ctx_sb = att_sb("ctx_sb", [CTX, TOK])
        wctx_sb = att_sb("wctx_sb", [CTX, 2, CTX])
        cq, ck = att_sb("cq", [CTX, TOK]), att_sb("ck", [CTX, TOK])
        sims = att_sb("sims", [P, TILES * SEQ])
        topk_work = [att_sb("topk_work0", [P, SEQ]), att_sb("topk_work1", [P, SEQ])]
        topk_8 = att_sb("topk_8", [P, 8])
        att.close()
        logits_t = sb("logits_t", [E, TOK])
        shifted = sb("shifted", [P, TILES, E])
        top_v, top_s = sb("top_v", [P, TILES, TOP]), sb("top_s", [P, TILES, TOP])
        top_i, top_if = sb("top_i", [P, TILES, TOP], U32), sb("top_if", [P, TILES, TOP])
        exp_all, exp_top = sb("exp_all", [P, TILES, E]), sb("exp_top", [P, TILES, TOP])
        sum_all, inv_all = sb("sum_all", [P, TILES]), sb("inv_all", [P, TILES])
        sum_top, inv_top = sb("sum_top", [P, TILES]), sb("inv_top", [P, TILES])
        sum_top_c, inv_both = sb("sum_top_c", [P, TILES]), sb("inv_both", [P, TILES])
        prob_top, route_w = sb("prob_top", [P, TILES, TOP]), sb("route_w", [P, TILES, TOP])
        onehot, onehot_s = sb("onehot", [P, TILES, PRIM, E]), sb("onehot_s", [P, TILES, TOP - PRIM, E])
        onehot_t = sb("onehot_t", [P, TILES, P])
        sec_part = [sb(f"sec_part{i}", [P, TILES, E]) for i in range(2)]
        sec_mask, sec_exp, sec_w = (sb(n, [P, TILES, E]) for n in ("sec_mask", "sec_exp", "sec_w"))
        cand = sb("cand", [P, TILES, PRIM, E])
        best = sb("best", [P, TILES, E])
        moved = [sb(f"moved{i}", [P, TILES, E]) for i in range(PRIM)]
        is_best = sb("is_best", [P, TILES, PRIM, E])
        take = sb("take", [P, TILES, PRIM, E])
        taken, prim_w = sb("taken", [P, TILES, PRIM]), sb("prim_w", [P, TILES, PRIM])
        prim_each = sb("prim_each", [P, TILES, PRIM, E])
        prim_all, kept = sb("prim_all", [P, TILES, E]), sb("kept", [P, TILES, E])
        combine = sb("combine", [P, TILES, E])
        combine_t = sb("combine_t", [E, TOK])
        cw = [sb(f"cw{i}", [P, TOK]) for i in range(EARLY)]
        early_h = [sb(f"early_h{n}", [P, BLK]) for n in range(EB)]
        early_u = [sb(f"early_u{i}", [P, BLK]) for i in range(2)]
        silu_g, silu_c, h_sb = early_h[0:2], early_h[2:4], early_h[4:6]
        h = [pair(f"h{i}", [P, BLK]) for i in range(3)]
        y_sb = xs

        combine_dram = nc.dram_tensor("combine_dram", [E, TOK], F32, kind="Internal").ap()

        acc = [ps(f"acc{b}", [P, 2, D]) for b in range(BATCH)]
        bank_f, bank_s = ps("bank_f", [P, BLK]), ps("bank_s", [P, BLK])
        bank_t, bank_z = ps("bank_t", [P, BLK]), ps("bank_z", [P, BLK])
        sim_banks = [bank_f, bank_s, bank_t, bank_z]

        in_x, in_xt, in_ctx, in_wctx, in_gam = (sem(f"in_{n}") for n in ("x", "xt", "ctx", "wctx", "gam"))
        in_gate, in_sim = sem("in_gate"), sem("in_sim")
        PIECES = "abvop"
        w_in, w_hi_done, w_lo_done = ({k: sem(f"w{k}_{s}") for k in PIECES} for s in ("in", "hi_done", "lo_done"))
        const_made, const_zero = sem("const_made"), sem("const_zero")
        xt_hi_done, xt_lo_done = sem("xt_hi_done"), sem("xt_lo_done")
        ctx_proj, ctx_proj_sb = sem("ctx_proj"), sem("ctx_proj_sb")
        sims_ready, sims_copied, sig_done, adj_scaled = (sem(n) for n in ("sims_ready", "sims_copied", "sig_done", "adj_scaled"))
        gam_sig, gam_done = sem("gam_sig"), sem("gam_done")
        seeded = sem("seeded")
        passed_pool, passed_dve = sem("passed_pool"), sem("passed_dve")
        filled, fill_hi, fill_lo = sem("filled"), sem("fill_hi"), sem("fill_lo")
        scored, masked, neg_done, exp_done = (sem(n) for n in ("scored", "masked", "neg_done", "exp_done"))
        inv_done, norm_done, turned = sem("inv_done"), sem("norm_done"), sem("turned")
        pt_hi_done, pt_lo_done, pv_done = sem("pt_hi_done"), sem("pt_lo_done"), sem("pv_done")
        z_hi_done, z_lo_done, projected = sem("z_hi_done"), sem("z_lo_done"), sem("projected")
        topk_step = sem("topk_step")
        stats_done, mv_done, std_done, rstd_done, shift_done, normed = (
            [sem(f"{n}{i}") for i in range(3)] for n in ("stats_done", "mv_done", "std_done", "rstd_done", "shift_done", "normed"))
        adj_sum, mixed_done = sem("adj_sum"), sem("mixed_done")
        x2_turned, x2t_hi_done, x2t_lo_done = sem("x2_turned"), sem("x2t_hi_done"), sem("x2t_lo_done")
        gate_hi_done, gate_lo_done, logits_done = sem("gate_hi_done"), sem("gate_lo_done"), sem("logits_done")
        logits_t_done, logits_t_out = sem("logits_t_done"), sem("logits_t_out")
        link_step, index_done, shifts_done, exps_done = (sem(n) for n in ("link_step", "index_done", "shifts_done", "exps_done"))
        onehot_done, secondary_done, onehot_turned, onehot_sb, cand_done, cand_sb = (
            sem(n) for n in ("onehot_done", "secondary_done", "onehot_turned", "onehot_sb", "cand_done", "cand_sb"))
        sec_step, sec_exp_done, moved_done, kept_done = (sem(n) for n in ("sec_step", "sec_exp_done", "moved_done", "kept_done"))
        combined, bd_made = sem("combined"), sem("bd_made")
        combine_turned, combine_sb, combine_out = (sem(n) for n in ("combine_turned", "combine_sb", "combine_out"))
        wf_in, wf_hi_done, wf_lo_done, cw_in = ([sem(f"{n}{i}") for i in range(EARLY)] for n in ("wf_in", "wf_hi", "wf_lo", "cw_in"))
        early_u_done, early_product, early_weighed = sem("early_u_done"), sem("early_product"), [sem(f"early_weighed{i}") for i in range(2)]
        gu_done, silu_done, silu_c_done, h_done, h_hi_done, h_lo_done, down_done = (
            sem(n) for n in ("gu_done", "silu_done", "silu_c_done", "h_done", "h_hi_done", "h_lo_done", "down_done"))
        y_done, y_out = [sem(f"y_done{b}") for b in range(BATCH)], [sem(f"y_out{b}") for b in range(BATCH)]

        def wait(eng, semaphore, value):
            if not isinstance(value, int) or value > 0:
                eng.wait_ge(semaphore, value)

        def settle(eng):
            eng.sem_inc(passed_pool if eng is nc.gpsimd else passed_dve, 1)

        raw_of = {"a": raw_a[:].rearrange("p s c e -> p (s c e)"), "b": raw_b[:].rearrange("p s c e -> p (s c e)"),
                  "v": raw_v[:].rearrange("p c e -> p (c e)"), "o": raw_o[0][:], "p": raw_o[1][:]}
        hi_of = {"a": wa_hi[:].rearrange("p s c e -> p (s c e)"), "b": wb_hi[:].rearrange("p s c e -> p (s c e)"),
                 "v": wv_hi[:].rearrange("p c e -> p (c e)"), "o": wo[0][0][:], "p": wo[1][0][:]}
        lo_of = {"a": wa_lo[:].rearrange("p s c e -> p (s c e)"), "b": wb_lo[:].rearrange("p s c e -> p (s c e)"),
                 "v": wv_lo[:].rearrange("p c e -> p (c e)"), "o": wo[0][1][:], "p": wo[1][1][:]}

        def piece_dram(k, q):
            if k == "v":
                return w_v[bass.ds(q, 1)].rearrange("o p n -> p (o n)")
            src, head = (w_qk if k in "ab" else w_o), 2 * q + (k in "bp")
            return src[bass.ds(head, 1)].rearrange("o p n -> p (o n)")

        SPLIT_SLOT = {3: ("a", 1), 4: ("p", 0), 5: ("v", 1), 6: ("b", 1), 0: ("o", 0)}
        LAG_PV, LAG_OUT = 2, 3

        def item_loop(eng, slot):
            for k in range(LAG_OUT):
                slot(k, k, 0, lambda lag, k=k: k >= lag, True)
            with eng.Fori(0, PAIRS - 1) as q:
                for k in range(LAG_OUT, LAG_OUT + 8):
                    slot(q * 8 + k, k % 8, q + k // 8, lambda lag: True, True)
            for k in range(LAG_OUT, LAG_OUT + 8):
                slot(8 * (PAIRS - 1) + k, k % 8, PAIRS - 1, lambda lag, k=k: k - lag < 8, False)

        def fills_in(n, q, live, more):
            fills = [f for f in fills_of_slot(n) if live(0) and (more or f not in FIRST)]
            return fills, PER_PAIR * q + len(FIRST) + AT_SLOT[n]

        def fill_views(what, f):
            if what == "v":
                return v_hi[:, 2 * f:2 * f + 2, :], v_lo[:, 2 * f:2 * f + 2, :]
            hi, lo = qk[f % 2]
            s = "qk".index(what)
            return hi[:, s, :], lo[:, s, :]

        def fill_src(what):
            return bank_f[:] if what != "v" else bank_f[:].rearrange("p (t e) -> p t e", t=2)

        def turned_batch(b):
            return sim_banks[b][:].rearrange("p (t c n) -> p t c n", t=2, c=KC)

        def of_batch(xt, b):
            return xt[:, :, b * SEQ:(b + 1) * SEQ].rearrange("p c (t n) -> p t c n", t=2)

        logits_t_bank, logits_bank = [acc[0], acc[2]], [acc[1], acc[3]]
        onehot_bank, cand_bank, combine_bank = logits_t_bank, logits_bank, logits_t_bank

        def bank_tile(bank, j, rows=P):
            return bank[0:rows].rearrange("p a d -> p (a d)")[:, j * P:(j + 1) * P]

        def whole(bank, rows=P):
            return bank[0:rows].rearrange("p a d -> p (a d)")

        G, U = [bank_f, bank_t], [bank_s, bank_z]

        def split_at_slot(k, s, K, last, split):
            if k == 4 and not last:
                split(0, s + 1)
            elif k == 0 and not isinstance(K, int):
                split(1, s)
            elif k == 2:
                split(2, s)

        def ffn_loop(eng, slot):
            slot(0, 0, 0, False)
            slot(1, 1, 0, False)
            with eng.Fori(0, FSTEPS - 1) as s:
                for k in range(2, 2 * FG + 2):
                    slot(s * 2 * FG + k, k % (2 * FG), s + k // (2 * FG), False)
            for k in range(2, 2 * FG + 2):
                slot(2 * FG * (FSTEPS - 1) + k, k % (2 * FG), FSTEPS - 1, True)

        LAST = BATCH * HEADS
        ADJ_AT = {(LAST, "turned"): 0, (LAST + 1, "projected"): 1, (LAST + 1, "end"): 2, (LAST + 2, "end"): 3}
        EARLY_SPLIT = {3: 0, 5: 1, 6: 2, 7: 3, 0: 4, 1: 5}
        DVE_DRAIN = {
            LAST: [("stats", 0, 0), ("moments", 0, 0)],
            LAST + 1: [("inverse", 0, 0), ("stats", 0, 1), ("shift", 0, 0), ("moments", 0, 1)],
            LAST + 2: [("inverse", 0, 1), ("stats", 0, 2), ("shift", 0, 1), ("moments", 0, 2), ("mix", 0), ("stats", 1, 0)]}
        DVE_MID = [
            ("mix", 1), ("moments", 1, 0), ("stats", 1, 1), ("inverse", 0, 2), ("inverse", 1, 0), ("moments", 1, 1),
            ("shift", 1, 0), ("shift", 0, 2), ("inverse", 1, 1), ("stats", 0, 3), ("shift", 1, 1), ("moments", 0, 3),
            ("mix", 2), ("stats", 1, 2), ("inverse", 0, 3), ("moments", 1, 2), ("shift", 0, 3), ("lo", 0), ("inverse", 1, 2),
            ("lo", 1), ("shift", 1, 2), ("mix", 3), ("stats", 1, 3), ("moments", 1, 3), ("lo", 2), ("inverse", 1, 3),
            ("shift", 1, 3), ("choose", 0), ("lo", 3), ("secondary", 0), ("choose", 1), ("secondary", 1)]
        DVE_LAST = [(step, 2, b) for b in (0, 1) for step in ("stats", "moments")] + [
            ("inverse", 2, 0), ("inverse", 2, 1), ("shift", 2, 0), ("last", 1), ("stats", 2, 2), ("moments", 2, 2), ("stats", 2, 3),
            ("moments", 2, 3), ("inverse", 2, 2), ("shift", 2, 2), ("inverse", 2, 3), ("last", 3)]
        ACT_DRAIN = {
            LAST: [("root", 0, 0)],
            LAST + 1: [("norm", 0, 0), ("root", 0, 1)],
            LAST + 2: [("norm", 0, 1), ("root", 0, 2)]}
        ACT_MID = [
            ("root", 1, 0), ("root", 1, 1), ("norm", 1, 0), ("norm", 0, 2), ("norm", 1, 1), ("root", 0, 3), ("hi", 0),
            ("root", 1, 2), ("hi", 1), ("norm", 0, 3), ("norm", 1, 2), ("root", 1, 3), ("logits", 0), ("hi", 2), ("norm", 1, 3),
            ("hi", 3), ("onehot", 0), ("early", 0), ("logits", 1), ("early", 1), ("cand", 0), ("exp",), ("early", 2),
            ("onehot", 1), ("early", 3), ("cand", 1)] + [
            ("early", n) for n in range(4, 8)] + [("combine",)] + [("early", n) for n in range(8, EB)]
        ACT_LAST = [("root", 2, 0), ("root", 2, 1), ("norm", 2, 0), ("root", 2, 2), ("root", 2, 3), ("norm", 2, 2)]
        PE_MID = [
            ("turn", 0), ("turn", 1), ("route", 0), ("turn", 2), ("logits", 0), ("early", 0), ("turn", 3), ("onehot", 0),
            ("route", 1), ("early", 1), ("logits", 1), ("similar", 0), ("early", 2), ("onehot", 1), ("early", 3),
            ("similar", 1)] + [
            ("early", n) for n in range(4, 8)] + [("combine", 0), ("combine", 1)] + [
            ("early", n) for n in range(8, EB)] + [("start",)]
        POOL_MID = [("early", 0), ("early", 1), ("mask",), ("exp",), ("early", 2), ("early", 3), ("kept",)] + [
            ("early", n) for n in range(4, EB)]

        block = ctx.enter_context(nc.Block())

        @block.sync
        def _(sp):
            def load_piece(k, q):
                wait(sp, w_lo_done[k], q)
                sp.dma_start(raw_of[k], piece_dram(k, q)).then_inc(w_in[k], 16)

            sp.dma_start(ctx_sb[:], ctx_t).then_inc(in_ctx, 16)
            sp.dma_start(wctx_sb[:], w_ctx).then_inc(in_wctx, 16)
            sp.dma_start(gam[:, 0:1], gamma_raw.to_broadcast([P, 1])).then_inc(in_gam, 16)
            sp.dma_start(xt_raw[:], x_t).then_inc(in_xt, 16)
            load_piece("a", 0)
            load_piece("v", 0)
            sp.dma_start(xs[:], x_tok.rearrange("(t p) d -> p t d", p=P)).then_inc(in_x, 16)
            for k in "bop":
                load_piece(k, 0)
            sp.dma_start(gate_raw[:], gate_t).then_inc(in_gate, 16)
            sp.wait_ge(const_zero, 2)
            for i in range(PRIM):
                sp.dma_start(blockdiag[i * E:(i + 1) * E, i * E:(i + 1) * E], sim_t).then_inc(in_sim, 16)
            for i in range(EARLY):
                sp.dma_start(wf_raw[i][:], w_ffn[i]).then_inc(wf_in[i], 16)
            with sp.Fori(1, PAIRS) as q:
                for k in "avbop":
                    load_piece(k, q)
            for i in range(FG):
                sp.wait_ge(wf_lo_done[i], 1)
                sp.dma_start(wf_raw[i][:], w_ffn[EARLY + i]).then_inc(wf_in[i], 16)

            sp.wait_ge(combine_sb, NBLK)
            sp.dma_start(combine_dram, combine_t[:]).then_inc(combine_out, 16)
            sp.wait_ge(combine_out, 16)

            def load_cw(buf, i, row_of):
                at = 0
                while at < P:
                    expert, inside = divmod(i * P + at, FF)
                    n = min(FF - inside, P - at)
                    src = combine_dram[bass.ds(row_of(expert), 1), :].to_broadcast([n, TOK])
                    sp.dma_start(cw[buf][at:at + n, :], src).then_inc(cw_in[buf], 16)
                    at += n

            for i in range(EARLY):
                load_cw(i, i, lambda expert: expert)
            per_step = FG * P // FF
            for i in range(FG):
                for c in range(NBLK):
                    n = EARLY_BLOCKS.index((i, c))
                    sp.wait_ge(early_weighed[n % 2], n // 2 + 1)
                load_cw(i, i, lambda expert: 2 * per_step + expert)
            with sp.Fori(1, FSTEPS) as s:
                for i in range(FG):
                    sp.wait_ge(wf_lo_done[i], s + 1)
                    sp.dma_start(wf_raw[i][:], w_ffn[bass.ds(s * FG + EARLY + i, 1)].rearrange("o p n -> p (o n)"))\
                        .then_inc(wf_in[i], 16)
                    sp.wait_ge(silu_c_done, s * 2 * FG - 2 * FG + 2 * i + 2)
                    load_cw(i, i, lambda expert: s * per_step + 2 * per_step + expert)
            for b in range(BATCH):
                sp.wait_ge(y_done[b], 1)
                sp.dma_start(out[b * SEQ:(b + 1) * SEQ].rearrange("(t p) d -> p t d", p=P),
                             y_sb[:, 2 * b:2 * b + 2, :]).then_inc(y_out[b], 16)
            for b in range(BATCH):
                sp.wait_ge(y_out[b], 16)

        @block.gpsimd
        def _(pool):
            pool.memset(ident[:], 0.0).then_inc(const_zero, 1)
            pool.memset(blockdiag[:], 0.0).then_inc(const_zero, 1)
            pool.memset(mask[:], 0.0).then_inc(const_zero, 1)
            pool.memset(one[:], 1.0).then_inc(const_zero, 1)
            pool.memset(zero[:], 0.0).then_inc(const_zero, 1)
            pool.memset(eps_col[:], EPS).then_inc(const_zero, 1)
            pool.wait_ge(const_zero, 6)
            pool.affine_select(out=ident[:], in_=ident[:], compare_op=ALU.not_equal, fill=1.0, base=0,
                               pattern=[[-1, P]], channel_multiplier=1).then_inc(const_made, 1)
            pool.affine_select(out=mask[:, P:], in_=mask[:, P:], compare_op=ALU.is_ge, fill=NEG, base=0,
                               pattern=[[-1, P]], channel_multiplier=1).then_inc(const_made, 1)
            pool.iota(iota_e[:], pattern=[[1, E]], base=0, channel_multiplier=0,
                      allow_small_or_imprecise_dtypes=True).then_inc(const_made, 1)

            def round_to_hi(dst, src):
                return pool.tensor_scalar(dst, src, one[0:src.shape[0], 0:1], zero[0:src.shape[0], 0:1], ALU.mult, ALU.add)

            def split_hi(k, q, free=None):
                pool.wait_ge(w_in[k], (q + 1) * 16)
                if free is not None:
                    pool.wait_ge(*free)
                settle(pool)
                round_to_hi(hi_of[k], raw_of[k]).then_inc(w_hi_done[k], 1)

            for k in "avbo":
                split_hi(k, 0)
            for b in range(BATCH):
                pool.wait_ge(sig_done, b + 1)
                pool.wait_ge(gam_done, 1)
                part = slice(2 * b * SEQ, 2 * (b + 1) * SEQ)
                pool.tensor_scalar(adj[:, part], adj[:, part],
                                   gam[:, 2:3], zero[:, 0:1], ALU.mult, ALU.add).then_inc(adj_scaled, 1)
            pool.wait_ge(in_sim, 16 * PRIM)
            pool.affine_select(out=blockdiag[:], in_=blockdiag[:], compare_op=ALU.not_equal, fill=1.0, base=0,
                               pattern=[[-1, P]], channel_multiplier=1).then_inc(bd_made, 1)
            pool.wait_ge(in_gate, 16)
            round_to_hi(gate_hi[:].rearrange("p c e -> p (c e)"), gate_raw[:].rearrange("p c e -> p (c e)")).then_inc(gate_hi_done, 1)

            def slot(N, n, q, live, more):
                if live(0):
                    dst = probs_n[n % 2]
                    pool.wait_ge(inv_done, N + 1)
                    wait(pool, turned, N - 1)
                    settle(pool)
                    pool.tensor_scalar(dst[:, 0:P], probs[:, 0:P], inv_sum[:, 0:1], zero[:, 0:1],
                                       ALU.mult, ALU.add).then_inc(norm_done, 1)
                    pool.tensor_scalar(dst[:, P:], probs[:, P:], inv_sum[:, 1:2], zero[:, 0:1],
                                       ALU.mult, ALU.add).then_inc(norm_done, 1)
                k, ahead = SPLIT_SLOT.get(n, (None, 0))
                if k and live(0) and (more or not ahead) and not (isinstance(N, int) and N == 0):
                    free = {"a": (filled, PER_PAIR * q + ORDER["k", 1] + 1),
                            "v": (filled, PER_PAIR * q + ORDER["v", 3] + 1),
                            "b": (filled, PER_PAIR * q + ORDER["k", 3] + 1),
                            "o": (projected, q * 8 - 4), "p": (projected, q * 8 + 1)}[k]
                    split_hi(k, q + ahead, free)
                    pool.wait_ge(w_hi_done[k], q + ahead + 1)
                    pool.tensor_tensor(lo_of[k], raw_of[k], hi_of[k].bitcast(F32), ALU.subtract).then_inc(w_lo_done[k], 1)
                if not more and n in EARLY_SPLIT and live(LAG_OUT):
                    i = EARLY_SPLIT[n]
                    pool.wait_ge(wf_in[i], 16)
                    round_to_hi(wf[i][0][:], wf_raw[i][:]).then_inc(wf_hi_done[i], 1)
                    pool.wait_ge(wf_hi_done[i], 1)
                    pool.tensor_tensor(wf[i][1][:], wf_raw[i][:], wf[i][0][:].bitcast(F32), ALU.subtract).then_inc(wf_lo_done[i], 1)

            item_loop(pool, slot)

            def secondary_mask():
                pool.wait_ge(secondary_done, 2)
                pool.tensor_tensor(sec_part[0][:], onehot_s[:, :, 0, :], onehot_s[:, :, 1, :], ALU.add)
                pool.tensor_tensor(sec_part[1][:], onehot_s[:, :, 2, :], onehot_s[:, :, 3, :], ALU.add).then_inc(sec_step, 1)
                pool.wait_ge(sec_step, 1)
                pool.tensor_tensor(sec_mask[:], sec_part[0][:], sec_part[1][:], ALU.add).then_inc(sec_step, 1)

            def secondary_exp():
                pool.wait_ge(sec_step, 2)
                pool.wait_ge(exps_done, 1)
                pool.tensor_tensor(sec_exp[:], sec_mask[:], exp_all[:], ALU.mult).then_inc(sec_exp_done, 1)

            def early_multiply(n):
                pool.wait_ge(early_u_done, n + 1)
                pool.tensor_tensor(early_h[n][:], early_h[n][:], early_u[n % 2][:], ALU.mult).then_inc(early_product, 1)

            def kept_weights():
                pool.wait_ge(moved_done, 1)
                pool.tensor_tensor(kept[:], sec_w[:], moved[0][:], ALU.subtract).then_inc(kept_done, 1)

            pool_steps = {"early": early_multiply, "mask": secondary_mask, "exp": secondary_exp, "kept": kept_weights}
            for name, *args in POOL_MID:
                pool_steps[name](*args)

            def split_ffn(i, s):
                pool.wait_ge(wf_in[i], (s + 2) * 16)
                settle(pool)
                round_to_hi(wf[i][0][:], wf_raw[i][:]).then_inc(wf_hi_done[i], 1)

            for n in range(1, EB, 2):
                i, c = EARLY_BLOCKS[n]
                pool.wait_ge(cw_in[i], 32)
                pool.wait_ge(early_product, n + 1)
                pool.tensor_tensor(early_h[n][:], early_h[n][:], cw[i][:, c * BLK:(c + 1) * BLK], ALU.mult)\
                    .then_inc(early_weighed[1], 1)
            for i in range(FG - 1):
                pool.wait_ge(down_done, EARLY_BLOCKS.index((i, NBLK - 1)) + 1)
                split_ffn(i, 0)

            def ffn_slot(K, k, s, last):
                if last and k < 2:
                    return
                i, c = k // 2, k % 2
                pool.wait_ge(cw_in[i], s * 32 + 64)
                pool.wait_ge(silu_done, K + EB + 1)
                wait(pool, h_done, K - 1)
                pool.tensor_tensor(silu_c[k % 2][:], silu_g[k % 2][:], cw[i][:, c * BLK:(c + 1) * BLK],
                                   ALU.mult).then_inc(silu_c_done, 1)
                split_at_slot(k, s, K, last, split_ffn)

            ffn_loop(pool, ffn_slot)

        @block.scalar
        def _(act):
            for n, dst in enumerate((cq, cq, ck, ck)):
                if n % 2 == 0:
                    act.wait_ge(ctx_proj, n + 1)
                    act.activation(dst[:, 0:BLK], acc[n][0:CTX].rearrange("p a b -> p (a b)"), ACT.Copy).then_inc(ctx_proj_sb, 1)
            act.wait_ge(in_gam, 16)
            act.activation(gam[:, 1:2], gam[:, 0:1], ACT.Sigmoid).then_inc(gam_sig, 1)
            for b in range(BATCH):
                act.wait_ge(sims_copied, b + 1)
                part = slice(2 * b * SEQ, 2 * (b + 1) * SEQ)
                act.activation(adj[:, part], sims[:, part], ACT.Sigmoid, scale=1.0 / 16).then_inc(sig_done, 1)
            for c in range(NBLK):
                act.wait_ge(in_xt, 16)
                act.activation(xt_hi[:, :, c * BLK:(c + 1) * BLK], xt_raw[:, :, c * BLK:(c + 1) * BLK], ACT.Copy).then_inc(xt_hi_done, 1)

            def fill_copy(what, f, index):
                act.wait_ge(filled, index + 1)
                act.activation(fill_views(what, f)[0], fill_src(what), ACT.Copy).then_inc(fill_hi, 1)

            for index, (what, f) in enumerate(FIRST):
                fill_copy(what, f, index)

            def slot(N, n, q, live, more):
                fills, base = fills_in(n, q, live, more)
                if live(LAG_OUT):
                    act.wait_ge(pv_done, N - LAG_OUT + 1)
                    act.activation(z_hi[:], bank_z[:, 0:2 * P], ACT.Copy).then_inc(z_hi_done, 1)
                if live(LAG_PV):
                    act.wait_ge(turned, N - LAG_PV + 1)
                    act.activation(pt_hi[:], bank_t[:, 0:3 * P], ACT.Copy).then_inc(pt_hi_done, 1)
                if fills:
                    fill_copy(*fills[0], base)
                if live(0):
                    act.wait_ge(neg_done, N + 1)
                    wait(act, norm_done, N * 2)
                    for j, (lo, hi) in enumerate(((0, P), (P, 3 * P))):
                        act.activation(probs[:, lo:hi], s_masked_sb[:, lo:hi], ACT.Exp, bias=neg_max[:, j:j + 1],
                                       scale=SCALE, accum_out=row_sum[:, j:j + 1]).then_inc(exp_done, 1)
                if len(fills) > 1:
                    fill_copy(*fills[1], base + 1)
                run_steps(ACT_DRAIN, N)

            def root(n, b):
                act.wait_ge(mv_done[n], b + 1)
                part = slice(2 * b, 2 * b + 2)
                act.activation(std[:, part], mv[:, part, 1], ACT.Sqrt, bias=eps_col[:, 0:1]).then_inc(std_done[n], 1)

            def norm(n, b):
                act.wait_ge(shift_done[n], b + 1 if n < 2 else b // 2 + 1)
                for t in (2 * b, 2 * b + 1):
                    src = (acc[b][:, t % 2, :], xs[:, t, :], acc[b][:, t % 2, :])[n]
                    dst = (xs, xs, y_sb)[n][:, t, :]
                    ins = act.activation(dst, src, ACT.Identity, bias=shift[:, t:t + 1], scale=rstd[:, t:t + 1])
                ins.then_inc(normed[n] if n < 2 else y_done[b], 1)

            def turned_hi(b):
                act.wait_ge(x2_turned, b + 1)
                act.activation(of_batch(xt_hi, b), turned_batch(b), ACT.Copy).then_inc(x2t_hi_done, 1)

            def early_parts(n):
                act.wait_ge(gu_done, n + 1)
                act.activation(early_h[n][:], G[n % 2][:], ACT.Silu).then_inc(silu_done, 1)
                wait(act, early_product, n - 1)
                act.activation(early_u[n % 2][:], U[n % 2][:], ACT.Copy).then_inc(early_u_done, 1)

            def logits_out(half):
                act.wait_ge(logits_t_done, half + 1)
                act.activation(logits_t[:, half * BLK:(half + 1) * BLK], whole(logits_t_bank[half], E), ACT.Copy).then_inc(logits_t_out, 1)

            def exponentials():
                act.wait_ge(shifts_done, 2)
                act.activation(exp_all[:], shifted[:], ACT.Exp).then_inc(exps_done, 1)
                act.activation(exp_top[:], top_s[:], ACT.Exp).then_inc(exps_done, 1)

            def onehot_out(half):
                act.wait_ge(onehot_turned, half + 1)
                act.activation(onehot_t[:, half * HALF:(half + 1) * HALF].rearrange("p t n -> p (t n)"), whole(onehot_bank[half]),
                               ACT.Copy).then_inc(onehot_sb, 1)

            def cand_out(half):
                act.wait_ge(cand_done, half + 1)
                act.activation(cand[:, half * HALF:(half + 1) * HALF].rearrange("p t k e -> p (t k e)"), whole(cand_bank[half]),
                               ACT.Copy).then_inc(cand_sb, 1)

            def combine_out_0():
                act.wait_ge(combine_turned, 1)
                act.activation(combine_t[:, 0:BLK], whole(combine_bank[0], E), ACT.Copy).then_inc(combine_sb, 1)

            act_steps = {"root": root, "norm": norm, "hi": turned_hi, "early": early_parts, "logits": logits_out, "exp": exponentials,
                         "onehot": onehot_out, "cand": cand_out, "combine": combine_out_0}

            def run_steps(steps, N=None):
                for name, *args in (steps.get(N, ()) if isinstance(N, int) else steps if N is None else ()):
                    act_steps[name](*args)

            item_loop(act, slot)
            run_steps(ACT_MID)

            for n in range(EB):
                act.wait_ge(early_weighed[n % 2], n // 2 + 1)
                wait(act, down_done, n - 2)
                act.activation(h[n % 3][0][:], early_h[n][:], ACT.Copy).then_inc(h_hi_done, 1)

            def ffn_slot(K, k, s, last):
                if not (last and k < 2):
                    act.wait_ge(gu_done, K + EB + 1)
                    wait(act, silu_c_done, K - 1)
                    act.activation(silu_g[k % 2][:], G[k % 2][:], ACT.Silu).then_inc(silu_done, 1)
                if not isinstance(K, int) or K >= 1:
                    if last and k == 1:
                        return
                    act.wait_ge(h_done, K)
                    act.activation(h[(k - 1) % 3][0][:], h_sb[(k - 1) % 2][:], ACT.Copy).then_inc(h_hi_done, 1)

            ffn_loop(act, ffn_slot)
            for name, *args in ACT_LAST:
                act_steps[name](*args)

        @block.vector
        def _(dve):
            for n, dst in enumerate((cq, cq, ck, ck)):
                if n % 2 == 1:
                    dve.wait_ge(ctx_proj, n + 1)
                    dve.tensor_copy(dst[:, BLK:], acc[n][0:CTX].rearrange("p a b -> p (a b)")).then_inc(ctx_proj_sb, 1)
            dve.wait_ge(gam_sig, 1)
            dve.tensor_scalar(gam[:, 2:3], gam[:, 1:2], 0.5, None, ALU.mult).then_inc(gam_done, 1)
            dve.tensor_scalar(gam[:, 3:4], gam[:, 1:2], -1.0, 2.0, ALU.mult, ALU.add).then_inc(gam_done, 1)
            for b in range(BATCH):
                dve.wait_ge(sims_ready, 2 * b + 2)
                dve.tensor_copy(sims[:, 2 * b * SEQ:2 * (b + 1) * SEQ], sim_banks[b][:]).then_inc(sims_copied, 1)

            def minus_hi(dst, src, hi):
                return dve.tensor_tensor(dst, src, hi.bitcast(F32), ALU.subtract)

            def split_lo(k, q):
                dve.wait_ge(w_hi_done[k], q + 1)
                minus_hi(lo_of[k], raw_of[k], hi_of[k]).then_inc(w_lo_done[k], 1)

            for c in range(NBLK):
                dve.wait_ge(xt_hi_done, c + 1)
                part = slice(c * BLK, (c + 1) * BLK)
                minus_hi(xt_lo[:, :, part], xt_raw[:, :, part], xt_hi[:, :, part]).then_inc(xt_lo_done, 1)
                split_lo("av"[c], 0)

            def fill_rest(what, f, index):
                dve.wait_ge(fill_hi, index + 1)
                hi, lo = fill_views(what, f)
                minus_hi(lo, fill_src(what), hi).then_inc(fill_lo, 1)

            for index, (what, f) in enumerate(FIRST):
                fill_rest(what, f, index)
            split_lo("b", 0)
            split_lo("o", 0)
            dve.wait_ge(gate_hi_done, 1)
            minus_hi(gate_lo[:], gate_raw[:], gate_hi[:]).then_inc(gate_lo_done, 1)

            dve.wait_ge(adj_scaled, BATCH)
            STEPS = 2 * ROUNDS + 1

            def topk(t, j):
                base = t * STEPS if not isinstance(t, int) else t * STEPS
                if j:
                    dve.wait_ge(topk_step, base + j)
                    settle(dve)
                tile = sims[:, bass.ds(t * SEQ, SEQ)]
                if j == 0:
                    ins = dve.tensor_copy(topk_work[0][:], tile)
                elif j == STEPS - 1:
                    last = (TOPK_ADJ - 1) % 8
                    view = adj[:, bass.ds(t * SEQ, SEQ)]
                    ins = dve.scalar_tensor_tensor(out=view, in0=tile, scalar=topk_8[:, last:last + 1], in1=view,
                                                   op0=ALU.is_ge, op1=ALU.mult)
                elif j % 2:
                    ins = dve.max(topk_8[:], topk_work[(j // 2) % 2][:])
                else:
                    ins = dve.match_replace(out=topk_work[(j // 2) % 2][:], in_to_replace=topk_8[:],
                                            in_values=topk_work[(j // 2 + 1) % 2][:], imm_value=-3.0e38)
                ins.then_inc(topk_step, 1)

            TOPK_OF = {3: (0, 3), 4: (3, 6), 5: (6, 9), 6: (9, 12), 7: (12, 15), 0: (15, 18), 1: (18, STEPS), 2: (0, 0)}

            def slot(N, n, q, live, more):
                fills, base = fills_in(n, q, live, more)
                first, end = TOPK_OF[n]
                steps = [(q if n >= LAG_OUT or not more else q - 1, j) for j in range(first, end)] if live(LAG_OUT) else []

                def one_step():
                    if steps:
                        topk(*steps.pop(0))

                if live(LAG_OUT):
                    dve.wait_ge(z_hi_done, N - LAG_OUT + 1)
                    minus_hi(z_lo[:], bank_z[:, 0:2 * P], z_hi[:]).then_inc(z_lo_done, 1)
                one_step()
                if live(LAG_PV):
                    dve.wait_ge(pt_hi_done, N - LAG_PV + 1)
                    minus_hi(pt_lo[:], bank_t[:, 0:3 * P], pt_hi[:]).then_inc(pt_lo_done, 1)
                one_step()
                if len(fills) > 1:
                    fill_rest(*fills[0], base)
                if live(0):
                    dve.wait_ge(scored, N + 1)
                    wait(dve, exp_done, N * 2)
                    settle(dve)
                    dve.tensor_tensor_reduce(out=s_masked_sb[:, 0:P], in0=bank_s[:, 0:P], in1=mask[:, P:], scale=1.0,
                                             scalar=-3.0e38, op0=ALU.add, op1=ALU.max, accum_out=row_max[:, 0:1]).then_inc(masked, 1)
                    dve.tensor_tensor_reduce(out=s_masked_sb[:, P:], in0=bank_s[:, P:3 * P], in1=mask[:], scale=1.0,
                                             scalar=-3.0e38, op0=ALU.add, op1=ALU.max, accum_out=row_max[:, 1:2]).then_inc(masked, 1)
                    dve.wait_ge(masked, N * 2 + 2)
                    dve.tensor_scalar(neg_max[:], row_max[:], -SCALE, None, ALU.mult).then_inc(neg_done, 1)
                one_step()
                if fills:
                    fill_rest(*fills[-1], base + len(fills) - 1)
                if live(0):
                    dve.wait_ge(exp_done, N * 2 + 2)
                    wait(dve, norm_done, N * 2)
                    dve.reciprocal(inv_sum[:], row_sum[:]).then_inc(inv_done, 1)
                while steps:
                    one_step()
                if isinstance(N, int):
                    run_steps(DVE_DRAIN.get(N, ()))

            def stats_of(n, b):
                if n == 0:
                    dve.wait_ge(projected, BATCH * (HEADS - 1) + b + 1)
                elif n == 1:
                    dve.wait_ge(mixed_done, b + 1)
                else:
                    dve.wait_ge(down_done, FT * NBLK - (b < 2))
                for t in (2 * b, 2 * b + 1):
                    ins = dve.bn_stats(stats[:, t, :], xs[:, t, :] if n == 1 else acc[b][:, t % 2, :])
                ins.then_inc(stats_done[n], 1)

            def moments_of(n, b):
                dve.wait_ge(stats_done[n], b + 1)
                for t in (2 * b, 2 * b + 1):
                    ins = dve.bn_aggr(mv[:, t, :], stats[:, t, :])
                ins.then_inc(mv_done[n], 1)

            def inverse_of(n, b):
                dve.wait_ge(std_done[n], b + 1)
                dve.reciprocal(rstd[:, 2 * b:2 * b + 2], std[:, 2 * b:2 * b + 2]).then_inc(rstd_done[n], 1)

            def shift_of(n, b):
                dve.wait_ge(rstd_done[n], b + 1)
                part = slice(2 * b, 2 * b + 2)
                dve.scalar_tensor_tensor(out=shift[:, part], in0=mv[:, part, 0], scalar=-1.0, in1=rstd[:, part],
                                         op0=ALU.mult, op1=ALU.mult).then_inc(shift_done[n], 1)

            def mix(b):
                dve.wait_ge(normed[0], b + 1)
                dve.wait_ge(adj_sum, b + 1)
                for t in (2 * b, 2 * b + 1):
                    ins = dve.scalar_tensor_tensor(out=xs[:, t, :], in0=xs[:, t, :], scalar=gam[:, 3:4],
                                                   in1=sim_banks[b][:, (t % 2) * SEQ:(t % 2 + 1) * SEQ], op0=ALU.mult, op1=ALU.add)
                ins.then_inc(mixed_done, 1)

            def turned_lo(b):
                dve.wait_ge(x2t_hi_done, b + 1)
                minus_hi(of_batch(xt_lo, b), turned_batch(b), of_batch(xt_hi, b)).then_inc(x2t_lo_done, 1)

            count = [0]

            def link(ins):
                count[0] += 1
                ins.then_inc(link_step, 1)
                dve.wait_ge(link_step, count[0])

            def choose(half):
                if half == 0:
                    dve.wait_ge(projected, BATCH * HEADS)
                dve.wait_ge(logits_done, half + 1)
                logits = whole(logits_bank[half])[:, 0:HALF * E].rearrange("p (t e) -> p t e", e=E)
                tiles = slice(half * HALF, (half + 1) * HALF)
                for t in range(HALF):
                    ins = dve.max(top_v[:, half * HALF + t, :], logits[:, t, :])
                link(ins)
                for t in range(HALF):
                    ins = dve.max_index(top_i[:, half * HALF + t, :], top_v[:, half * HALF + t, :], logits[:, t, :])
                link(ins)
                dve.tensor_copy(top_if[:, tiles], top_i[:, tiles]).then_inc(index_done, 1)
                first = top_v[:, tiles, 0:1]
                dve.tensor_tensor(top_s[:, tiles], top_v[:, tiles], first.to_broadcast([P, HALF, TOP]), ALU.subtract)
                dve.tensor_tensor(shifted[:, tiles], logits, first.to_broadcast([P, HALF, E]), ALU.subtract).then_inc(shifts_done, 1)
                dve.wait_ge(index_done, half + 1)
                dve.tensor_tensor(onehot[:, tiles], *index_and_number(top_if[:, tiles, 0:PRIM]), ALU.is_equal).then_inc(onehot_done, 1)

            def index_and_number(index):
                return (index.rearrange("p t (k a) -> p t k a", a=1).to_broadcast([P, HALF, PRIM, E]),
                        iota_e[:].rearrange("p (a k e) -> p a k e", a=1, k=1).to_broadcast([P, HALF, PRIM, E]))

            def secondary(half):
                tiles = slice(half * HALF, (half + 1) * HALF)
                dve.tensor_tensor(onehot_s[:, tiles], *index_and_number(top_if[:, tiles, PRIM:]), ALU.is_equal).then_inc(secondary_done, 1)

            dve_steps = {"stats": stats_of, "moments": moments_of, "inverse": inverse_of, "shift": shift_of, "mix": mix,
                         "lo": turned_lo, "choose": choose, "secondary": secondary}

            def run_steps(steps):
                for name, *args in steps:
                    dve_steps[name](*args)

            item_loop(dve, slot)
            run_steps(DVE_MID)

            dve.wait_ge(exps_done, 2)

            def col(a, n):
                return a[:].rearrange("p (t o) -> p t o", o=1).to_broadcast([P, TILES, n])

            link(dve.tensor_reduce(sum_all[:], exp_all[:], AX.X, ALU.add))
            link(dve.reciprocal(inv_all[:], sum_all[:]))
            link(dve.tensor_tensor(prob_top[:], exp_top[:], col(inv_all, TOP), ALU.mult))
            link(dve.tensor_reduce(sum_top[:], prob_top[:], AX.X, ALU.add))
            link(dve.tensor_scalar(sum_top_c[:], sum_top[:], 1.0e-12, None, ALU.max))
            link(dve.reciprocal(inv_top[:], sum_top_c[:]))
            dve.tensor_tensor(route_w[:], prob_top[:], col(inv_top, TOP), ALU.mult)
            link(dve.tensor_tensor(inv_both[:], inv_all[:], inv_top[:], ALU.mult))
            dve.wait_ge(sec_exp_done, 1)
            dve.tensor_tensor(sec_w[:], sec_exp[:], col(inv_both, E), ALU.mult)
            dve.wait_ge(cand_sb, 2)
            link(dve.tensor_reduce(best[:], cand[:].rearrange("p t k e -> p t e k"), AX.X, ALU.max))
            dve.scalar_tensor_tensor(out=moved[0][:], in0=best[:], scalar=0.5, in1=sec_w[:], op0=ALU.is_ge, op1=ALU.mult)\
                .then_inc(moved_done, 1)
            best_b = best[:].rearrange("p t (k e) -> p t k e", k=1).to_broadcast([P, TILES, PRIM, E])
            link(dve.tensor_tensor(is_best[:], cand[:], best_b, ALU.is_equal))
            for i in range(PRIM):
                link(dve.tensor_tensor(take[:, :, i, :], is_best[:, :, i, :], moved[i][:], ALU.mult))
                if i < PRIM - 1:
                    link(dve.tensor_tensor(moved[i + 1][:], moved[i][:], take[:, :, i, :], ALU.subtract))
            link(dve.tensor_reduce(taken[:], take[:], AX.X, ALU.add))
            link(dve.tensor_tensor(prim_w[:], taken[:], route_w[:, :, 0:PRIM], ALU.add))
            w_b = prim_w[:].rearrange("p t (k a) -> p t k a", a=1).to_broadcast([P, TILES, PRIM, E])
            link(dve.tensor_tensor(prim_each[:], onehot[:], w_b, ALU.mult))
            link(dve.tensor_reduce(prim_all[:], prim_each[:].rearrange("p t k e -> p t e k"), AX.X, ALU.add))
            dve.wait_ge(kept_done, 1)
            dve.tensor_tensor(combine[:], prim_all[:], kept[:], ALU.add).then_inc(combined, 1)
            dve.wait_ge(combine_turned, 2)
            dve.tensor_copy(combine_t[:, BLK:], whole(combine_bank[1], E)).then_inc(combine_sb, 1)

            def weigh(n):
                i, c = EARLY_BLOCKS[n]
                dve.wait_ge(cw_in[i], 32)
                dve.wait_ge(early_product, n + 1)
                dve.tensor_tensor(early_h[n][:], early_h[n][:], cw[i][:, c * BLK:(c + 1) * BLK], ALU.mult)\
                    .then_inc(early_weighed[0], 1)

            def early_lo(n):
                dve.wait_ge(h_hi_done, n + 1)
                minus_hi(h[n % 3][1][:], early_h[n][:], h[n % 3][0][:]).then_inc(h_lo_done, 1)

            weigh(0)
            for n in range(0, EB, 2):
                if n + 2 < EB:
                    weigh(n + 2)
                early_lo(n)
                early_lo(n + 1)

            def split_ffn(i, s):
                dve.wait_ge(wf_hi_done[i], s + 2)
                minus_hi(wf[i][1][:], wf_raw[i][:], wf[i][0][:]).then_inc(wf_lo_done[i], 1)

            for i in range(FG - 1):
                split_ffn(i, 0)

            def ffn_slot(K, k, s, last):
                if not (last and k < 2):
                    dve.wait_ge(silu_c_done, K + 1)
                    dve.wait_ge(h_lo_done, K + EB - 1)
                    dve.tensor_tensor(h_sb[k % 2][:], U[k % 2][:], silu_c[k % 2][:], ALU.mult).then_inc(h_done, 1)
                if (not isinstance(K, int) or K >= 1) and not (last and k == 1):
                    dve.wait_ge(h_hi_done, K + EB)
                    minus_hi(h[(k - 1) % 3][1][:], h_sb[(k - 1) % 2][:], h[(k - 1) % 3][0][:]).then_inc(h_lo_done, 1)
                split_at_slot(k, s, K, last, split_ffn)

            ffn_loop(dve, ffn_slot)

            def last_norm(b):
                dve.wait_ge(rstd_done[2], b + 1)
                for t in (2 * b, 2 * b + 1):
                    ins = dve.tensor_scalar(y_sb[:, t, :], acc[b][:, t % 2, :], mv[:, t, 0:1], rstd[:, t:t + 1],
                                            ALU.subtract, ALU.mult)
                ins.then_inc(y_done[b], 1)

            dve_steps["last"] = last_norm
            run_steps(DVE_LAST)

        @block.tensor
        def _(pe):
            def three(dst, a, b, start, stop, first_of=True):
                (ah, al), (bh, bl) = a, b
                pe.matmul(dst, ah, bh, start=start, stop=False, skip_group_check=True)
                pe.matmul(dst, ah, bl, start=False, stop=False, skip_group_check=True)
                return pe.matmul(dst, al, bh, start=False, stop=stop, skip_group_check=True)

            pe.wait_ge(in_ctx, 16)
            pe.wait_ge(in_wctx, 16)
            for n in range(4):
                pe.matmul(acc[n][0:CTX].rearrange("p a b -> p (a b)"), wctx_sb[:, n // 2, :],
                          ctx_sb[:, (n % 2) * BLK:(n % 2 + 1) * BLK], start=True, stop=True).then_inc(ctx_proj, 1)
            pe.wait_ge(ctx_proj_sb, 4)
            for t in range(TILES):
                b = t // 2
                pe.matmul(sim_banks[t // 2][:, (t % 2) * SEQ:(t % 2 + 1) * SEQ], cq[:, t * P:(t + 1) * P],
                          ck[:, b * SEQ:(b + 1) * SEQ], start=True, stop=True).then_inc(sims_ready, 1)
            pe.wait_ge(in_x, 16)
            pe.wait_ge(const_made, 3)

            def seed(t):
                return pe.matmul(acc[t // 2][:, t % 2, :], ident[:], xs[:, t, :], start=(t % 2 == 0), stop=(t % 2 == 1),
                                 skip_group_check=True)
            for t in range(TILES):
                ins = seed(t)
            ins.then_inc(seeded, 1)

            def fill(what, f, index):
                wait(pe, fill_lo, index)
                g = f // 2
                if what == "v":
                    for j in range(2):
                        t = 2 * f + j
                        for c in range(KC):
                            tok = slice(t * P, (t + 1) * P)
                            ins = three(bank_f[:, j * 2 * P:(j + 1) * 2 * P], (xt_hi[:, c, tok], xt_lo[:, c, tok]),
                                        (wv_hi[:, c, :], wv_lo[:, c, :]), j == 0 and c == 0, j == 1 and c == KC - 1)
                else:
                    hi, lo = (wa_hi, wa_lo) if g == 0 else (wb_hi, wb_lo)
                    s, part = "qk".index(what), slice((f % 2) * BLK, (f % 2 + 1) * BLK)
                    for c in range(KC):
                        ins = three(bank_f[:], (hi[:, s, c, :], lo[:, s, c, :]), (xt_hi[:, c, part], xt_lo[:, c, part]),
                                    c == 0, c == KC - 1)
                ins.then_inc(filled, 1)

            pe.wait_ge(sims_copied, BATCH)
            pe.wait_ge(xt_lo_done, NBLK)
            pe.wait_ge(w_lo_done["a"], 1)
            pe.wait_ge(w_lo_done["v"], 1)
            for index, (what, f) in enumerate(FIRST):
                fill(what, f, index)

            def need_weights(what, f, q):
                if (what, f) == ("q", 0):
                    pe.wait_ge(w_lo_done["a"], q + 2)
                elif (what, f) == ("v", 0):
                    pe.wait_ge(w_lo_done["v"], q + 2)
                elif (what, f) == ("q", 2):
                    pe.wait_ge(w_lo_done["b"], q + 1)

            def slot(N, n, q, live, more):
                fills, base = fills_in(n, q, live, more)
                if live(LAG_PV):
                    pe.wait_ge(norm_done, (N - LAG_PV) * 2 + 2)
                    wait(pe, pt_lo_done, N - LAG_PV)
                    for j in range(3):
                        ins = pe.transpose(bank_t[:, j * P:(j + 1) * P], probs_n[n % 2][:, j * P:(j + 1) * P], ident[:])
                    ins.then_inc(turned, 1)
                if isinstance(N, int):
                    adjacency_at(N, "turned")
                if len(fills) > 1:
                    need_weights(*fills[0], q)
                    fill(*fills[0], base)
                if live(0):
                    g = n // 2
                    pe.wait_ge(fill_lo, PER_PAIR * q + ORDER["k", g] + 1)
                    wait(pe, masked, N * 2)
                    (hi, lo), off = qk[g % 2], (n % 2) * SEQ
                    for j in range(2):
                        tok, keys = slice(off + j * P, off + (j + 1) * P), slice(off, off + (j + 1) * P)
                        ins = three(bank_s[:, (0, P)[j]:(P, 3 * P)[j]], (hi[:, 0, tok], lo[:, 0, tok]),
                                    (hi[:, 1, keys], lo[:, 1, keys]), j == 0, j == 1)
                    ins.then_inc(scored, 1)
                if len(fills) == 1:
                    need_weights(*fills[0], q)
                    fill(*fills[0], base)
                if live(LAG_OUT):
                    m = (n - LAG_OUT) % 8
                    a, b = m // 4, m % 4
                    pe.wait_ge(z_lo_done, N - LAG_OUT + 1)
                    if b == 0:
                        pe.wait_ge(w_lo_done["op"[a]], q + 1)
                    for j in range(2):
                        part = slice(j * P, (j + 1) * P)
                        ins = three(acc[b][:, j, :], (z_hi[:, part], z_lo[:, part]), (wo[a][0][:], wo[a][1][:]), False, False)
                    ins.then_inc(projected, 1)
                if isinstance(N, int):
                    adjacency_at(N, "projected")
                if len(fills) > 1:
                    need_weights(*fills[1], q)
                    fill(*fills[1], base + 1)
                if live(LAG_PV):
                    m = (n - LAG_PV) % 8
                    a, b = m // 4, m % 4
                    pe.wait_ge(pt_lo_done, N - LAG_PV + 1)
                    if a == 0:
                        pe.wait_ge(fill_lo, PER_PAIR * q + ORDER["v", b] + 1)
                    wait(pe, z_lo_done, N - LAG_PV)
                    e = slice(a * DH, (a + 1) * DH)
                    three(bank_z[:, 0:2 * P], (v_hi[:, 2 * b, e], v_lo[:, 2 * b, e]), (pt_hi[:, 0:2 * P], pt_lo[:, 0:2 * P]), True, False)
                    three(bank_z[:, P:2 * P], (v_hi[:, 2 * b + 1, e], v_lo[:, 2 * b + 1, e]),
                          (pt_hi[:, 2 * P:], pt_lo[:, 2 * P:]), False, True).then_inc(pv_done, 1)
                if isinstance(N, int):
                    adjacency_at(N, "end")

            def adjacency(b):
                pe.wait_ge(topk_step, (2 * b + 2) * (2 * ROUNDS + 1))
                pe.wait_ge(*[(fill_lo, PER_PAIR * PAIRS), (masked, 2 * BATCH * HEADS),
                             (pt_lo_done, BATCH * HEADS), (z_lo_done, BATCH * HEADS)][b])
                for r in range(2):
                    t = 2 * b + r
                    for c in range(2):
                        part = sim_banks[b][:, r * SEQ + c * P:r * SEQ + (c + 1) * P]
                        blk = adj[:, (2 * b + c) * SEQ + r * P:(2 * b + c) * SEQ + (r + 1) * P]
                        pe.matmul(part, blk, ident[:], start=(r == 0 and c == 0), stop=False, skip_group_check=True)
                    ins = pe.matmul(sim_banks[b][:, r * SEQ:(r + 1) * SEQ], ident[:], adj[:, t * SEQ:(t + 1) * SEQ], start=False,
                                    stop=(r == 1), skip_group_check=True)
                ins.then_inc(adj_sum, 1)

            def adjacency_at(N, place):
                if (N, place) in ADJ_AT:
                    adjacency(ADJ_AT[N, place])

            def turn(b):
                pe.wait_ge(normed[1], b + 1)
                for t in range(2):
                    for c in range(KC):
                        ins = pe.transpose(turned_batch(b)[:, t, c, :], xs[:, 2 * b + t, c * P:(c + 1) * P], ident[:])
                ins.then_inc(x2_turned, 1)

            def route(half):
                pe.wait_ge(x2t_lo_done, 2 * half + 2)
                pe.wait_ge(gate_lo_done, 1)
                part = slice(half * BLK, (half + 1) * BLK)
                for c in range(KC):
                    ins = three(whole(logits_t_bank[half], E), (gate_hi[:, c, :], gate_lo[:, c, :]), (xt_hi[:, c, part], xt_lo[:, c, part]),
                                c == 0, c == KC - 1)
                ins.then_inc(logits_t_done, 1)

            def turn_logits(half):
                pe.wait_ge(logits_t_out, half + 1)
                for j in range(HALF):
                    ins = pe.transpose(whole(logits_bank[half])[:, j * E:(j + 1) * E],
                                       logits_t[:, (half * HALF + j) * P:(half * HALF + j + 1) * P], ident[0:E, 0:E])
                ins.then_inc(logits_done, 1)

            def turn_onehot(half):
                pe.wait_ge(onehot_done, half + 1)
                for j in range(HALF):
                    ins = pe.transpose(bank_tile(onehot_bank[half], j), onehot[:, half * HALF + j].rearrange("p k e -> p (k e)"), ident[:])
                ins.then_inc(onehot_turned, 1)

            def similar(half):
                pe.wait_ge(bd_made, 1)
                pe.wait_ge(onehot_sb, half + 1)
                pe.wait_ge(shifts_done, half + 1)
                for j in range(HALF):
                    ins = pe.matmul(bank_tile(cand_bank[half], j), onehot_t[:, half * HALF + j, :], blockdiag[:], start=(j == 0),
                                    stop=(j == HALF - 1), skip_group_check=True)
                ins.then_inc(cand_done, 1)

            def turn_combine(half):
                pe.wait_ge(combined, 1)
                for j in range(HALF):
                    ins = pe.transpose(bank_tile(combine_bank[half], j, E), combine[:, half * HALF + j, :], ident[:])
                ins.then_inc(combine_turned, 1)

            def hidden(tile, c, bank):
                hi, lo = wf[tile]
                part = slice(c * BLK, (c + 1) * BLK)
                for g, dst in enumerate((G[bank], U[bank])):
                    for d in range(KC):
                        w = slice((g * KC + d) * P, (g * KC + d + 1) * P)
                        ins = three(dst[:], (hi[:, w], lo[:, w]), (xt_hi[:, d, part], xt_lo[:, d, part]), d == 0, d == KC - 1)
                ins.then_inc(gu_done, 1)

            def down(tile, c, n):
                hi, lo = wf[tile]
                hh, hl = h[n]
                for t in range(HALF):
                    at, tok = HALF * c + t, slice(t * P, (t + 1) * P)
                    ins = three(acc[at // 2][:, at % 2, :], (hh[:, tok], hl[:, tok]), (hi[:, 4 * P:], lo[:, 4 * P:]), False, False)
                ins.then_inc(down_done, 1)

            def early(n):
                i, c = EARLY_BLOCKS[n]
                pe.wait_ge(wf_lo_done[i], 1)
                pe.wait_ge(x2t_lo_done, BATCH if n % 2 else 2 * c + 2)
                wait(pe, early_u_done, n - 1)
                hidden(i, c, n % 2)

            def start_sums():
                pe.wait_ge(combine_sb, NBLK)
                pe.wait_ge(cand_sb, 2)
                for t in range(TILES):
                    seed(t)

            pe_steps = {"turn": turn, "route": route, "logits": turn_logits, "onehot": turn_onehot, "similar": similar,
                        "combine": turn_combine, "early": early, "start": start_sums}
            item_loop(pe, slot)
            for name, *args in PE_MID:
                pe_steps[name](*args)
            for n, (i, c) in enumerate(EARLY_BLOCKS):
                pe.wait_ge(h_lo_done, n + 1)
                down(i, c, n % 3)

            def ffn_slot(K, k, s, last):
                i, c = k // 2, k % 2
                if not (last and k < 2):
                    if c == 0:
                        pe.wait_ge(wf_lo_done[i], s + 2)
                    if isinstance(K, int) and K < 2:
                        pe.wait_ge(early_u_done, EB + K - 1)
                    else:
                        pe.wait_ge(h_done, K - 1)
                    hidden(i, c, k % 2)
                if not isinstance(K, int) or K >= 2:
                    pe.wait_ge(h_lo_done, K + EB - 1)
                    down(((k - 2) % (2 * FG)) // 2, c, (k - 2) % 3)

            ffn_loop(pe, ffn_slot)


_OUT = [((BATCH, SEQ, D), "float32")]


def kernel(x, ctx_512, L0_attn_W_Q, L0_attn_W_K, L0_attn_W_V, L0_attn_W_O, L0_xattn_Wq, L0_xattn_Wk,
           L0_xattn_gamma_raw, L0_ffn_gate_weight, L0_ffn_gate_up_proj, L0_ffn_down_proj, L0_ffn_similarity):
    import numpy as np
    import concourse.bacc as bacc
    from concourse.bass_utils import run_bass_kernel_spmd as run

    def heads_t(w):
        return np.asarray(w).reshape(HEADS, DH, KC, P).transpose(0, 3, 2, 1)

    tokens = np.asarray(x).reshape(TOK, D)
    w_qk = np.stack([heads_t(L0_attn_W_Q), heads_t(L0_attn_W_K)], axis=2).reshape(HEADS, P, -1)
    w_v = heads_t(L0_attn_W_V).reshape(PAIRS, 2, P, KC, DH).transpose(0, 2, 3, 1, 4).reshape(PAIRS, P, -1)
    gate_up = np.asarray(L0_ffn_gate_up_proj).reshape(E, 2, FF, D).transpose(1, 0, 2, 3).reshape(2, FT, P, KC, P)
    w_ffn = np.concatenate([gate_up.transpose(1, 4, 0, 3, 2).reshape(FT, P, -1),
                            np.asarray(L0_ffn_down_proj).transpose(0, 2, 1).reshape(FT, P, D)], axis=2)
    arrays = {
        "x_tok": tokens,
        "x_t": tokens.reshape(TOK, KC, P).transpose(2, 1, 0),
        "w_qk": w_qk,
        "w_v": w_v,
        "w_o": np.asarray(L0_attn_W_O).transpose(0, 2, 1),
        "ctx_t": np.asarray(ctx_512).reshape(TOK, CTX).T,
        "w_ctx": np.stack([np.asarray(L0_xattn_Wq).T, np.asarray(L0_xattn_Wk).T], axis=1),
        "gamma_raw": np.asarray(L0_xattn_gamma_raw).reshape(1, 1),
        "gate_t": np.asarray(L0_ffn_gate_weight).reshape(E, KC, P).transpose(2, 1, 0),
        "w_ffn": w_ffn,
        "sim_t": np.asarray(L0_ffn_similarity).T,
    }
    arrays = {k: np.ascontiguousarray(v) for k, v in arrays.items()}
    nc = bacc.Bacc("TRN2", target_bir_lowering=False, num_devices=1)
    args = {k: nc.dram_tensor(k, v.shape, mybir.dt.from_np(v.dtype), kind="ExternalInput").ap() for k, v in arrays.items()}
    out = nc.dram_tensor("out", [TOK, D], F32, kind="ExternalOutput").ap()
    program(nc, **args, out=out)
    r = run(nc, [arrays], core_ids=[0])
    return r.results[0]["out"].reshape(BATCH, SEQ, D)
```

```python
from contextlib import ExitStack

import concourse.bass as bass
from concourse import mybir

F32 = mybir.dt.float32
F32R = mybir.dt.float32r
U32 = mybir.dt.uint32
ALU = mybir.AluOpType
ACT = mybir.ActivationFunctionType
AX = mybir.AxisListType

P = 128
BATCH, SEQ, D = 4, 256, 256
TOK = BATCH * SEQ
TILES = TOK // P
KC = D // P
HEADS, DH = 16, 128
PAIRS = HEADS // 2
CTX = 64
TOPK_ADJ = int(SEQ * 0.3)
E, FF = 32, 96
TOP, PRIM = 8, 4
FT = E * FF // P
FG = 3
EARLY = 2 * FG
FSTEPS = (FT - EARLY) // FG
BLK = 512
NBLK = TOK // BLK
EARLY_BLOCKS = [(i, c) for c in range(NBLK) for i in range(EARLY)]
EB = len(EARLY_BLOCKS)
HALF = TILES // 2
NEG = -1.0e9
EPS = 1.0e-5
SCALE = float(DH) ** -0.5
ROUNDS = (TOPK_ADJ + 7) // 8


def item(n):
    return n // 2 % 2, n // 4 * 2 + n % 2


def fills_of_slot(n):
    return {0: [("v", 1)], 1: [("k", 1), ("v", 2)], 2: [("q", 2)], 3: [("k", 2), ("v", 3)],
            4: [("q", 3)], 5: [("k", 3), ("q", 0)], 6: [("k", 0)], 7: [("v", 0), ("q", 1)]}[n]


PER_PAIR = sum(len(fills_of_slot(n)) for n in range(8))
FIRST = [("q", 0), ("k", 0), ("v", 0), ("q", 1)]
AT_SLOT = [sum(len(fills_of_slot(m)) for m in range(n)) for n in range(8)]
ORDER = {f: n for n, f in enumerate(FIRST)}
ORDER.update({f: len(FIRST) + AT_SLOT[n] + m
              for n in range(8) for m, f in enumerate(fills_of_slot(n)) if f not in FIRST})


def program(nc, x_tok, x_t, w_qk, w_v, w_o, ctx_t, w_ctx, gamma_raw, gate_t, w_ffn, sim_t, out):
    ctx = ExitStack()
    with ctx:
        def sb(name, shape, dt=F32):
            return ctx.enter_context(nc.sbuf_tensor(name, shape, dt))

        def pair(name, shape):
            return sb(name + "_hi", shape, F32R), sb(name + "_lo", shape, F32R)

        def ps(name, shape):
            return ctx.enter_context(nc.psum_tensor(name, shape, F32))

        def sem(name):
            return ctx.enter_context(nc.semaphore(name))

        ident = sb("ident", [P, P])
        mask = sb("mask", [P, 2 * P])
        iota_e = sb("iota_e", [P, E])
        xs = sb("xs", [P, TILES, D])
        xt_hi, xt_lo = pair("xt", [P, KC, TOK])
        one = sb("one", [P, 1])
        zero = sb("zero", [P, 1])
        adj = sb("adj", [P, TILES * SEQ])
        gam = sb("gam", [P, 4])
        stats = sb("stats", [P, TILES, 6])
        mv = sb("mv", [P, TILES, 2])
        std, rstd, shift = sb("std", [P, TILES]), sb("rstd", [P, TILES]), sb("shift", [P, TILES])
        eps_col = sb("eps_col", [P, 1])
        gate_raw = sb("gate_raw", [P, KC, E])
        gate_hi, gate_lo = pair("gate", [P, KC, E])
        blockdiag = sb("blockdiag", [P, P])
        wf_raw = [sb(f"wf_raw{i}", [P, 6 * P]) for i in range(EARLY)]
        wf = [pair(f"wf{i}", [P, 6 * P]) for i in range(EARLY)]
        att = ExitStack()

        def att_sb(name, shape, dt=F32):
            return att.enter_context(nc.sbuf_tensor(name, shape, dt))

        def att_pair(name, shape):
            return att_sb(name + "_hi", shape, F32R), att_sb(name + "_lo", shape, F32R)

        xt_raw = att_sb("xt_raw", [P, KC, TOK])
        raw_a, raw_b = att_sb("raw_a", [P, 2, KC, P]), att_sb("raw_b", [P, 2, KC, P])
        raw_v = att_sb("raw_v", [P, KC, 2 * P])
        raw_o = [att_sb("raw_o0", [P, D]), att_sb("raw_o1", [P, D])]
        wa_hi, wa_lo = att_pair("wa", [P, 2, KC, P])
        wb_hi, wb_lo = att_pair("wb", [P, 2, KC, P])
        wv_hi, wv_lo = att_pair("wv", [P, KC, 2 * P])
        wo = [att_pair("wo0", [P, D]), att_pair("wo1", [P, D])]
        qk = [att_pair("qk0", [P, 2, BLK]), att_pair("qk1", [P, 2, BLK])]
        fill_sb = [att_sb(f"fill_sb{i}", [P, BLK]) for i in range(2)]
        v_hi, v_lo = att_pair("v", [P, TILES, 2 * DH])
        s_masked_sb = att_sb("s_masked_sb", [P, 3 * P])
        row_max, neg_max = att_sb("row_max", [P, 2]), att_sb("neg_max", [P, 2])
        row_sum, inv_sum = att_sb("row_sum", [P, 2]), att_sb("inv_sum", [P, 2])
        probs, probs_n = att_sb("probs", [P, 3 * P]), [att_sb(f"probs_n{i}", [P, 3 * P]) for i in range(2)]
        pt_hi, pt_lo = att_pair("pt", [P, 3 * P])
        z_hi, z_lo = att_pair("z", [P, 2 * P])
        ctx_raw, ctx_hl = att_sb("ctx_raw", [P, TOK]), att_sb("ctx_hl", [P, TOK], F32R)
        wctx_raw, wctx_hi = att_sb("wctx_raw", [P, 2, P]), att_sb("wctx_hi", [P, 2, P], F32R)
        wctx_lo = att_sb("wctx_lo", [P, 2, P], F32R)
        cq_hi, cq_lo = att_sb("cq_hi", [P, TOK], F32R), att_sb("cq_lo", [CTX, TOK], F32R)
        ck_hl = att_sb("ck_hl", [P, TOK], F32R)
        sims = att_sb("sims", [P, TILES * SEQ])
        topk_work = [att_sb("topk_work0", [P, SEQ]), att_sb("topk_work1", [P, SEQ])]
        topk_8 = att_sb("topk_8", [P, 8])
        att.close()
        logits_t = sb("logits_t", [E, TOK])
        shifted = sb("shifted", [P, TILES, E])
        top_v, top_s = sb("top_v", [P, TILES, TOP]), sb("top_s", [P, TILES, TOP])
        top_i, top_if = sb("top_i", [P, TILES, TOP], U32), sb("top_if", [P, TILES, TOP])
        exp_all, exp_top = sb("exp_all", [P, TILES, E]), sb("exp_top", [P, TILES, TOP])
        sum_all, inv_all = sb("sum_all", [P, TILES]), sb("inv_all", [P, TILES])
        sum_top, inv_top = sb("sum_top", [P, TILES]), sb("inv_top", [P, TILES])
        sum_top_c, inv_both = sb("sum_top_c", [P, TILES]), sb("inv_both", [P, TILES])
        prob_top, route_w = sb("prob_top", [P, TILES, TOP]), sb("route_w", [P, TILES, TOP])
        onehot, onehot_s = sb("onehot", [P, TILES, PRIM, E]), sb("onehot_s", [P, TILES, TOP - PRIM, E])
        onehot_t = sb("onehot_t", [P, TILES, P])
        sec_part = [sb(f"sec_part{i}", [P, TILES, E]) for i in range(2)]
        sec_mask, sec_exp, sec_w = (sb(n, [P, TILES, E]) for n in ("sec_mask", "sec_exp", "sec_w"))
        cand = sb("cand", [P, TILES, PRIM, E])
        best = sb("best", [P, TILES, E])
        moved = [sb(f"moved{i}", [P, TILES, E]) for i in range(PRIM)]
        is_best = sb("is_best", [P, TILES, PRIM, E])
        take = sb("take", [P, TILES, PRIM, E])
        taken, prim_w = sb("taken", [P, TILES, PRIM]), sb("prim_w", [P, TILES, PRIM])
        prim_each = sb("prim_each", [P, TILES, PRIM, E])
        prim_all, kept = sb("prim_all", [P, TILES, E]), sb("kept", [P, TILES, E])
        combine = sb("combine", [P, TILES, E])
        combine_t = sb("combine_t", [E, TOK])
        cw = [sb(f"cw{i}", [P, TOK]) for i in range(EARLY)]
        early_h = [sb(f"early_h{n}", [P, BLK]) for n in range(EB)]
        early_u = [sb(f"early_u{i}", [P, BLK]) for i in range(2)]
        silu_g, silu_c, h_sb = early_h[0:2], early_h[2:4], early_h[4:6]
        h = [pair(f"h{i}", [P, BLK]) for i in range(3)]
        y_sb = xs

        combine_dram = nc.dram_tensor("combine_dram", [E, TOK], F32, kind="Internal").ap()

        acc = [ps(f"acc{b}", [P, 2, D]) for b in range(BATCH)]
        bank_f, bank_s = ps("bank_f", [P, BLK]), ps("bank_s", [P, BLK])
        bank_t, bank_z = ps("bank_t", [P, BLK]), ps("bank_z", [P, BLK])
        sim_banks = [bank_f, bank_s, bank_t, bank_z]

        in_x, in_xt, in_ctx, in_wctx, in_gam = (sem(f"in_{n}") for n in ("x", "xt", "ctx", "wctx", "gam"))
        in_gate, in_sim = sem("in_gate"), sem("in_sim")
        PIECES = "abvop"
        w_in, w_hi_done, w_lo_done = ({k: sem(f"w{k}_{s}") for k in PIECES} for s in ("in", "hi_done", "lo_done"))
        const_made, const_zero = sem("const_made"), sem("const_zero")
        xt_hi_done, xt_lo_done = [sem(f"xt_hi_done{c}") for c in range(NBLK)], sem("xt_lo_done")
        wctx_hi_done, wctx_lo_done, ctx_hi_done, ctx_lo_done = (sem(n) for n in ("wctx_hi_done", "wctx_lo_done", "ctx_hi_done", "ctx_lo_done"))
        ctx_proj, ctx_proj_hi, ctx_proj_lo = sem("ctx_proj"), sem("ctx_proj_hi"), sem("ctx_proj_lo")
        sims_ready, sims_copied, sims_copied_late, sig_done, adj_scaled = (sem(n) for n in ("sims_ready", "sims_copied", "sims_copied_late", "sig_done", "adj_scaled"))
        gam_sig, gam_done = sem("gam_sig"), sem("gam_done")
        passed_pool, passed_dve = sem("passed_pool"), sem("passed_dve")
        filled, fill_out, fill_hi, fill_lo = sem("filled"), sem("fill_out"), sem("fill_hi"), sem("fill_lo")
        scored, masked, neg_done, exp_done = (sem(n) for n in ("scored", "masked", "neg_done", "exp_done"))
        inv_done, norm_done, turned = sem("inv_done"), sem("norm_done"), sem("turned")
        pt_hi_done, pt_lo_done, pv_done = sem("pt_hi_done"), sem("pt_lo_done"), sem("pv_done")
        z_hi_done, z_lo_done, projected = sem("z_hi_done"), sem("z_lo_done"), sem("projected")
        topk_step = sem("topk_step")
        stats_done, mv_done, std_done, rstd_done, shift_done, normed = (
            [sem(f"{n}{i}") for i in range(3)] for n in ("stats_done", "mv_done", "std_done", "rstd_done", "shift_done", "normed"))
        normed_last = sem("normed_last")
        adj_sum, mixed_done = sem("adj_sum"), sem("mixed_done")
        x2_turned, x2t_hi_done, x2t_lo_done = sem("x2_turned"), sem("x2t_hi_done"), sem("x2t_lo_done")
        gate_hi_done, gate_lo_done, logits_done = sem("gate_hi_done"), sem("gate_lo_done"), sem("logits_done")
        logits_t_done, logits_t_out = sem("logits_t_done"), sem("logits_t_out")
        link_step, index_done, shifts_done, exps_done = (sem(n) for n in ("link_step", "index_done", "shifts_done", "exps_done"))
        onehot_done, secondary_done, onehot_turned, onehot_sb, cand_done, cand_sb = (
            sem(n) for n in ("onehot_done", "secondary_done", "onehot_turned", "onehot_sb", "cand_done", "cand_sb"))
        sec_step, sec_exp_done, moved_done, kept_done = (sem(n) for n in ("sec_step", "sec_exp_done", "moved_done", "kept_done"))
        combined, blockdiag_made = sem("combined"), sem("blockdiag_made")
        combine_turned, combine_sb, combine_out = (sem(n) for n in ("combine_turned", "combine_sb", "combine_out"))
        wf_in, wf_hi_done, wf_lo_done, cw_in = ([sem(f"{n}{i}") for i in range(EARLY)] for n in ("wf_in", "wf_hi", "wf_lo", "cw_in"))
        early_u_done, early_product, early_weighed = sem("early_u_done"), sem("early_product"), [sem(f"early_weighed{i}") for i in range(2)]
        gu_done, silu_done, silu_c_done, h_done, h_hi_done, h_lo_done, down_done = (
            sem(n) for n in ("gu_done", "silu_done", "silu_c_done", "h_done", "h_hi_done", "h_lo_done", "down_done"))
        y_done, y_out = [sem(f"y_done{b}") for b in range(BATCH)], [sem(f"y_out{b}") for b in range(BATCH)]

        def wait(eng, semaphore, value):
            if not isinstance(value, int) or value > 0:
                eng.wait_ge(semaphore, value)

        def settle(eng):
            eng.sem_inc(passed_pool if eng is nc.gpsimd else passed_dve, 1)

        raw_of = {"a": raw_a[:].rearrange("p s c e -> p (s c e)"), "b": raw_b[:].rearrange("p s c e -> p (s c e)"),
                  "v": raw_v[:].rearrange("p c e -> p (c e)"), "o": raw_o[0][:], "p": raw_o[1][:]}
        hi_of = {"a": wa_hi[:].rearrange("p s c e -> p (s c e)"), "b": wb_hi[:].rearrange("p s c e -> p (s c e)"),
                 "v": wv_hi[:].rearrange("p c e -> p (c e)"), "o": wo[0][0][:], "p": wo[1][0][:]}
        lo_of = {"a": wa_lo[:].rearrange("p s c e -> p (s c e)"), "b": wb_lo[:].rearrange("p s c e -> p (s c e)"),
                 "v": wv_lo[:].rearrange("p c e -> p (c e)"), "o": wo[0][1][:], "p": wo[1][1][:]}

        def piece_dram(k, q):
            if k == "v":
                return w_v[bass.ds(q, 1)].rearrange("o p n -> p (o n)")
            src, head = (w_qk if k in "ab" else w_o), 2 * q + (k in "bp")
            return src[bass.ds(head, 1)].rearrange("o p n -> p (o n)")

        SPLIT_SLOT = {3: ("a", 1), 2: ("p", 0), 4: ("v", 1), 5: ("b", 1), 0: ("o", 0)}
        LAG_PV, LAG_OUT = 2, 3

        def item_loop(eng, slot):
            for k in range(LAG_OUT):
                slot(k, k, 0, lambda lag, k=k: k >= lag, True)
            with eng.Fori(0, PAIRS - 1) as q:
                for k in range(LAG_OUT, LAG_OUT + 8):
                    slot(q * 8 + k, k % 8, q + k // 8, lambda lag: True, True)
            for k in range(LAG_OUT, LAG_OUT + 8):
                slot(8 * (PAIRS - 1) + k, k % 8, PAIRS - 1, lambda lag, k=k: k - lag < 8, False)

        def fills_in(n, q, live, more):
            found = [None, None]
            fills = fills_of_slot(n)
            for m, fill in enumerate(fills):
                if live(0) and (more or fill not in FIRST):
                    at = AT_SLOT[n] + m
                    found[m + 2 - len(fills)] = (*fill, PER_PAIR * q + len(FIRST) + at, at)
            return found

        def left_fill(n, q, live, more):
            before, of = (n - 1, q) if n else (7, q - 1)
            return fills_in(before, of, lambda lag: live(lag + 1), more)[1]

        def fill_views(what, f):
            if what == "v":
                return v_hi[:, 2 * f:2 * f + 2, :], v_lo[:, 2 * f:2 * f + 2, :]
            hi, lo = qk[f % 2]
            s = "qk".index(what)
            return hi[:, s, :], lo[:, s, :]

        def fill_src(what, place):
            copy = fill_sb[place % 2][:]
            return copy if what != "v" else copy.rearrange("p (t e) -> p t e", t=2)

        def turned_batch(b):
            bank = (bank_f[:], bank_s[:], whole(acc[2]), whole(acc[3]))[b]
            return bank.rearrange("p (t c n) -> p t c n", t=2, c=KC)

        def of_batch(xt, b):
            return xt[:, :, b * SEQ:(b + 1) * SEQ].rearrange("p c (t n) -> p t c n", t=2)

        logits_t_bank, logits_bank = [acc[0], acc[2]], [acc[1], acc[3]]
        onehot_bank, cand_bank, combine_bank = logits_t_bank, logits_bank, logits_t_bank

        def bank_tile(bank, j, rows=P):
            return bank[0:rows].rearrange("p a d -> p (a d)")[:, j * P:(j + 1) * P]

        def whole(bank, rows=P):
            return bank[0:rows].rearrange("p a d -> p (a d)")

        CTX_PROJ = [(0, 0), (1, 0), (0, 1), (1, 1)]

        def proj_hi(n):
            what, c = CTX_PROJ[n]
            return (cq_hi, ck_hl)[what][:, c * BLK:(c + 1) * BLK]

        G, U = [bank_f, bank_t], [bank_s, bank_z]

        def split_at_slot(k, s, K, last, split):
            if k == 4 and not last:
                split(0, s + 1)
            elif k == 0 and not isinstance(K, int):
                split(1, s)
            elif k == 2:
                split(2, s)

        def ffn_loop(eng, slot):
            slot(0, 0, 0, False)
            slot(1, 1, 0, False)
            with eng.Fori(0, FSTEPS - 1) as s:
                for k in range(2, 2 * FG + 2):
                    slot(s * 2 * FG + k, k % (2 * FG), s + k // (2 * FG), False)
            for k in range(2, 2 * FG + 2):
                slot(2 * FG * (FSTEPS - 1) + k, k % (2 * FG), FSTEPS - 1, True)

        LAST = BATCH * HEADS
        WARM = 3
        EARLY_SPLIT = {3: 0, 4: 1, 5: 2, 6: 3, 7: 4, 0: 5}

        block = ctx.enter_context(nc.Block())

        @block.sync
        def _(sp):
            def load_piece(k, q):
                wait(sp, w_lo_done[k], q)
                sp.dma_start(raw_of[k], piece_dram(k, q)).then_inc(w_in[k], 16)

            sp.dma_start(wctx_raw[:], w_ctx).then_inc(in_wctx, 16)
            for half in range(2):
                sp.dma_start(ctx_raw[half * CTX:(half + 1) * CTX], ctx_t).then_inc(in_ctx, 16)
            sp.dma_start(gam[:, 0:1], gamma_raw.to_broadcast([P, 1])).then_inc(in_gam, 16)
            sp.dma_start(xt_raw[:], x_t).then_inc(in_xt, 16)
            load_piece("a", 0)
            load_piece("v", 0)
            sp.dma_start(xs[:], x_tok.rearrange("(t p) d -> p t d", p=P)).then_inc(in_x, 16)
            for k in "bop":
                load_piece(k, 0)
            sp.dma_start(gate_raw[:], gate_t).then_inc(in_gate, 16)
            sp.wait_ge(const_zero, 2)
            for i in range(PRIM):
                sp.dma_start(blockdiag[i * E:(i + 1) * E, i * E:(i + 1) * E], sim_t).then_inc(in_sim, 16)
            for i in range(EARLY):
                sp.dma_start(wf_raw[i][:], w_ffn[i]).then_inc(wf_in[i], 16)
            with sp.Fori(1, PAIRS) as q:
                for k in "avbop":
                    load_piece(k, q)
            for i in range(FG):
                sp.wait_ge(wf_lo_done[i], 1)
                sp.dma_start(wf_raw[i][:], w_ffn[EARLY + i]).then_inc(wf_in[i], 16)

            sp.wait_ge(combine_sb, NBLK)
            sp.dma_start(combine_dram, combine_t[:]).then_inc(combine_out, 16)
            sp.wait_ge(combine_out, 16)

            def load_cw(buf, i, row_of):
                at = 0
                while at < P:
                    expert, inside = divmod(i * P + at, FF)
                    n = min(FF - inside, P - at)
                    src = combine_dram[bass.ds(row_of(expert), 1), :].to_broadcast([n, TOK])
                    sp.dma_start(cw[buf][at:at + n, :], src).then_inc(cw_in[buf], 16)
                    at += n

            for i in range(EARLY):
                load_cw(i, i, lambda expert: expert)
            per_step = FG * P // FF
            for i in range(FG):
                for c in range(NBLK):
                    n = EARLY_BLOCKS.index((i, c))
                    sp.wait_ge(early_weighed[n % 2], n // 2 + 1)
                load_cw(i, i, lambda expert: 2 * per_step + expert)
            with sp.Fori(1, FSTEPS) as s:
                for i in range(FG):
                    sp.wait_ge(wf_lo_done[i], s + 1)
                    sp.dma_start(wf_raw[i][:], w_ffn[bass.ds(s * FG + EARLY + i, 1)].rearrange("o p n -> p (o n)"))\
                        .then_inc(wf_in[i], 16)
                    sp.wait_ge(silu_c_done, s * 2 * FG - 2 * FG + 2 * i + 2)
                    load_cw(i, i, lambda expert: s * per_step + 2 * per_step + expert)
            for b in range(BATCH):
                sp.wait_ge(y_done[b], 1)
                sp.dma_start(out[b * SEQ:(b + 1) * SEQ].rearrange("(t p) d -> p t d", p=P),
                             y_sb[:, 2 * b:2 * b + 2, :]).then_inc(y_out[b], 16)
            for b in range(BATCH):
                sp.wait_ge(y_out[b], 16)

        @block.gpsimd
        def _(pool):
            pool.memset(ident[:], 0.0).then_inc(const_zero, 1)
            pool.memset(blockdiag[:], 0.0).then_inc(const_zero, 1)
            pool.memset(mask[:], 0.0).then_inc(const_zero, 1)
            pool.memset(one[:], 1.0).then_inc(const_zero, 1)
            pool.memset(zero[:], 0.0).then_inc(const_zero, 1)
            pool.memset(eps_col[:], EPS).then_inc(const_zero, 1)
            pool.wait_ge(const_zero, 6)
            pool.affine_select(out=ident[:], in_=ident[:], compare_op=ALU.not_equal, fill=1.0, base=0,
                               pattern=[[-1, P]], channel_multiplier=1).then_inc(const_made, 1)
            pool.affine_select(out=mask[:, P:], in_=mask[:, P:], compare_op=ALU.is_ge, fill=NEG, base=0,
                               pattern=[[-1, P]], channel_multiplier=1).then_inc(const_made, 1)
            pool.iota(iota_e[:], pattern=[[1, E]], base=0, channel_multiplier=0,
                      allow_small_or_imprecise_dtypes=True).then_inc(const_made, 1)

            def round_to_hi(dst, src):
                return pool.tensor_scalar(dst, src, one[0:src.shape[0], 0:1], zero[0:src.shape[0], 0:1], ALU.mult, ALU.add)

            def split_hi(k, q, free=None):
                pool.wait_ge(w_in[k], (q + 1) * 16)
                if free is not None:
                    wait(pool, *free)
                settle(pool)
                round_to_hi(hi_of[k], raw_of[k]).then_inc(w_hi_done[k], 1)

            pool.wait_ge(in_xt, 16)
            for c in range(KC):
                ins = round_to_hi(xt_hi[:, c, 0:BLK], xt_raw[:, c, 0:BLK])
            ins.then_inc(xt_hi_done[0], 1)
            split_hi("a", 0)
            pool.wait_ge(w_hi_done["a"], 1)
            pool.tensor_tensor(lo_of["a"], raw_of["a"], hi_of["a"].bitcast(F32), ALU.subtract).then_inc(w_lo_done["a"], 1)
            for k in "vbo":
                split_hi(k, 0)

            def adjacency_scale(b):
                pool.wait_ge(sig_done, b + 1)
                pool.wait_ge(gam_done, 1)
                part = slice(2 * b * SEQ, 2 * (b + 1) * SEQ)
                pool.tensor_scalar(adj[:, part], adj[:, part],
                                   gam[:, 2:3], zero[:, 0:1], ALU.mult, ALU.add).then_inc(adj_scaled, 1)

            def slot(N, n, q, live, more):
                if live(0):
                    dst = probs_n[n % 2]
                    pool.wait_ge(inv_done, N + 1)
                    wait(pool, turned, N - 1)
                    settle(pool)
                    pool.tensor_scalar(dst[:, 0:P], probs[:, 0:P], inv_sum[:, 0:1], zero[:, 0:1],
                                       ALU.mult, ALU.add).then_inc(norm_done, 1)
                    pool.tensor_scalar(dst[:, P:], probs[:, P:], inv_sum[:, 1:2], zero[:, 0:1],
                                       ALU.mult, ALU.add).then_inc(norm_done, 1)
                if isinstance(N, int) and N in (0, 1):
                    adjacency_scale(2 * N)
                    adjacency_scale(2 * N + 1)
                elif isinstance(N, int) and N == 2:
                    pool.wait_ge(in_sim, 16 * PRIM)
                    pool.affine_select(out=blockdiag[:], in_=blockdiag[:], compare_op=ALU.not_equal, fill=1.0, base=0,
                                       pattern=[[-1, P]], channel_multiplier=1).then_inc(blockdiag_made, 1)
                    pool.wait_ge(in_gate, 16)
                    round_to_hi(gate_hi[:].rearrange("p c e -> p (c e)"), gate_raw[:].rearrange("p c e -> p (c e)")).then_inc(gate_hi_done, 1)
                k, ahead = SPLIT_SLOT.get(n, (None, 0))
                if k and live(0) and (more or not ahead) and not (isinstance(N, int) and N == 0):
                    free = {"a": (filled, PER_PAIR * q + ORDER["k", 2] + 1),
                            "v": (filled, PER_PAIR * q + ORDER["v", 3] + 1),
                            "b": (filled, PER_PAIR * q + ORDER["k", 3] + 1),
                            "o": (projected, q * 8 - 2), "p": (projected, q * 8)}[k]
                    split_hi(k, q + ahead, free)
                    pool.wait_ge(w_hi_done[k], q + ahead + 1)
                    pool.tensor_tensor(lo_of[k], raw_of[k], hi_of[k].bitcast(F32), ALU.subtract).then_inc(w_lo_done[k], 1)
                if not more and n in EARLY_SPLIT and live(LAG_OUT):
                    i = EARLY_SPLIT[n]
                    pool.wait_ge(wf_in[i], 16)
                    round_to_hi(wf[i][0][:], wf_raw[i][:]).then_inc(wf_hi_done[i], 1)
                    pool.wait_ge(wf_hi_done[i], 1)
                    pool.tensor_tensor(wf[i][1][:], wf_raw[i][:], wf[i][0][:].bitcast(F32), ALU.subtract).then_inc(wf_lo_done[i], 1)

            item_loop(pool, slot)

            def secondary_mask():
                pool.wait_ge(secondary_done, 2)
                pool.tensor_tensor(sec_part[0][:], onehot_s[:, :, 0, :], onehot_s[:, :, 1, :], ALU.add)
                pool.tensor_tensor(sec_part[1][:], onehot_s[:, :, 2, :], onehot_s[:, :, 3, :], ALU.add).then_inc(sec_step, 1)
                pool.wait_ge(sec_step, 1)
                pool.tensor_tensor(sec_mask[:], sec_part[0][:], sec_part[1][:], ALU.add).then_inc(sec_step, 1)

            def secondary_exp():
                pool.wait_ge(sec_step, 2)
                pool.wait_ge(exps_done, 1)
                pool.tensor_tensor(sec_exp[:], sec_mask[:], exp_all[:], ALU.mult).then_inc(sec_exp_done, 1)

            def early_multiply(n):
                pool.wait_ge(early_u_done, n + 1)
                pool.tensor_tensor(early_h[n][:], early_h[n][:], early_u[n % 2][:], ALU.mult).then_inc(early_product, 1)

            def kept_weights():
                pool.wait_ge(moved_done, 1)
                pool.tensor_tensor(kept[:], sec_w[:], moved[0][:], ALU.subtract).then_inc(kept_done, 1)

            for n in range(0, 3):
                early_multiply(n)
            secondary_mask()
            secondary_exp()
            early_multiply(3)
            kept_weights()
            for n in range(4, EB):
                early_multiply(n)

            def split_ffn(i, s):
                pool.wait_ge(wf_in[i], (s + 2) * 16)
                settle(pool)
                round_to_hi(wf[i][0][:], wf_raw[i][:]).then_inc(wf_hi_done[i], 1)

            for n in range(1, EB, 2):
                i, c = EARLY_BLOCKS[n]
                pool.wait_ge(cw_in[i], 32)
                pool.wait_ge(early_product, n + 1)
                pool.tensor_tensor(early_h[n][:], early_h[n][:], cw[i][:, c * BLK:(c + 1) * BLK], ALU.mult)\
                    .then_inc(early_weighed[1], 1)
            for i in range(FG - 1):
                pool.wait_ge(down_done, EARLY_BLOCKS.index((i, NBLK - 1)) + 1)
                split_ffn(i, 0)

            def ffn_slot(K, k, s, last):
                if last and k < 2:
                    return
                i, c = k // 2, k % 2
                pool.wait_ge(cw_in[i], s * 32 + 64)
                pool.wait_ge(silu_done, K + EB + 1)
                wait(pool, h_done, K - 1)
                pool.tensor_tensor(silu_c[k % 2][:], silu_g[k % 2][:], cw[i][:, c * BLK:(c + 1) * BLK],
                                   ALU.mult).then_inc(silu_c_done, 1)
                split_at_slot(k, s, K, last, split_ffn)

            ffn_loop(pool, ffn_slot)

        @block.scalar
        def _(act):
            act.wait_ge(in_wctx, 16)
            act.activation(wctx_hi[:], wctx_raw[:], ACT.Copy).then_inc(wctx_hi_done, 1)
            act.wait_ge(in_ctx, 32)
            for c in range(NBLK):
                part = slice(c * BLK, (c + 1) * BLK)
                act.activation(ctx_hl[:, part], ctx_raw[:, part], ACT.Copy).then_inc(ctx_hi_done, 1)
            for n in range(len(CTX_PROJ)):
                act.wait_ge(ctx_proj, n + 1)
                act.activation(proj_hi(n), whole(acc[n]), ACT.Copy).then_inc(ctx_proj_hi, 1)
            for b in range(2):
                act.wait_ge(sims_ready, 2 * b + 2)
                act.activation(sims[:, 2 * b * SEQ:2 * (b + 1) * SEQ], sim_banks[b][:], ACT.Copy).then_inc(sims_copied, 1)
            act.wait_ge(in_gam, 16)
            act.activation(gam[:, 1:2], gam[:, 0:1], ACT.Sigmoid).then_inc(gam_sig, 1)
            act.wait_ge(in_xt, 16)
            act.activation(xt_hi[:, :, BLK:], xt_raw[:, :, BLK:], ACT.Copy).then_inc(xt_hi_done[1], 1)

            def adjacency_sigmoid(b):
                act.wait_ge(*((sims_copied, b + 1) if b < 2 else (sims_copied_late, b - 1)))
                part = slice(2 * b * SEQ, 2 * (b + 1) * SEQ)
                act.activation(adj[:, part], sims[:, part], ACT.Sigmoid, scale=1.0 / 16).then_inc(sig_done, 1)

            def fill_copy(what, f, index, place):
                act.wait_ge(filled, index + 1)
                wait(act, fill_lo, index - 1)
                act.activation(fill_sb[place % 2][:], bank_f[:], ACT.Copy).then_inc(fill_out, 1)

            def fill_top(what, f, index, place):
                act.wait_ge(fill_out, index + 1)
                act.activation(fill_views(what, f)[0], fill_src(what, place), ACT.Copy).then_inc(fill_hi, 1)

            for index, (what, f) in enumerate(FIRST[:2]):
                fill_copy(what, f, index, index)
                fill_top(what, f, index, index)
                adjacency_sigmoid(index)
            fill_copy(*FIRST[2], 2, 2)

            def slot(N, n, q, live, more):
                first, second = fills_in(n, q, live, more)
                left = left_fill(n, q, live, more)
                if live(LAG_OUT):
                    act.wait_ge(pv_done, N - LAG_OUT + 1)
                    act.activation(z_hi[:], bank_z[:, 0:2 * P], ACT.Copy).then_inc(z_hi_done, 1)
                if live(LAG_PV):
                    act.wait_ge(turned, N - LAG_PV + 1)
                    act.activation(pt_hi[:], bank_t[:, 0:3 * P], ACT.Copy).then_inc(pt_hi_done, 1)
                if isinstance(N, int) and N == 0:
                    adjacency_sigmoid(2)
                    adjacency_sigmoid(3)
                if left:
                    fill_top(*left)
                if first:
                    fill_copy(*first)
                    fill_top(*first)
                if live(0):
                    act.wait_ge(neg_done, N + 1)
                    wait(act, norm_done, N * 2)
                    for j, (lo, hi) in enumerate(((0, P), (P, 3 * P))):
                        act.activation(probs[:, lo:hi], s_masked_sb[:, lo:hi], ACT.Exp, bias=neg_max[:, j:j + 1],
                                       scale=SCALE, accum_out=row_sum[:, j:j + 1]).then_inc(exp_done, 1)
                if isinstance(N, int) and N == 0:
                    fill_copy(*FIRST[3], 3, 3)
                    fill_top(*FIRST[2], 2, 2)
                    fill_top(*FIRST[3], 3, 3)
                if second:
                    fill_copy(*second)
                if isinstance(N, int):
                    draining(N)

            def root(n, b):
                act.wait_ge(mv_done[n], b + 1)
                part = slice(2 * b, 2 * b + 2)
                act.activation(std[:, part], mv[:, part, 1], ACT.Sqrt, bias=eps_col[:, 0:1]).then_inc(std_done[n], 1)

            def norm(n, b):
                act.wait_ge(shift_done[n], b + 1 if n < 2 else b // 2 + 1)
                for t in (2 * b, 2 * b + 1):
                    src = (acc[b][:, t % 2, :], xs[:, t, :], acc[b][:, t % 2, :])[n]
                    dst = (xs, xs, y_sb)[n][:, t, :]
                    ins = act.activation(dst, src, ACT.Identity, bias=shift[:, t:t + 1], scale=rstd[:, t:t + 1])
                ins.then_inc(normed[n] if n < 2 else y_done[b], 1)

            def turned_hi(b):
                act.wait_ge(x2_turned, b + 1)
                act.activation(of_batch(xt_hi, b), turned_batch(b), ACT.Copy).then_inc(x2t_hi_done, 1)

            def early_parts(n):
                act.wait_ge(gu_done, n + 1)
                act.activation(early_h[n][:], G[n % 2][:], ACT.Silu).then_inc(silu_done, 1)
                wait(act, early_product, n - 1)
                act.activation(early_u[n % 2][:], U[n % 2][:], ACT.Copy).then_inc(early_u_done, 1)

            def logits_out(half):
                act.wait_ge(logits_t_done, half + 1)
                act.activation(logits_t[:, half * BLK:(half + 1) * BLK], whole(logits_t_bank[half], E), ACT.Copy).then_inc(logits_t_out, 1)

            def exponentials():
                act.wait_ge(shifts_done, 2)
                act.activation(exp_all[:], shifted[:], ACT.Exp).then_inc(exps_done, 1)
                act.activation(exp_top[:], top_s[:], ACT.Exp).then_inc(exps_done, 1)

            def onehot_out(half):
                act.wait_ge(onehot_turned, half + 1)
                act.activation(onehot_t[:, half * HALF:(half + 1) * HALF].rearrange("p t n -> p (t n)"), whole(onehot_bank[half]),
                               ACT.Copy).then_inc(onehot_sb, 1)

            def cand_out(half):
                act.wait_ge(cand_done, half + 1)
                act.activation(cand[:, half * HALF:(half + 1) * HALF].rearrange("p t k e -> p (t k e)"), whole(cand_bank[half]),
                               ACT.Copy).then_inc(cand_sb, 1)

            def combine_t_out():
                act.wait_ge(combine_turned, 1)
                act.activation(combine_t[:, 0:BLK], whole(combine_bank[0], E), ACT.Copy).then_inc(combine_sb, 1)

            def draining(N):
                if N == LAST:
                    root(0, 0)
                    root(0, 1)
                    norm(0, 0)
                elif N == LAST + 1:
                    norm(0, 1)
                    root(1, 0)
                elif N == LAST + 2:
                    norm(1, 0)
                    root(1, 1)

            item_loop(act, slot)

            norm(1, 1)
            root(0, 2)
            turned_hi(0)
            root(0, 3)
            turned_hi(1)
            norm(0, 2)
            norm(0, 3)
            logits_out(0)
            root(1, 2)
            root(1, 3)
            norm(1, 2)
            turned_hi(2)
            turned_hi(3)
            early_parts(0)
            onehot_out(0)
            logits_out(1)
            early_parts(1)
            early_parts(2)
            cand_out(0)
            onehot_out(1)
            exponentials()
            early_parts(3)
            cand_out(1)
            for n in range(4, 9):
                early_parts(n)
            combine_t_out()
            for n in range(9, EB):
                early_parts(n)

            for n in range(EB):
                act.wait_ge(early_weighed[n % 2], n // 2 + 1)
                wait(act, down_done, n - 2)
                act.activation(h[n % 3][0][:], early_h[n][:], ACT.Copy).then_inc(h_hi_done, 1)

            def ffn_slot(K, k, s, last):
                if not (last and k < 2):
                    act.wait_ge(gu_done, K + EB + 1)
                    wait(act, silu_c_done, K - 1)
                    act.activation(silu_g[k % 2][:], G[k % 2][:], ACT.Silu).then_inc(silu_done, 1)
                if not isinstance(K, int) or K >= 1:
                    if last and k == 1:
                        return
                    act.wait_ge(h_done, K)
                    act.activation(h[(k - 1) % 3][0][:], h_sb[(k - 1) % 2][:], ACT.Copy).then_inc(h_hi_done, 1)

            ffn_loop(act, ffn_slot)

            root(2, 0)
            root(2, 1)
            norm(2, 0)
            root(2, 2)
            root(2, 3)
            norm(2, 2)

        @block.vector
        def _(dve):
            def minus_hi(dst, src, hi):
                return dve.tensor_tensor(dst, src, hi.bitcast(F32), ALU.subtract)

            dve.wait_ge(wctx_hi_done, 1)
            minus_hi(wctx_lo[:], wctx_raw[:], wctx_hi[:]).then_inc(wctx_lo_done, 1)
            for c in range(NBLK):
                dve.wait_ge(ctx_hi_done, c + 1)
                part = slice(c * BLK, (c + 1) * BLK)
                minus_hi(ctx_hl[CTX:, part], ctx_raw[CTX:, part], ctx_hl[CTX:, part]).then_inc(ctx_lo_done, 1)
            for n, (what, c) in enumerate(CTX_PROJ):
                dve.wait_ge(ctx_proj_hi, n + 1)
                rows = slice(0, CTX) if what == 0 else slice(CTX, P)
                dst = cq_lo[:, c * BLK:(c + 1) * BLK] if what == 0 else proj_hi(n)[rows]
                minus_hi(dst, whole(acc[n])[rows], proj_hi(n)[rows]).then_inc(ctx_proj_lo, 1)

            def sims_out(b):
                dve.wait_ge(sims_ready, 2 * b + 2)
                dve.tensor_copy(sims[:, 2 * b * SEQ:2 * (b + 1) * SEQ], sim_banks[b][:]).then_inc(sims_copied_late, 1)

            def split_lo(k, q):
                dve.wait_ge(w_hi_done[k], q + 1)
                minus_hi(lo_of[k], raw_of[k], hi_of[k]).then_inc(w_lo_done[k], 1)

            def xt_rest(c):
                dve.wait_ge(xt_hi_done[c], 1)
                part = slice(c * BLK, (c + 1) * BLK)
                minus_hi(xt_lo[:, :, part], xt_raw[:, :, part], xt_hi[:, :, part]).then_inc(xt_lo_done, 1)

            xt_rest(0)
            dve.wait_ge(gam_sig, 1)
            dve.tensor_scalar(gam[:, 2:3], gam[:, 1:2], 0.5, None, ALU.mult).then_inc(gam_done, 1)
            dve.tensor_scalar(gam[:, 3:4], gam[:, 1:2], -1.0, 2.0, ALU.mult, ALU.add).then_inc(gam_done, 1)
            split_lo("v", 0)

            def fill_rest(what, f, index, place):
                dve.wait_ge(fill_hi, index + 1)
                hi, lo = fill_views(what, f)
                minus_hi(lo, fill_src(what, place), hi).then_inc(fill_lo, 1)

            for index, (what, f) in enumerate(FIRST[:2]):
                fill_rest(what, f, index, index)
                sims_out(2 + index)
            split_lo("b", 0)
            xt_rest(1)

            STEPS = 2 * ROUNDS + 1

            def topk(t, j):
                base = t * STEPS
                if j:
                    dve.wait_ge(topk_step, base + j)
                    if j == STEPS - 1:
                        dve.wait_ge(adj_scaled, BATCH)
                    settle(dve)
                tile = sims[:, bass.ds(t * SEQ, SEQ)]
                if j == 0:
                    ins = dve.tensor_copy(topk_work[0][:], tile)
                elif j == STEPS - 1:
                    last = (TOPK_ADJ - 1) % 8
                    view = adj[:, bass.ds(t * SEQ, SEQ)]
                    ins = dve.scalar_tensor_tensor(out=view, in0=tile, scalar=topk_8[:, last:last + 1], in1=view,
                                                   op0=ALU.is_ge, op1=ALU.mult)
                elif j % 2:
                    ins = dve.max(topk_8[:], topk_work[(j // 2) % 2][:])
                else:
                    ins = dve.match_replace(out=topk_work[(j // 2) % 2][:], in_to_replace=topk_8[:],
                                            in_values=topk_work[(j // 2 + 1) % 2][:], imm_value=-3.0e38)
                ins.then_inc(topk_step, 1)

            TOPK_OF = {n: (3 * (n - 1), 3 * n) if n else (0, 0) for n in range(8)}

            def slot(N, n, q, live, more):
                first, second = fills_in(n, q, live, more)
                left = left_fill(n, q, live, more)
                steps = [(q, j) for j in range(*TOPK_OF[n])] if live(0) else []

                def one_step():
                    if steps:
                        topk(*steps.pop(0))

                if live(LAG_OUT):
                    dve.wait_ge(z_hi_done, N - LAG_OUT + 1)
                    minus_hi(z_lo[:], bank_z[:, 0:2 * P], z_hi[:]).then_inc(z_lo_done, 1)
                if live(LAG_PV):
                    dve.wait_ge(pt_hi_done, N - LAG_PV + 1)
                    minus_hi(pt_lo[:], bank_t[:, 0:3 * P], pt_hi[:]).then_inc(pt_lo_done, 1)
                if n % 2:
                    if left:
                        fill_rest(*left)
                    one_step()
                if live(0):
                    dve.wait_ge(scored, N + 1)
                    wait(dve, exp_done, N * 2)
                    settle(dve)
                    dve.tensor_tensor_reduce(out=s_masked_sb[:, 0:P], in0=bank_s[:, 0:P], in1=mask[:, P:], scale=1.0,
                                             scalar=-3.0e38, op0=ALU.add, op1=ALU.max, accum_out=row_max[:, 0:1]).then_inc(masked, 1)
                    dve.tensor_tensor_reduce(out=s_masked_sb[:, P:], in0=bank_s[:, P:3 * P], in1=mask[:], scale=1.0,
                                             scalar=-3.0e38, op0=ALU.add, op1=ALU.max, accum_out=row_max[:, 1:2]).then_inc(masked, 1)
                    dve.wait_ge(masked, N * 2 + 2)
                    dve.tensor_scalar(neg_max[:], row_max[:], -SCALE, None, ALU.mult).then_inc(neg_done, 1)
                if isinstance(N, int) and N == 1:
                    split_lo("o", 0)
                if not more and n == LAG_OUT and live(LAG_OUT):
                    dve.wait_ge(gate_hi_done, 1)
                    minus_hi(gate_lo[:], gate_raw[:], gate_hi[:]).then_inc(gate_lo_done, 1)
                if left and n % 2 == 0:
                    fill_rest(*left)
                if first:
                    fill_rest(*first)
                one_step()
                if live(0):
                    dve.wait_ge(exp_done, N * 2 + 2)
                    wait(dve, norm_done, N * 2)
                    dve.reciprocal(inv_sum[:], row_sum[:]).then_inc(inv_done, 1)
                if isinstance(N, int) and N == 0:
                    for index, (what, f) in list(enumerate(FIRST))[2:]:
                        fill_rest(what, f, index, index)
                if isinstance(N, int):
                    draining(N)
                while steps:
                    one_step()

            def stats_of(n, b):
                if n == 0:
                    dve.wait_ge(projected, LAST - 8 + 1 + max(n for n in range(8) if item(n)[1] == b))
                elif n == 1:
                    dve.wait_ge(mixed_done, b + 1)
                else:
                    dve.wait_ge(down_done, FT * NBLK - (b < 2))
                for t in (2 * b, 2 * b + 1):
                    ins = dve.bn_stats(stats[:, t, :], xs[:, t, :] if n == 1 else acc[b][:, t % 2, :])
                ins.then_inc(stats_done[n], 1)

            def moments_of(n, b):
                dve.wait_ge(stats_done[n], b + 1)
                for t in (2 * b, 2 * b + 1):
                    ins = dve.bn_aggr(mv[:, t, :], stats[:, t, :])
                ins.then_inc(mv_done[n], 1)

            def inverse_of(n, b):
                dve.wait_ge(std_done[n], b + 1)
                dve.reciprocal(rstd[:, 2 * b:2 * b + 2], std[:, 2 * b:2 * b + 2]).then_inc(rstd_done[n], 1)

            def shift_of(n, b):
                dve.wait_ge(rstd_done[n], b + 1)
                part = slice(2 * b, 2 * b + 2)
                dve.scalar_tensor_tensor(out=shift[:, part], in0=mv[:, part, 0], scalar=-1.0, in1=rstd[:, part],
                                         op0=ALU.mult, op1=ALU.mult).then_inc(shift_done[n], 1)

            def mix(b):
                dve.wait_ge(normed[0], b + 1)
                dve.wait_ge(adj_sum, b + 1)
                for t in (2 * b, 2 * b + 1):
                    ins = dve.scalar_tensor_tensor(out=xs[:, t, :], in0=xs[:, t, :], scalar=gam[:, 3:4],
                                                   in1=sim_banks[b][:, (t % 2) * SEQ:(t % 2 + 1) * SEQ], op0=ALU.mult, op1=ALU.add)
                ins.then_inc(mixed_done, 1)

            def second_norm(b):
                dve.wait_ge(rstd_done[1], b + 1)
                for t in (2 * b, 2 * b + 1):
                    ins = dve.tensor_scalar(xs[:, t, :], xs[:, t, :], mv[:, t, 0:1], rstd[:, t:t + 1], ALU.subtract, ALU.mult)
                ins.then_inc(normed_last, 1)

            def turned_lo(b):
                dve.wait_ge(x2t_hi_done, b + 1)
                minus_hi(of_batch(xt_lo, b), turned_batch(b), of_batch(xt_hi, b)).then_inc(x2t_lo_done, 1)

            count = [0]

            def link(ins):
                count[0] += 1
                ins.then_inc(link_step, 1)
                dve.wait_ge(link_step, count[0])

            def choose(half):
                if half == 0:
                    dve.wait_ge(projected, BATCH * HEADS)
                dve.wait_ge(logits_done, half + 1)
                logits = whole(logits_bank[half])[:, 0:HALF * E].rearrange("p (t e) -> p t e", e=E)
                tiles = slice(half * HALF, (half + 1) * HALF)
                for t in range(HALF):
                    ins = dve.max(top_v[:, half * HALF + t, :], logits[:, t, :])
                link(ins)
                for t in range(HALF):
                    ins = dve.max_index(top_i[:, half * HALF + t, :], top_v[:, half * HALF + t, :], logits[:, t, :])
                link(ins)
                dve.tensor_copy(top_if[:, tiles], top_i[:, tiles]).then_inc(index_done, 1)
                first = top_v[:, tiles, 0:1]
                dve.tensor_tensor(top_s[:, tiles], top_v[:, tiles], first.to_broadcast([P, HALF, TOP]), ALU.subtract)
                dve.tensor_tensor(shifted[:, tiles], logits, first.to_broadcast([P, HALF, E]), ALU.subtract).then_inc(shifts_done, 1)
                dve.wait_ge(index_done, half + 1)
                dve.tensor_tensor(onehot[:, tiles], *index_and_number(top_if[:, tiles, 0:PRIM]), ALU.is_equal).then_inc(onehot_done, 1)

            def index_and_number(index):
                return (index.rearrange("p t (k a) -> p t k a", a=1).to_broadcast([P, HALF, PRIM, E]),
                        iota_e[:].rearrange("p (a k e) -> p a k e", a=1, k=1).to_broadcast([P, HALF, PRIM, E]))

            def secondary(half):
                tiles = slice(half * HALF, (half + 1) * HALF)
                dve.tensor_tensor(onehot_s[:, tiles], *index_and_number(top_if[:, tiles, PRIM:]), ALU.is_equal).then_inc(secondary_done, 1)

            def draining(N):
                if N == LAST - 1:
                    stats_of(0, 0)
                    moments_of(0, 0)
                    stats_of(0, 1)
                    moments_of(0, 1)
                elif N == LAST:
                    inverse_of(0, 0)
                    shift_of(0, 0)
                    inverse_of(0, 1)
                    shift_of(0, 1)
                elif N == LAST + 1:
                    mix(0)
                    stats_of(1, 0)
                    moments_of(1, 0)
                    inverse_of(1, 0)
                    shift_of(1, 0)
                elif N == LAST + 2:
                    mix(1)
                    stats_of(1, 1)
                    moments_of(1, 1)
                    stats_of(0, 2)
                    moments_of(0, 2)
                    inverse_of(1, 1)
                    shift_of(1, 1)
                    stats_of(0, 3)
                    moments_of(0, 3)

            item_loop(dve, slot)

            inverse_of(0, 2)
            shift_of(0, 2)
            turned_lo(0)
            inverse_of(0, 3)
            shift_of(0, 3)
            turned_lo(1)
            mix(2)
            stats_of(1, 2)
            moments_of(1, 2)
            mix(3)
            stats_of(1, 3)
            moments_of(1, 3)
            inverse_of(1, 2)
            shift_of(1, 2)
            inverse_of(1, 3)
            second_norm(3)
            choose(0)
            turned_lo(2)
            turned_lo(3)
            secondary(0)
            choose(1)
            secondary(1)

            dve.wait_ge(exps_done, 2)

            def col(a, n):
                return a[:].rearrange("p (t o) -> p t o", o=1).to_broadcast([P, TILES, n])

            link(dve.tensor_reduce(sum_all[:], exp_all[:], AX.X, ALU.add))
            link(dve.reciprocal(inv_all[:], sum_all[:]))
            link(dve.tensor_tensor(prob_top[:], exp_top[:], col(inv_all, TOP), ALU.mult))
            link(dve.tensor_reduce(sum_top[:], prob_top[:], AX.X, ALU.add))
            link(dve.tensor_scalar(sum_top_c[:], sum_top[:], 1.0e-12, None, ALU.max))
            link(dve.reciprocal(inv_top[:], sum_top_c[:]))
            dve.tensor_tensor(route_w[:], prob_top[:], col(inv_top, TOP), ALU.mult)
            link(dve.tensor_tensor(inv_both[:], inv_all[:], inv_top[:], ALU.mult))
            dve.wait_ge(sec_exp_done, 1)
            dve.tensor_tensor(sec_w[:], sec_exp[:], col(inv_both, E), ALU.mult)
            dve.wait_ge(cand_sb, 2)
            link(dve.tensor_reduce(best[:], cand[:].rearrange("p t k e -> p t e k"), AX.X, ALU.max))
            dve.scalar_tensor_tensor(out=moved[0][:], in0=best[:], scalar=0.5, in1=sec_w[:], op0=ALU.is_ge, op1=ALU.mult)\
                .then_inc(moved_done, 1)
            best_b = best[:].rearrange("p t (k e) -> p t k e", k=1).to_broadcast([P, TILES, PRIM, E])
            link(dve.tensor_tensor(is_best[:], cand[:], best_b, ALU.is_equal))
            for i in range(PRIM):
                link(dve.tensor_tensor(take[:, :, i, :], is_best[:, :, i, :], moved[i][:], ALU.mult))
                if i < PRIM - 1:
                    link(dve.tensor_tensor(moved[i + 1][:], moved[i][:], take[:, :, i, :], ALU.subtract))
            link(dve.tensor_reduce(taken[:], take[:], AX.X, ALU.add))
            link(dve.tensor_tensor(prim_w[:], taken[:], route_w[:, :, 0:PRIM], ALU.add))
            w_b = prim_w[:].rearrange("p t (k a) -> p t k a", a=1).to_broadcast([P, TILES, PRIM, E])
            link(dve.tensor_tensor(prim_each[:], onehot[:], w_b, ALU.mult))
            link(dve.tensor_reduce(prim_all[:], prim_each[:].rearrange("p t k e -> p t e k"), AX.X, ALU.add))
            dve.wait_ge(kept_done, 1)
            dve.tensor_tensor(combine[:], prim_all[:], kept[:], ALU.add).then_inc(combined, 1)
            dve.wait_ge(combine_turned, 2)
            dve.tensor_copy(combine_t[:, BLK:], whole(combine_bank[1], E)).then_inc(combine_sb, 1)

            def weigh(n):
                i, c = EARLY_BLOCKS[n]
                dve.wait_ge(cw_in[i], 32)
                dve.wait_ge(early_product, n + 1)
                dve.tensor_tensor(early_h[n][:], early_h[n][:], cw[i][:, c * BLK:(c + 1) * BLK], ALU.mult)\
                    .then_inc(early_weighed[0], 1)

            def early_lo(n):
                dve.wait_ge(h_hi_done, n + 1)
                minus_hi(h[n % 3][1][:], early_h[n][:], h[n % 3][0][:]).then_inc(h_lo_done, 1)

            weigh(0)
            for n in range(0, EB, 2):
                if n + 2 < EB:
                    weigh(n + 2)
                early_lo(n)
                early_lo(n + 1)

            def split_ffn(i, s):
                dve.wait_ge(wf_hi_done[i], s + 2)
                minus_hi(wf[i][1][:], wf_raw[i][:], wf[i][0][:]).then_inc(wf_lo_done[i], 1)

            for i in range(FG - 1):
                split_ffn(i, 0)

            def ffn_slot(K, k, s, last):
                if (not isinstance(K, int) or K >= 1) and not (last and k == 1):
                    dve.wait_ge(h_hi_done, K + EB)
                    minus_hi(h[(k - 1) % 3][1][:], h_sb[(k - 1) % 2][:], h[(k - 1) % 3][0][:]).then_inc(h_lo_done, 1)
                if not (last and k < 2):
                    dve.wait_ge(silu_c_done, K + 1)
                    dve.wait_ge(h_lo_done, K + EB - 1)
                    dve.tensor_tensor(h_sb[k % 2][:], U[k % 2][:], silu_c[k % 2][:], ALU.mult).then_inc(h_done, 1)
                split_at_slot(k, s, K, last, split_ffn)

            ffn_loop(dve, ffn_slot)

            def last_norm(b):
                dve.wait_ge(rstd_done[2], b + 1)
                for t in (2 * b, 2 * b + 1):
                    ins = dve.tensor_scalar(y_sb[:, t, :], acc[b][:, t % 2, :], mv[:, t, 0:1], rstd[:, t:t + 1],
                                            ALU.subtract, ALU.mult)
                ins.then_inc(y_done[b], 1)

            stats_of(2, 0)
            moments_of(2, 0)
            stats_of(2, 1)
            moments_of(2, 1)
            inverse_of(2, 0)
            shift_of(2, 0)
            inverse_of(2, 1)
            stats_of(2, 2)
            moments_of(2, 2)
            stats_of(2, 3)
            moments_of(2, 3)
            inverse_of(2, 2)
            shift_of(2, 2)
            last_norm(1)
            inverse_of(2, 3)
            last_norm(3)

        @block.tensor
        def _(pe):
            def three(dst, a, b, start, stop, first_of=True):
                (ah, al), (bh, bl) = a, b
                pe.matmul(dst, ah, bh, start=start, stop=False, skip_group_check=True)
                pe.matmul(dst, ah, bl, start=False, stop=False, skip_group_check=True)
                return pe.matmul(dst, al, bh, start=False, stop=stop, skip_group_check=True)

            pe.wait_ge(const_made, 2)
            for n in range(WARM):
                pe.matmul(bank_f[:, 0:2 * P], ident[:], mask[:], start=True, stop=True)
            pe.wait_ge(wctx_lo_done, 1)
            for n, (what, c) in enumerate(CTX_PROJ):
                pe.wait_ge(ctx_lo_done, c + 1)
                part = slice(c * BLK, (c + 1) * BLK)
                pe.matmul(whole(acc[n]), wctx_hi[:, what, :], ctx_hl[:, part], start=True, stop=False)
                pe.matmul(whole(acc[n]), wctx_lo[0:CTX, what, :], ctx_hl[0:CTX, part], start=False, stop=True).then_inc(ctx_proj, 1)

            def similarities(b):
                pe.wait_ge(ctx_proj_lo, 2 * (b // 2) + 2)
                keys = slice(b * SEQ, (b + 1) * SEQ)
                for t in (2 * b, 2 * b + 1):
                    dst, tok = sim_banks[b][:, (t % 2) * SEQ:(t % 2 + 1) * SEQ], slice(t * P, (t + 1) * P)
                    pe.matmul(dst, cq_hi[:, tok], ck_hl[:, keys], start=(t % 2 == 0), stop=False, skip_group_check=True)
                    pe.matmul(dst, cq_lo[:, tok], ck_hl[0:CTX, keys], start=False, stop=(t % 2 == 1), skip_group_check=True).then_inc(sims_ready, 1)

            for b in range(BATCH):
                similarities(b)

            def seed(t):
                return pe.matmul(acc[t // 2][:, t % 2, :], ident[:], xs[:, t, :], start=(t % 2 == 0), stop=(t % 2 == 1),
                                 skip_group_check=True)

            def seed_batch(b):
                for t in (2 * b, 2 * b + 1):
                    seed(t)

            def fill(what, f, index):
                wait(pe, fill_out, index)
                if what == "v":
                    for j in range(2):
                        t = 2 * f + j
                        for c in range(KC):
                            tok = slice(t * P, (t + 1) * P)
                            ins = three(bank_f[:, j * 2 * P:(j + 1) * 2 * P], (xt_hi[:, c, tok], xt_lo[:, c, tok]),
                                        (wv_hi[:, c, :], wv_lo[:, c, :]), j == 0 and c == 0, j == 1 and c == KC - 1)
                else:
                    hi, lo = (wa_hi, wa_lo) if f % 2 == 0 else (wb_hi, wb_lo)
                    s, part = "qk".index(what), slice(f // 2 * BLK, (f // 2 + 1) * BLK)
                    for c in range(KC):
                        ins = three(bank_f[:], (hi[:, s, c, :], lo[:, s, c, :]), (xt_hi[:, c, part], xt_lo[:, c, part]),
                                    c == 0, c == KC - 1)
                ins.then_inc(filled, 1)

            pe.wait_ge(const_made, 3)
            pe.wait_ge(sims_copied, 1)
            for index, (what, f) in enumerate(FIRST[:3]):
                pe.wait_ge(xt_lo_done, 1)
                pe.wait_ge(w_lo_done["v" if what == "v" else "a"], 1)
                fill(what, f, index)
                if index == 0:
                    pe.wait_ge(in_x, 16)
                seed_batch(index)

            def need_weights(what, f, q):
                if (what, f) == ("q", 0):
                    pe.wait_ge(w_lo_done["a"], q + 2)
                elif (what, f) == ("v", 0):
                    pe.wait_ge(w_lo_done["v"], q + 2)
                elif (what, f) == ("q", 1):
                    pe.wait_ge(w_lo_done["b"], q + 2)

            def slot(N, n, q, live, more):
                first, second = fills_in(n, q, live, more)
                if live(LAG_PV):
                    if isinstance(N, int) and N == LAG_PV:
                        pe.wait_ge(sims_copied_late, 2)
                    pe.wait_ge(norm_done, (N - LAG_PV) * 2 + 2)
                    wait(pe, pt_lo_done, N - LAG_PV)
                    for j in range(3):
                        ins = pe.transpose(bank_t[:, j * P:(j + 1) * P], probs_n[n % 2][:, j * P:(j + 1) * P], ident[:])
                    ins.then_inc(turned, 1)
                if isinstance(N, int) and N == 1:
                    pe.wait_ge(xt_lo_done, NBLK)
                if first:
                    need_weights(*first[:2], q)
                    fill(*first[:3])
                if live(0):
                    g = n // 2
                    if isinstance(N, int) and N == 0:
                        pe.wait_ge(sims_copied, 2)
                    pe.wait_ge(fill_lo, PER_PAIR * q + ORDER["k", g] + 1)
                    wait(pe, masked, N * 2)
                    (hi, lo), off = qk[g % 2], (n % 2) * SEQ
                    for j in range(2):
                        tok, keys = slice(off + j * P, off + (j + 1) * P), slice(off, off + (j + 1) * P)
                        ins = three(bank_s[:, (0, P)[j]:(P, 3 * P)[j]], (hi[:, 0, tok], lo[:, 0, tok]),
                                    (hi[:, 1, keys], lo[:, 1, keys]), j == 0, j == 1)
                    ins.then_inc(scored, 1)
                if isinstance(N, int) and N == 0:
                    pe.wait_ge(w_lo_done["b"], 1)
                    fill(*FIRST[3], 3)
                    seed_batch(3)
                if second and len(fills_of_slot(n)) == 1:
                    need_weights(*second[:2], q)
                    fill(*second[:3])
                if live(LAG_OUT):
                    m = (n - LAG_OUT) % 8
                    a, b = item(m)
                    pe.wait_ge(z_lo_done, N - LAG_OUT + 1)
                    if b == 0:
                        pe.wait_ge(w_lo_done["op"[a]], q + 1)
                    for j in range(2):
                        part = slice(j * P, (j + 1) * P)
                        ins = three(acc[b][:, j, :], (z_hi[:, part], z_lo[:, part]), (wo[a][0][:], wo[a][1][:]), False, False)
                    ins.then_inc(projected, 1)
                if isinstance(N, int):
                    draining(N, "projected")
                if second and len(fills_of_slot(n)) == 2:
                    need_weights(*second[:2], q)
                    fill(*second[:3])
                if live(LAG_PV):
                    m = (n - LAG_PV) % 8
                    a, b = item(m)
                    pe.wait_ge(pt_lo_done, N - LAG_PV + 1)
                    if a == 0:
                        pe.wait_ge(fill_lo, PER_PAIR * q + ORDER["v", b] + 1)
                    wait(pe, z_lo_done, N - LAG_PV)
                    e = slice(a * DH, (a + 1) * DH)
                    three(bank_z[:, 0:2 * P], (v_hi[:, 2 * b, e], v_lo[:, 2 * b, e]), (pt_hi[:, 0:2 * P], pt_lo[:, 0:2 * P]), True, False)
                    three(bank_z[:, P:2 * P], (v_hi[:, 2 * b + 1, e], v_lo[:, 2 * b + 1, e]),
                          (pt_hi[:, 2 * P:], pt_lo[:, 2 * P:]), False, True).then_inc(pv_done, 1)
                if isinstance(N, int):
                    draining(N, "end")

            def adjacency(b):
                pe.wait_ge(topk_step, (2 * b + 2) * (2 * ROUNDS + 1))
                pe.wait_ge(*[(fill_out, PER_PAIR * PAIRS), (masked, 2 * BATCH * HEADS),
                             (pt_lo_done, BATCH * HEADS), (z_lo_done, BATCH * HEADS)][b])
                for r in range(2):
                    t = 2 * b + r
                    for c in range(2):
                        part = sim_banks[b][:, r * SEQ + c * P:r * SEQ + (c + 1) * P]
                        blk = adj[:, (2 * b + c) * SEQ + r * P:(2 * b + c) * SEQ + (r + 1) * P]
                        pe.matmul(part, blk, ident[:], start=(r == 0 and c == 0), stop=False, skip_group_check=True)
                    ins = pe.matmul(sim_banks[b][:, r * SEQ:(r + 1) * SEQ], ident[:], adj[:, t * SEQ:(t + 1) * SEQ], start=False,
                                    stop=(r == 1), skip_group_check=True)
                ins.then_inc(adj_sum, 1)

            def draining(N, place):
                if (N, place) == (LAST - 1, "projected"):
                    adjacency(0)
                elif (N, place) == (LAST + 1, "end"):
                    adjacency(1)
                elif (N, place) == (LAST + 2, "end"):
                    turn(0)
                    adjacency(2)
                    turn(1)
                    adjacency(3)

            def turn(b):
                if b < BATCH - 1:
                    pe.wait_ge(normed[1], b + 1)
                else:
                    pe.wait_ge(normed_last, 1)
                for t in range(2):
                    for c in range(KC):
                        ins = pe.transpose(turned_batch(b)[:, t, c, :], xs[:, 2 * b + t, c * P:(c + 1) * P], ident[:])
                ins.then_inc(x2_turned, 1)

            def route(half):
                pe.wait_ge(x2t_lo_done, 2 * half + 2)
                pe.wait_ge(gate_lo_done, 1)
                part = slice(half * BLK, (half + 1) * BLK)
                for c in range(KC):
                    ins = three(whole(logits_t_bank[half], E), (gate_hi[:, c, :], gate_lo[:, c, :]), (xt_hi[:, c, part], xt_lo[:, c, part]),
                                c == 0, c == KC - 1)
                ins.then_inc(logits_t_done, 1)

            def turn_logits(half):
                pe.wait_ge(logits_t_out, half + 1)
                for j in range(HALF):
                    ins = pe.transpose(whole(logits_bank[half])[:, j * E:(j + 1) * E],
                                       logits_t[:, (half * HALF + j) * P:(half * HALF + j + 1) * P], ident[0:E, 0:E])
                ins.then_inc(logits_done, 1)

            def turn_onehot(half):
                pe.wait_ge(onehot_done, half + 1)
                for j in range(HALF):
                    ins = pe.transpose(bank_tile(onehot_bank[half], j), onehot[:, half * HALF + j].rearrange("p k e -> p (k e)"), ident[:])
                ins.then_inc(onehot_turned, 1)

            def similar(half):
                pe.wait_ge(blockdiag_made, 1)
                pe.wait_ge(onehot_sb, half + 1)
                pe.wait_ge(shifts_done, half + 1)
                for j in range(HALF):
                    ins = pe.matmul(bank_tile(cand_bank[half], j), onehot_t[:, half * HALF + j, :], blockdiag[:], start=(j == 0),
                                    stop=(j == HALF - 1), skip_group_check=True)
                ins.then_inc(cand_done, 1)

            def turn_combine(half):
                pe.wait_ge(combined, 1)
                for j in range(HALF):
                    ins = pe.transpose(bank_tile(combine_bank[half], j, E), combine[:, half * HALF + j, :], ident[:])
                ins.then_inc(combine_turned, 1)

            def hidden(tile, c, bank, of=(0, 1)):
                hi, lo = wf[tile]
                part = slice(c * BLK, (c + 1) * BLK)
                for g in of:
                    dst = (G[bank], U[bank])[g]
                    for d in range(KC):
                        w = slice((g * KC + d) * P, (g * KC + d + 1) * P)
                        ins = three(dst[:], (hi[:, w], lo[:, w]), (xt_hi[:, d, part], xt_lo[:, d, part]), d == 0, d == KC - 1)
                if 1 in of:
                    ins.then_inc(gu_done, 1)

            def down(tile, c, n):
                hi, lo = wf[tile]
                hh, hl = h[n]
                for t in range(HALF):
                    at, tok = HALF * c + t, slice(t * P, (t + 1) * P)
                    ins = three(acc[at // 2][:, at % 2, :], (hh[:, tok], hl[:, tok]), (hi[:, 4 * P:], lo[:, 4 * P:]), False, False)
                ins.then_inc(down_done, 1)

            def early_g(n):
                i, c = EARLY_BLOCKS[n]
                pe.wait_ge(wf_lo_done[i], 1)
                pe.wait_ge(x2t_lo_done, 2 * c + 2)
                if n == 1:
                    pe.wait_ge(mixed_done, BATCH)
                wait(pe, early_u_done, n - 1)
                hidden(i, c, n % 2, of=(0,))

            def early_u(n):
                i, c = EARLY_BLOCKS[n]
                hidden(i, c, n % 2, of=(1,))

            def early(n):
                early_g(n)
                early_u(n)

            def start_sums():
                pe.wait_ge(combine_sb, NBLK)
                pe.wait_ge(cand_sb, 2)
                for t in range(TILES):
                    seed(t)

            item_loop(pe, slot)

            route(0)
            early_g(0)
            turn_logits(0)
            early_u(0)
            early_g(1)
            turn(2)
            turn(3)
            early_u(1)
            route(1)
            turn_onehot(0)
            early_g(2)
            turn_logits(1)
            early_u(2)
            similar(0)
            early_g(3)
            turn_onehot(1)
            early_u(3)
            early_g(4)
            similar(1)
            early_u(4)
            for n in range(5, 9):
                early(n)
            turn_combine(0)
            turn_combine(1)
            for n in range(9, EB):
                early(n)
            start_sums()

            for n, (i, c) in enumerate(EARLY_BLOCKS):
                pe.wait_ge(h_lo_done, n + 1)
                down(i, c, n % 3)

            def ffn_slot(K, k, s, last):
                i, c = k // 2, k % 2
                if not (last and k < 2):
                    if c == 0:
                        pe.wait_ge(wf_lo_done[i], s + 2)
                    if isinstance(K, int) and K < 2:
                        pe.wait_ge(early_u_done, EB + K - 1)
                    else:
                        pe.wait_ge(h_done, K - 1)
                    hidden(i, c, k % 2)
                if not isinstance(K, int) or K >= 2:
                    pe.wait_ge(h_lo_done, K + EB - 1)
                    down(((k - 2) % (2 * FG)) // 2, c, (k - 2) % 3)

            ffn_loop(pe, ffn_slot)


_OUT = [((BATCH, SEQ, D), "float32")]


def kernel(x, ctx_512, L0_attn_W_Q, L0_attn_W_K, L0_attn_W_V, L0_attn_W_O, L0_xattn_Wq, L0_xattn_Wk,
           L0_xattn_gamma_raw, L0_ffn_gate_weight, L0_ffn_gate_up_proj, L0_ffn_down_proj, L0_ffn_similarity):
    import numpy as np
    import concourse.bacc as bacc
    from concourse.bass_utils import run_bass_kernel_spmd as run

    def heads_t(w):
        return np.asarray(w).reshape(HEADS, DH, KC, P).transpose(0, 3, 2, 1)

    tokens = np.asarray(x).reshape(TOK, D)
    w_qk = np.stack([heads_t(L0_attn_W_Q), heads_t(L0_attn_W_K)], axis=2).reshape(HEADS, P, -1)
    w_v = heads_t(L0_attn_W_V).reshape(PAIRS, 2, P, KC, DH).transpose(0, 2, 3, 1, 4).reshape(PAIRS, P, -1)
    gate_up = np.asarray(L0_ffn_gate_up_proj).reshape(E, 2, FF, D).transpose(1, 0, 2, 3).reshape(2, FT, P, KC, P)
    w_ffn = np.concatenate([gate_up.transpose(1, 4, 0, 3, 2).reshape(FT, P, -1),
                            np.asarray(L0_ffn_down_proj).transpose(0, 2, 1).reshape(FT, P, D)], axis=2)
    arrays = {
        "x_tok": tokens,
        "x_t": tokens.reshape(TOK, KC, P).transpose(2, 1, 0),
        "w_qk": w_qk,
        "w_v": w_v,
        "w_o": np.asarray(L0_attn_W_O).transpose(0, 2, 1),
        "ctx_t": np.asarray(ctx_512).reshape(TOK, CTX).T,
        "w_ctx": np.tile(np.stack([np.asarray(L0_xattn_Wq).T, np.asarray(L0_xattn_Wk).T], axis=1), (2, 1, 2)),
        "gamma_raw": np.asarray(L0_xattn_gamma_raw).reshape(1, 1),
        "gate_t": np.asarray(L0_ffn_gate_weight).reshape(E, KC, P).transpose(2, 1, 0),
        "w_ffn": w_ffn,
        "sim_t": np.asarray(L0_ffn_similarity).T,
    }
    arrays = {k: np.ascontiguousarray(v) for k, v in arrays.items()}
    nc = bacc.Bacc("TRN2", target_bir_lowering=False, num_devices=1)
    args = {k: nc.dram_tensor(k, v.shape, mybir.dt.from_np(v.dtype), kind="ExternalInput").ap() for k, v in arrays.items()}
    out = nc.dram_tensor("out", [TOK, D], F32, kind="ExternalOutput").ap()
    program(nc, **args, out=out)
    r = run(nc, [arrays], core_ids=[0])
    return r.results[0]["out"].reshape(BATCH, SEQ, D)
```
